# Optimizing a Trainium2 kernel written in Bass

```python
import numpy as np
import jax
import jax.numpy as jnp

def _softmax(x, axis=-1):
    return jax.nn.softmax(x, axis=axis)

def _gelu(x):
    return jax.nn.gelu(x, approximate=True)

def _silu(x):
    return jax.nn.silu(x)

def _sigmoid(x):
    return jax.nn.sigmoid(x)

def _layernorm(x, axis=-1, eps=1e-05):
    m = jnp.mean(x, axis=axis, keepdims=True)
    v = jnp.var(x, axis=axis, keepdims=True)
    return (x - m) / jnp.sqrt(v + eps)

def _scatter_add(tgt, idx, src, axis=0):
    return tgt.at[idx].add(src)

def _segment_sum(src, seg, n):
    return jax.ops.segment_sum(src, seg, n)
kernel_name = 'mk_macaron_d2_jaxref_r8_47e290'

def setup_inputs(seed: int=0):
    np.random.seed(seed)
    _w = jnp.asarray

    def _L0_attn_setup():
        import jax, jax.numpy as jnp
        import numpy as np
        import math
        B, T, E, H = (2, 256, 128, 16)
        D = E // H
        THETA = 10000.0

        def _rope(x):
            d = x.shape[-1]
            t = x.shape[1]
            freqs = 1.0 / THETA ** (jnp.arange(0, d, 2, dtype=jnp.float32) / d)
            ang = jnp.arange(t, dtype=jnp.float32)[:, None] * freqs[None, :]
            cos = jnp.cos(ang)[None, :, None, :]
            sin = jnp.sin(ang)[None, :, None, :]
            xr = x[..., 0::2]
            xi = x[..., 1::2]
            o = jnp.stack([xr * cos - xi * sin, xr * sin + xi * cos], axis=-1)
            return o.reshape(x.shape)
        key = jax.random.key(seed)
        k1, k2, k3 = jax.random.split(key, 3)
        x = jax.random.normal(k1, (B, T, E), dtype=jnp.float32)
        W_qkv = jax.random.normal(k2, (3 * E, E), dtype=jnp.float32) * 0.02
        b_qkv = jax.random.normal(k3, (3 * E,), dtype=jnp.float32) * 0.02
        return {'x': x, 'W_qkv': W_qkv, 'b_qkv': b_qkv}
    _L0_attn_in = _L0_attn_setup()

    def _L0_ffn_setup():
        import jax, jax.numpy as jnp
        import numpy as np
        D_MODEL = 128
        M = 64
        INNER = 16
        key = jax.random.key(seed)
        ks = jax.random.split(key, 9)

        def init(k, shape, fan_in):
            bound = 1.0 / np.sqrt(fan_in)
            return jax.random.uniform(k, shape, jnp.float32, -bound, bound)
        x = jax.random.normal(ks[0], (16, 512, D_MODEL), dtype=jnp.float32)
        Win = init(ks[1], (D_MODEL, M), D_MODEL)
        bin_ = init(ks[2], (M,), D_MODEL)
        W1 = init(ks[3], (M, INNER), 1)
        b1 = init(ks[4], (M, INNER), 1)
        W2 = init(ks[5], (M, INNER), INNER)
        b2 = init(ks[6], (M,), INNER)
        Wout = init(ks[7], (M, D_MODEL), M)
        bout = init(ks[8], (D_MODEL,), M)
        return {'x': x, 'Win': Win, 'bin_': bin_, 'W1': W1, 'b1': b1, 'W2': W2, 'b2': b2, 'Wout': Wout, 'bout': bout}
    _L0_ffn_in = _L0_ffn_setup()

    def _L1_attn_setup():
        import jax, jax.numpy as jnp
        import numpy as np
        D_MODEL = 128
        D_STATE = 128
        D_CONV = 4
        EXPAND = 2
        D_INNER = EXPAND * D_MODEL
        HEADDIM = 64
        NHEADS = D_INNER // HEADDIM
        NGROUPS = 1
        CONV_DIM = D_INNER + 2 * NGROUPS * D_STATE
        D_IN_PROJ = 2 * D_INNER + 2 * NGROUPS * D_STATE + NHEADS
        BATCH, SEQLEN = (2, 256)

        def _mamba2(u, Wi, conv_w, conv_b, dt_bias, A_log, D, norm_w, Wo):
            b, L, _ = u.shape
            zxbcdt = u @ Wi.T
            z = zxbcdt[..., :D_INNER]
            xBC = zxbcdt[..., D_INNER:D_INNER + CONV_DIM]
            dt = zxbcdt[..., D_INNER + CONV_DIM:]
            xBC_t = jnp.moveaxis(xBC, 1, 2)
            xBC_t = jnp.pad(xBC_t, ((0, 0), (0, 0), (D_CONV - 1, 0)))
            conv = jax.lax.conv_general_dilated(xBC_t, conv_w, (1,), 'VALID', feature_group_count=CONV_DIM, dimension_numbers=('NCH', 'OIH', 'NCH'))
            xBC = jax.nn.silu(jnp.moveaxis(conv, 1, 2) + conv_b)
            x = xBC[..., :D_INNER].reshape(b, L, NHEADS, HEADDIM)
            Bm = xBC[..., D_INNER:D_INNER + NGROUPS * D_STATE].reshape(b, L, D_STATE)
            Cm = xBC[..., D_INNER + NGROUPS * D_STATE:].reshape(b, L, D_STATE)
            dt = jax.nn.softplus(dt + dt_bias)
            A = -jnp.exp(A_log)

            def step(h, inp):
                x_t, B_t, C_t, dt_t = inp
                dA = jnp.exp(dt_t * A)
                h = h * dA[..., None, None] + (dt_t[..., None] * x_t)[..., None] * B_t[:, None, None, :]
                y_t = jnp.einsum('bhpn,bn->bhp', h, C_t)
                return (h, y_t)
            h0 = jnp.zeros((b, NHEADS, HEADDIM, D_STATE), u.dtype)
            xs = (jnp.moveaxis(x, 1, 0), jnp.moveaxis(Bm, 1, 0), jnp.moveaxis(Cm, 1, 0), jnp.moveaxis(dt, 1, 0))
            _, ys = jax.lax.scan(step, h0, xs)
            y = jnp.moveaxis(ys, 0, 1) + D[None, None, :, None] * x
            y = y.reshape(b, L, D_INNER)
            y = y * jax.nn.silu(z)
            y = y * jax.lax.rsqrt(jnp.mean(y * y, axis=-1, keepdims=True) + 1e-05) * norm_w
            return y @ Wo.T
        key = jax.random.key(seed)
        ks = jax.random.split(key, 21)

        def lin(k, o, i):
            return jax.random.normal(k, (o, i), jnp.float32) / np.sqrt(i).astype(np.float32)
        d = {'u': jax.random.normal(ks[0], (BATCH, SEQLEN, D_MODEL), jnp.float32)}
        for i, sfx in enumerate(['f', 'b']):
            b0 = 1 + i * 10
            d[f'Wi_{sfx}'] = lin(ks[b0], D_IN_PROJ, D_MODEL)
            d[f'conv_w_{sfx}'] = jax.random.normal(ks[b0 + 1], (CONV_DIM, 1, D_CONV), jnp.float32) / np.sqrt(D_CONV).astype(np.float32)
            d[f'conv_b_{sfx}'] = jnp.zeros((CONV_DIM,), jnp.float32)
            dt = jnp.exp(jax.random.uniform(ks[b0 + 2], (NHEADS,), jnp.float32) * (np.log(0.1) - np.log(0.001)) + np.log(0.001))
            d[f'dt_bias_{sfx}'] = dt + jnp.log(-jnp.expm1(-dt))
            d[f'A_log_{sfx}'] = jnp.log(jax.random.uniform(ks[b0 + 3], (NHEADS,), jnp.float32, minval=1.0, maxval=16.0))
            d[f'D_{sfx}'] = jnp.ones((NHEADS,), jnp.float32)
            d[f'norm_w_{sfx}'] = jnp.ones((D_INNER,), jnp.float32)
            d[f'Wo_{sfx}'] = lin(ks[b0 + 4], D_MODEL, D_INNER)
        return d
    _L1_attn_in = _L1_attn_setup()

    def _L1_ffn_setup():
        import jax, jax.numpy as jnp
        import numpy as np
        B, S, H, F, E, K = (4, 256, 128, 448, 8, 2)
        CAP_FACTOR = 1.25

        def _moe_forward(hidden_states, gate_w, w1, w2, w3):
            b, s, h = hidden_states.shape
            dtype = hidden_states.dtype
            x = hidden_states.reshape(-1, h)
            router_logits = x @ gate_w.T
            expert_weights = jax.nn.softmax(router_logits.astype(jnp.float32), axis=1)
            _, selected_experts = jax.lax.top_k(expert_weights, K)
            top_k_idx = selected_experts.reshape(b, s, K)
            probs = expert_weights.reshape(b, s, E)
            capacity = int(s * K / E * CAP_FACTOR)
            expert_mask = jax.nn.one_hot(top_k_idx, E, dtype=jnp.int32)
            mask_fused = expert_mask.reshape(b, s * K, E)
            count_fused = jnp.cumsum(mask_fused, axis=1)
            count = count_fused.reshape(b, s, K, E)
            trunc_mask = expert_mask * (count <= capacity).astype(jnp.int32)
            combined_mask = trunc_mask.sum(axis=2)
            masked_probs = probs * combined_mask
            pos_fused = mask_fused * count_fused
            pos = pos_fused.reshape(b, s, K, E)
            combined_pos = pos.sum(axis=2) * combined_mask
            pos_in_cap = jax.nn.one_hot(combined_pos, capacity + 1, dtype=jnp.int32)
            combine_mask = masked_probs[..., None] * pos_in_cap
            combine_mask = combine_mask[..., 1:].astype(dtype)
            dispatch_mask = (combine_mask != 0).astype(dtype)
            dispatch = jnp.einsum('bsm,bsec->ebcm', hidden_states, dispatch_mask)
            h1 = jnp.einsum('ebcm,emh->ebch', dispatch, w1)
            h3 = jnp.einsum('ebcm,emh->ebch', dispatch, w3)
            expert_out = jnp.einsum('ebch,ehm->ebcm', jax.nn.silu(h1) * h3, w2)
            final = jnp.einsum('ebcm,bsec->bsm', expert_out, combine_mask)
            return final
        key = jax.random.key(seed)
        k1, k2, k3, k4, k5 = jax.random.split(key, 5)
        s_h = 1.0 / np.sqrt(H)
        s_f = 1.0 / np.sqrt(F)
        return {'hidden_states': jax.random.normal(k1, (B, S, H), dtype=jnp.float32), 'gate_w': jax.random.normal(k2, (E, H), dtype=jnp.float32) * s_h, 'w1': jax.random.normal(k3, (E, H, F), dtype=jnp.float32) * s_h, 'w2': jax.random.normal(k4, (E, F, H), dtype=jnp.float32) * s_f, 'w3': jax.random.normal(k5, (E, H, F), dtype=jnp.float32) * s_h}
    _L1_ffn_in = _L1_ffn_setup()
    _d = {'L0_attn_x': _L0_attn_in['x'], 'L0_attn_W_qkv': _L0_attn_in['W_qkv'], 'L0_attn_b_qkv': _L0_attn_in['b_qkv'], 'L0_ffn_Win': _L0_ffn_in['Win'], 'L0_ffn_bin_': _L0_ffn_in['bin_'], 'L0_ffn_W1': _L0_ffn_in['W1'], 'L0_ffn_b1': _L0_ffn_in['b1'], 'L0_ffn_W2': _L0_ffn_in['W2'], 'L0_ffn_b2': _L0_ffn_in['b2'], 'L0_ffn_Wout': _L0_ffn_in['Wout'], 'L0_ffn_bout': _L0_ffn_in['bout'], 'L1_attn_Wi_f': _L1_attn_in['Wi_f'], 'L1_attn_conv_w_f': _L1_attn_in['conv_w_f'], 'L1_attn_conv_b_f': _L1_attn_in['conv_b_f'], 'L1_attn_dt_bias_f': _L1_attn_in['dt_bias_f'], 'L1_attn_A_log_f': _L1_attn_in['A_log_f'], 'L1_attn_D_f': _L1_attn_in['D_f'], 'L1_attn_norm_w_f': _L1_attn_in['norm_w_f'], 'L1_attn_Wo_f': _L1_attn_in['Wo_f'], 'L1_attn_Wi_b': _L1_attn_in['Wi_b'], 'L1_attn_conv_w_b': _L1_attn_in['conv_w_b'], 'L1_attn_conv_b_b': _L1_attn_in['conv_b_b'], 'L1_attn_dt_bias_b': _L1_attn_in['dt_bias_b'], 'L1_attn_A_log_b': _L1_attn_in['A_log_b'], 'L1_attn_D_b': _L1_attn_in['D_b'], 'L1_attn_norm_w_b': _L1_attn_in['norm_w_b'], 'L1_attn_Wo_b': _L1_attn_in['Wo_b'], 'L1_ffn_gate_w': _L1_ffn_in['gate_w'], 'L1_ffn_w1': _L1_ffn_in['w1'], 'L1_ffn_w2': _L1_ffn_in['w2'], 'L1_ffn_w3': _L1_ffn_in['w3']}
    _x0 = _d['L0_attn_x']
    _d['L0_attn_x'] = jax.random.normal(jax.random.fold_in(jax.random.key(seed), 1), (2, 1024, 128), dtype=_x0.dtype)
    del _x0
    return _d

def reference(L0_attn_x, L0_attn_W_qkv, L0_attn_b_qkv, L0_ffn_Win, L0_ffn_bin_, L0_ffn_W1, L0_ffn_b1, L0_ffn_W2, L0_ffn_b2, L0_ffn_Wout, L0_ffn_bout, L1_attn_Wi_f, L1_attn_conv_w_f, L1_attn_conv_b_f, L1_attn_dt_bias_f, L1_attn_A_log_f, L1_attn_D_f, L1_attn_norm_w_f, L1_attn_Wo_f, L1_attn_Wi_b, L1_attn_conv_w_b, L1_attn_conv_b_b, L1_attn_dt_bias_b, L1_attn_A_log_b, L1_attn_D_b, L1_attn_norm_w_b, L1_attn_Wo_b, L1_ffn_gate_w, L1_ffn_w1, L1_ffn_w2, L1_ffn_w3):

    def _L0_attn_ref(x, W_qkv, b_qkv):
        import jax, jax.numpy as jnp
        import numpy as np
        import math
        B, T, E, H = (2, 256, 128, 16)
        D = E // H
        THETA = 10000.0

        def _rope(x):
            d = x.shape[-1]
            t = x.shape[1]
            freqs = 1.0 / THETA ** (jnp.arange(0, d, 2, dtype=jnp.float32) / d)
            ang = jnp.arange(t, dtype=jnp.float32)[:, None] * freqs[None, :]
            cos = jnp.cos(ang)[None, :, None, :]
            sin = jnp.sin(ang)[None, :, None, :]
            xr = x[..., 0::2]
            xi = x[..., 1::2]
            o = jnp.stack([xr * cos - xi * sin, xr * sin + xi * cos], axis=-1)
            return o.reshape(x.shape)
        b, t, _ = x.shape
        qkv = x @ W_qkv.T + b_qkv
        qkv = qkv.reshape(b, t, 3, H, D)
        q, k, v = (qkv[:, :, 0], qkv[:, :, 1], qkv[:, :, 2])
        q = _rope(q)
        k = _rope(k)
        q = q.transpose(0, 2, 1, 3)
        k = k.transpose(0, 2, 1, 3)
        v = v.transpose(0, 2, 1, 3)
        scores = jnp.einsum('bhqd,bhkd->bhqk', q, k) / math.sqrt(D)
        w = jax.nn.softmax(scores, axis=-1)
        out = jnp.einsum('bhqk,bhkd->bhqd', w, v)
        return out.transpose(0, 2, 1, 3).reshape(b, t, E)

    def _L0_ffn_ref(x, Win, bin_, W1, b1, W2, b2, Wout, bout):
        import jax, jax.numpy as jnp
        import numpy as np
        D_MODEL = 128
        M = 64
        INNER = 16
        s = jnp.einsum('btd,dm->btm', x, Win) + bin_
        h = jax.nn.relu(s[..., None] * W1 + b1)
        g = jnp.einsum('btmh,mh->btm', h, W2) + b2
        out = jnp.einsum('btm,md->btd', g, Wout) + bout
        return out

    def _L1_attn_ref(u, Wi_f, conv_w_f, conv_b_f, dt_bias_f, A_log_f, D_f, norm_w_f, Wo_f, Wi_b, conv_w_b, conv_b_b, dt_bias_b, A_log_b, D_b, norm_w_b, Wo_b):
        import jax, jax.numpy as jnp
        import numpy as np
        D_MODEL = 128
        D_STATE = 128
        D_CONV = 4
        EXPAND = 2
        D_INNER = EXPAND * D_MODEL
        HEADDIM = 64
        NHEADS = D_INNER // HEADDIM
        NGROUPS = 1
        CONV_DIM = D_INNER + 2 * NGROUPS * D_STATE
        D_IN_PROJ = 2 * D_INNER + 2 * NGROUPS * D_STATE + NHEADS
        BATCH, SEQLEN = (2, 256)

        def _mamba2(u, Wi, conv_w, conv_b, dt_bias, A_log, D, norm_w, Wo):
            b, L, _ = u.shape
            zxbcdt = u @ Wi.T
            z = zxbcdt[..., :D_INNER]
            xBC = zxbcdt[..., D_INNER:D_INNER + CONV_DIM]
            dt = zxbcdt[..., D_INNER + CONV_DIM:]
            xBC_t = jnp.moveaxis(xBC, 1, 2)
            xBC_t = jnp.pad(xBC_t, ((0, 0), (0, 0), (D_CONV - 1, 0)))
            conv = jax.lax.conv_general_dilated(xBC_t, conv_w, (1,), 'VALID', feature_group_count=CONV_DIM, dimension_numbers=('NCH', 'OIH', 'NCH'))
            xBC = jax.nn.silu(jnp.moveaxis(conv, 1, 2) + conv_b)
            x = xBC[..., :D_INNER].reshape(b, L, NHEADS, HEADDIM)
            Bm = xBC[..., D_INNER:D_INNER + NGROUPS * D_STATE].reshape(b, L, D_STATE)
            Cm = xBC[..., D_INNER + NGROUPS * D_STATE:].reshape(b, L, D_STATE)
            dt = jax.nn.softplus(dt + dt_bias)
            A = -jnp.exp(A_log)

            def step(h, inp):
                x_t, B_t, C_t, dt_t = inp
                dA = jnp.exp(dt_t * A)
                h = h * dA[..., None, None] + (dt_t[..., None] * x_t)[..., None] * B_t[:, None, None, :]
                y_t = jnp.einsum('bhpn,bn->bhp', h, C_t)
                return (h, y_t)
            h0 = jnp.zeros((b, NHEADS, HEADDIM, D_STATE), u.dtype)
            xs = (jnp.moveaxis(x, 1, 0), jnp.moveaxis(Bm, 1, 0), jnp.moveaxis(Cm, 1, 0), jnp.moveaxis(dt, 1, 0))
            _, ys = jax.lax.scan(step, h0, xs)
            y = jnp.moveaxis(ys, 0, 1) + D[None, None, :, None] * x
            y = y.reshape(b, L, D_INNER)
            y = y * jax.nn.silu(z)
            y = y * jax.lax.rsqrt(jnp.mean(y * y, axis=-1, keepdims=True) + 1e-05) * norm_w
            return y @ Wo.T
        out_f = _mamba2(u, Wi_f, conv_w_f, conv_b_f, dt_bias_f, A_log_f, D_f, norm_w_f, Wo_f)
        out_b = _mamba2(u[:, ::-1], Wi_b, conv_w_b, conv_b_b, dt_bias_b, A_log_b, D_b, norm_w_b, Wo_b)
        return (out_f + out_b[:, ::-1]) * 0.5

    def _L1_ffn_ref(hidden_states, gate_w, w1, w2, w3):
        import jax, jax.numpy as jnp
        import numpy as np
        B, S, H, F, E, K = (4, 256, 128, 448, 8, 2)
        CAP_FACTOR = 1.25

        def _moe_forward(hidden_states, gate_w, w1, w2, w3):
            b, s, h = hidden_states.shape
            dtype = hidden_states.dtype
            x = hidden_states.reshape(-1, h)
            router_logits = x @ gate_w.T
            expert_weights = jax.nn.softmax(router_logits.astype(jnp.float32), axis=1)
            _, selected_experts = jax.lax.top_k(expert_weights, K)
            top_k_idx = selected_experts.reshape(b, s, K)
            probs = expert_weights.reshape(b, s, E)
            capacity = int(s * K / E * CAP_FACTOR)
            expert_mask = jax.nn.one_hot(top_k_idx, E, dtype=jnp.int32)
            mask_fused = expert_mask.reshape(b, s * K, E)
            count_fused = jnp.cumsum(mask_fused, axis=1)
            count = count_fused.reshape(b, s, K, E)
            trunc_mask = expert_mask * (count <= capacity).astype(jnp.int32)
            combined_mask = trunc_mask.sum(axis=2)
            masked_probs = probs * combined_mask
            pos_fused = mask_fused * count_fused
            pos = pos_fused.reshape(b, s, K, E)
            combined_pos = pos.sum(axis=2) * combined_mask
            pos_in_cap = jax.nn.one_hot(combined_pos, capacity + 1, dtype=jnp.int32)
            combine_mask = masked_probs[..., None] * pos_in_cap
            combine_mask = combine_mask[..., 1:].astype(dtype)
            dispatch_mask = (combine_mask != 0).astype(dtype)
            dispatch = jnp.einsum('bsm,bsec->ebcm', hidden_states, dispatch_mask)
            h1 = jnp.einsum('ebcm,emh->ebch', dispatch, w1)
            h3 = jnp.einsum('ebcm,emh->ebch', dispatch, w3)
            expert_out = jnp.einsum('ebch,ehm->ebcm', jax.nn.silu(h1) * h3, w2)
            final = jnp.einsum('ebcm,bsec->bsm', expert_out, combine_mask)
            return final
        return _moe_forward(hidden_states, gate_w, w1, w2, w3)
    x = L0_attn_x
    x = x + 0.5 * _L0_ffn_ref(_layernorm(x, axis=-1), L0_ffn_Win, L0_ffn_bin_, L0_ffn_W1, L0_ffn_b1, L0_ffn_W2, L0_ffn_b2, L0_ffn_Wout, L0_ffn_bout)
    x = x + _L0_attn_ref(_layernorm(x, axis=-1), L0_attn_W_qkv, L0_attn_b_qkv)
    x = x + 0.5 * _L0_ffn_ref(_layernorm(x, axis=-1), L0_ffn_Win, L0_ffn_bin_, L0_ffn_W1, L0_ffn_b1, L0_ffn_W2, L0_ffn_b2, L0_ffn_Wout, L0_ffn_bout)
    x = x + 0.5 * _L1_ffn_ref(_layernorm(x, axis=-1), L1_ffn_gate_w, L1_ffn_w1, L1_ffn_w2, L1_ffn_w3)
    x = x + _L1_attn_ref(_layernorm(x, axis=-1), L1_attn_Wi_f, L1_attn_conv_w_f, L1_attn_conv_b_f, L1_attn_dt_bias_f, L1_attn_A_log_f, L1_attn_D_f, L1_attn_norm_w_f, L1_attn_Wo_f, L1_attn_Wi_b, L1_attn_conv_w_b, L1_attn_conv_b_b, L1_attn_dt_bias_b, L1_attn_A_log_b, L1_attn_D_b, L1_attn_norm_w_b, L1_attn_Wo_b)
    x = x + 0.5 * _L1_ffn_ref(_layernorm(x, axis=-1), L1_ffn_gate_w, L1_ffn_w1, L1_ffn_w2, L1_ffn_w3)
    return x

_drawn_inputs = setup_inputs


def setup_inputs(seed=0):
    import zlib

    import numpy as np

    out = dict(_drawn_inputs(seed))
    spreads = {'L1_attn_conv_b_f': (0.0, 0.1),
     'L1_attn_D_f': (1.0, 0.2),
     'L1_attn_norm_w_f': (1.0, 0.2),
     'L1_attn_conv_b_b': (0.0, 0.1),
     'L1_attn_D_b': (1.0, 0.2),
     'L1_attn_norm_w_b': (1.0, 0.2)}
    factors = {'L0_ffn_bin_': 4.648}
    for name, (base, spread) in spreads.items():
        noise = np.random.default_rng([zlib.crc32(name.encode()), seed]).standard_normal(out[name].shape)
        drawn = base * np.exp(spread * noise) if base else spread * noise
        out[name] = jnp.asarray(drawn.astype(out[name].dtype))
    for name, factor in factors.items():
        out[name] = (out[name] * factor).astype(out[name].dtype)
    return out
```

```python
from contextlib import ExitStack

import numpy as np

import concourse.bass as bass
from concourse import mybir

F32 = mybir.dt.float32
BF16 = mybir.dt.bfloat16
I32 = mybir.dt.int32
U32 = mybir.dt.uint32
ALU = mybir.AluOpType
ACT = mybir.ActivationFunctionType
AX_X = mybir.AxisListType.X

P = 128
B, T, D = 2, 1024, 128
TILES = B * T // P
TPB = T // P
GROUP = 4
GROUPS = TILES // GROUP
GT = GROUP * P
BANK = 512
LN_EPS = 1e-5

M, INNER = 64, 16
ON_PE = 8
HEADS, HD = 16, 8
PARTS = 3
HG = 4
HGROUPS = HEADS // HG
QK_ROWS = PARTS * PARTS * HD
QK_PAD = 96
NO_SHIFT_BOUND = 40.0
E_, CAP, FF = 8, 320, 448
TOPK = 2
FC = 112
FCH = FF // FC
SLOTS = E_ * CAP
DIN, NST, NH, HP = 256, 128, 4, 64
TAPS = 4


def host_constants():
    c = {}
    c["identity"] = np.eye(P, dtype=np.float32)
    freqs = (1.0 / np.float32(10000.0) ** (np.arange(0, HD, 2, dtype=np.float32) / np.float32(HD))).astype(np.float32)
    ang = np.arange(T, dtype=np.float32)[None, :] * freqs[:, None]
    cos, sin = np.cos(ang).astype(np.float32), np.sin(ang).astype(np.float32)
    sign = np.where(np.arange(HD) % 2 == 0, -1.0, 1.0).astype(np.float32)
    c["rope_cos"] = np.tile(np.repeat(cos, 2, axis=0), (HEADS, 1))
    c["rope_sin"] = np.tile(np.repeat(sin, 2, axis=0) * sign[:, None], (HEADS, 1))
    c["head_of_row"] = np.kron(np.eye(HEADS, dtype=np.float32), np.ones((HD, 1), np.float32))
    c["expert_iota"] = np.arange(E_, dtype=np.float32)[None, :]
    c["token"] = np.arange(T, dtype=np.float32).reshape(TPB, P).T
    return {k: np.ascontiguousarray(v) for k, v in c.items()}


def layout(inputs):
    a = {}
    f = lambda k: np.asarray(inputs[k])
    twice = lambda v: np.concatenate([v, v], axis=0)
    a["x"] = f("L0_attn_x")
    a["win"] = f("L0_ffn_Win")
    a["ffn_w1"] = twice(f("L0_ffn_W1"))
    a["ffn_b1"] = twice(f("L0_ffn_b1"))
    a["ffn_w2"] = twice(f("L0_ffn_W2"))
    a["ffn_bin"] = twice(f("L0_ffn_bin_"))[:, None]
    a["ffn_b2"] = twice(f("L0_ffn_b2"))[:, None]
    a["wout"] = f("L0_ffn_Wout")
    a["bout"] = f("L0_ffn_bout")[None, :]
    w, b = f("L0_attn_W_qkv"), f("L0_attn_b_qkv")
    swap = np.arange(D).reshape(-1, 2)[:, ::-1].ravel()
    wq, wk, wv = w[:D], w[D:2 * D], w[2 * D:]
    bq, bk, bv = b[:D], b[D:2 * D], b[2 * D:]
    a["w_qkv"] = np.stack([wq.T, wq[swap].T, wk.T, wk[swap].T, wv.T], axis=1)
    a["b_qk"] = np.stack([bq, bq[swap], bk, bk[swap]], axis=1)
    a["b_v"] = bv[None, :]
    a["gate"] = f("L1_ffn_gate_w").T
    a["w1"] = f("L1_ffn_w1").transpose(1, 0, 2)
    a["w3"] = f("L1_ffn_w3").transpose(1, 0, 2)
    a["w2"] = f("L1_ffn_w2").reshape(E_, FCH, FC, D).transpose(2, 0, 1, 3)
    both = lambda n, g: np.stack([g(f(f"L1_attn_{n}_f")), g(f(f"L1_attn_{n}_b"))], axis=1)
    columns = lambda v: v.reshape(-1, P).T
    z_end, x_end = DIN, DIN + 4 * P
    a["mb_w_xbc"] = both("Wi", lambda w: w[z_end:x_end].T.reshape(D, 4, P))
    a["mb_w_z"] = both("Wi", lambda w: w[:z_end].T.reshape(D, 2, P))
    a["mb_w_dt"] = both("Wi", lambda w: w[x_end:].T).reshape(D, 2 * NH)
    a["mb_taps"] = both("conv_w", lambda w: w[:, 0, :].reshape(4, P, TAPS).transpose(1, 0, 2))
    a["mb_conv_b"] = both("conv_b", columns)
    a["mb_skip"] = both("D", lambda v: columns(np.repeat(v, HP)))
    a["mb_norm_w"] = both("norm_w", columns)
    a["mb_wo"] = both("Wo", lambda w: w.T.reshape(2, P, D).transpose(1, 0, 2))
    a["mb_dt_bias"] = both("dt_bias", lambda v: v[None, :]).reshape(1, 2 * NH)
    a["mb_a_log"] = both("A_log", lambda v: v[None, :]).reshape(1, 2 * NH)
    a.update(host_constants())
    return {k: np.ascontiguousarray(v) for k, v in a.items()}


class Core:

    def __init__(self, nc, dram, ctx):
        self.nc, self.dram, self.ctx = nc, dram, ctx
        self.stage_sems, self.retired = [], []

    def sb(self, name, shape, dt=F32, ctx=None):
        return (ctx or self.ctx).enter_context(self.nc.sbuf_tensor(name, shape, dt))

    def sem(self, name, ctx=None):
        s = self.nc.alloc_semaphore(name)
        if ctx is not None:
            self.stage_sems.append(s)
        return s

    def end_stage(self):
        for s in self.retired:
            self.nc.release_semaphore(s)
        numbers = sorted(s.num for s in self.stage_sems)
        while numbers:
            n = 1
            while n < len(numbers) and numbers[n] == numbers[0] + n:
                n += 1
            self.nc.gpsimd.sem_clear(range(numbers[0], numbers[0] + n))
            numbers = numbers[n:]
        self.retired, self.stage_sems = self.stage_sems, []


class Chain:

    def __init__(self, eng, sem):
        self.eng, self.sem, self.n = eng, sem, 0

    def step(self, ins):
        ins.then_inc(self.sem, 1)
        self.n += 1
        return self.n

    def wait(self):
        self.eng.wait_ge(self.sem, self.n)


class LayerNorm:

    def __init__(self, core, name, ctx, xT, psum, order=range(GROUPS), xn=None):
        self.core, self.order, self.xT = core, list(order), xT
        self.psum = psum
        self.stats = core.sb(f"{name}_stats", [P, TILES, 6], ctx=ctx)
        self.mv = core.sb(f"{name}_mv", [P, TILES, 2], ctx=ctx)
        self.std = core.sb(f"{name}_std", [P, TILES], ctx=ctx)
        self.rstd = core.sb(f"{name}_rstd", [P, TILES], ctx=ctx)
        self.xn = xn if xn is not None else core.sb(f"{name}_xn", [P, TILES, D], ctx=ctx)
        self.aggregated = core.sem(f"{name}_aggregated", ctx)
        self.rooted = core.sem(f"{name}_rooted", ctx)
        self.normed = core.sem(f"{name}_normed", ctx)
        self.turned = core.sem(f"{name}_turned", ctx)
        self.ready = core.sem(f"{name}_ready", ctx)

    def group_tiles(self, i):
        return range(self.order[i] * GROUP, self.order[i] * GROUP + GROUP)

    def vector_stats(self, dve, ch, i):
        nc, x = self.core.nc, self.core.x
        for n in self.group_tiles(i):
            ch.step(nc.vector.bn_stats(self.stats[:, n, :], x[:, n, :]))
        ch.wait()
        for n in self.group_tiles(i):
            ins = nc.vector.bn_aggr(self.mv[:, n, :], self.stats[:, n, :])
        ins.then_inc(self.aggregated, 1)

    def scalar_root(self, act, i):
        tiles = self.group_tiles(i)
        act.wait_ge(self.aggregated, i + 1)
        self.core.nc.scalar.activation(self.std[:, tiles[0]:tiles[-1] + 1], self.mv[:, tiles[0]:tiles[-1] + 1, 1], ACT.Sqrt,
                                       bias=self.core.eps[:]).then_inc(self.rooted, 1)

    def vector_group(self, dve, ch, i):
        nc, x, tiles = self.core.nc, self.core.x, self.group_tiles(i)
        dve.wait_ge(self.aggregated, i + 1)
        dve.wait_ge(self.rooted, i + 1)
        ch.step(nc.vector.reciprocal(self.rstd[:, tiles[0]:tiles[-1] + 1], self.std[:, tiles[0]:tiles[-1] + 1]))
        ch.wait()
        for n in tiles:
            ins = nc.vector.tensor_scalar(self.xn[:, n, :], x[:, n, :], self.mv[:, n, 0:1], self.rstd[:, n:n + 1],
                                          ALU.subtract, ALU.mult)
        ins.then_inc(self.normed, 1)

    def tensor_group(self, pe, i):
        nc = self.core.nc
        pe.wait_ge(self.normed, i + 1)
        if i >= 2:
            pe.wait_ge(self.ready, i - 1)
        for j in range(GROUP):
            ins = nc.tensor.transpose(self.psum[:, i % 2, j * P:(j + 1) * P], self.xn[:, self.order[i] * GROUP + j, :],
                                      self.core.ident[:])
        ins.then_inc(self.turned, 1)

    def scalar_group(self, act, i):
        act.wait_ge(self.turned, i + 1)
        g = self.order[i]
        self.core.nc.scalar.copy(self.xT[:, g * GT:(g + 1) * GT], self.psum[:, i % 2, :]).then_inc(self.ready, 1)


def load_constants(core, ctx):
    nc, d = core.nc, core.dram
    core.x = core.sb("x_sb", [P, TILES, D])
    core.ident = core.sb("ident", [P, P])
    core.eps = core.sb("eps", [P, 1])
    core.loaded = {}

    def wait(eng, *names):
        for n in names:
            eng.wait_ge(core.loaded[n], 16)
    core.landed = wait


def load_ffn(core, ctx):
    sb = lambda n, shape: core.sb(n, shape, ctx=ctx)
    core.win = sb("win_sb", [D, M])
    core.w1 = sb("w1_sb", [P, INNER])
    core.b1 = sb("b1_sb", [P, INNER])
    core.w2 = sb("w2_sb", [P, INNER])
    core.bin = sb("bin_sb", [P, 1])
    core.b2 = sb("b2_sb", [P, 1])
    core.wout = sb("wout_sb", [P, B, D])
    core.bout = sb("bout_sb", [P, D])
    core.b_pre = sb("b_pre", [P, INNER])
    core.diag = sb("diag", [P, ON_PE, P])
    core.bout_half = sb("bout_half", [P, D])


class Setup:

    def __init__(self, core):
        d, self.core = core.dram, core
        tokens = d["x"].rearrange("b (j p) d -> p (b j) d", p=P)
        groups = [slice(g * GROUP, (g + 1) * GROUP) for g in range(GROUPS)]
        self.x_loads = [(f"x{g}", core.x[:, s, :], tokens[:, s, :]) for g, s in enumerate(groups)]
        self.ffn_loads = [("ident", core.ident[:], d["identity"]), ("win", core.win[:], d["win"]),
                          ("ffn_w1", core.w1[:], d["ffn_w1"]), ("ffn_b1", core.b1[:], d["ffn_b1"]), ("ffn_bin", core.bin[:], d["ffn_bin"]),
                          ("ffn_w2", core.w2[:], d["ffn_w2"]), ("ffn_b2", core.b2[:], d["ffn_b2"]),
                          ("bout", core.bout[:], d["bout"].to_broadcast([P, D])),
                          ("wout_0", core.wout[0:M, 0, :], d["wout"]), ("wout_1", core.wout[M:P, 1, :], d["wout"])]
        for name, _, _ in (*self.x_loads, *self.ffn_loads):
            core.loaded[name] = core.sem(f"ld_{name}")
        self.zeros = core.sb("zeros", [P, SLOTS // P, core.moe.ROW], ctx=core.early)
        self.zeroed, self.ones_set, self.tri_set, self.set = (core.sem(n) for n in ("zeroed", "ones_set", "tri_set", "constants_set"))

    def start(self, eng, loads):
        for name, dst, src in loads:
            eng.dma_start(dst, src).then_inc(self.core.loaded[name], 16)

    def sync(self, sp):
        core, moe = self.core, self.core.moe
        self.start(sp, self.x_loads)
        self.start(sp, (*core.attention.loads, *moe.loads, *core.mamba.loads))
        sp.wait_ge(self.zeroed, 2)
        for r in range(2 * B):
            sp.dma_start(moe.slots[r].rearrange("(p n) d -> p n d", p=P), self.zeros[:]).then_inc(moe.cleared, 16)
            sp.dma_start(moe.rows[r].rearrange("(p n) d -> p n d", p=P), self.zeros[:, 0:TOPK * T // P, 0:D]).then_inc(moe.cleared, 16)

    def scalar(self, act):
        self.start(act, self.ffn_loads)

    def vector(self, dve):
        nc, core = self.core.nc, self.core
        nc.vector.memset(core.eps[:], LN_EPS).then_inc(self.set, 1)
        nc.vector.memset(core.wout[0:M, 1, :], 0.0).then_inc(self.set, 1)
        nc.vector.memset(core.wout[M:P, 0, :], 0.0).then_inc(self.set, 1)

    def gpsimd(self, pool):
        nc, moe, zeros = self.core.nc, self.core.moe, self.zeros
        nc.gpsimd.memset(zeros[:], 0.0).then_inc(self.zeroed, 1)
        nc.gpsimd.memset(moe.tri[:], 1.0).then_inc(self.ones_set, 1)
        pool.wait_ge(self.zeroed, 1)
        nc.gpsimd.memset(zeros[:, :, moe.TOKEN], moe.NOWHERE).then_inc(self.zeroed, 1)
        pool.wait_ge(self.ones_set, 1)
        nc.gpsimd.affine_select(out=moe.tri[:, 0, :], in_=moe.tri[:, 0, :], compare_op=ALU.is_ge, fill=0.0, base=0,
                                pattern=[[1, P]], channel_multiplier=-1).then_inc(self.tri_set, 1)


def ffn(core, name, setup=None):
    nc, ctx = core.nc, ExitStack()
    RING = 4
    xT = core.sb(f"{name}_xT", [D, B * T], ctx=ctx)
    relu = core.sb(f"{name}_relu", [P, RING, T], ctx=ctx)
    acc = core.sb(f"{name}_acc", [P, T], ctx=ctx)
    mix = core.sb(f"{name}_mix", [P, T], ctx=ctx)
    xb = core.sb(f"{name}_xb", [P, TILES, D], ctx=ctx)
    psum = lambda n, shape: ctx.enter_context(nc.psum_tensor(f"{name}_{n}", shape, F32))
    ps_t, ps_s, ps_g, ps_o = psum("ps_t", [P, 2, BANK]), psum("ps_s", [P, T]), psum("ps_g", [P, T]), psum("ps_o", [P, 2, BANK])
    sem = lambda n: core.sem(f"{name}_{n}", ctx)
    s_done, relu_done, pe_used, dve_used = sem("s_done"), sem("relu_done"), sem("pe_used"), sem("dve_used")
    mixed, out_done, out_read, xb_done, steps = sem("mixed"), sem("out_done"), sem("out_read"), sem("xb_done"), sem("steps")
    made = sem("made")
    ln = LayerNorm(core, f"{name}_ln", ctx, xT, ps_t)
    on_pe = [h for h in range(INNER) if h % 2 == 1]
    on_dve = [h for h in range(INNER) if h % 2 == 0]
    slot = {h: i for i, h in enumerate(on_pe)}

    def freed(eng, h):
        if h >= RING:
            old = h - RING
            if old in on_pe:
                eng.wait_ge(pe_used, on_pe.index(old) + 1)
            else:
                eng.wait_ge(dve_used, on_dve.index(old) + 1)

    with nc.Block() as block:
        @block.sync
        def _(sp):
            if setup:
                setup.sync(sp)

        @block.vector
        def _(dve):
            ch = Chain(dve, steps)
            if setup:
                setup.vector(dve)
            for i in range(GROUPS):
                core.landed(dve, f"x{i}")
                ln.vector_stats(dve, ch, i)
            if setup:
                core.landed(dve, "ffn_w1", "ffn_b1", "ffn_bin")
                nc.vector.scalar_tensor_tensor(core.b_pre[:], core.w1[:], core.bin[:], core.b1[:], ALU.mult, ALU.add).then_inc(made, 1)
                core.landed(dve, "bout")
                nc.vector.tensor_scalar(core.bout_half[:], core.bout[:], 0.5, None, ALU.mult).then_inc(made, 1)
            for i in range(GROUPS):
                ln.vector_group(dve, ch, i)
            core.landed(dve, "ffn_w2", "ident", "ffn_b2")
            if setup:
                for n in range(ON_PE):
                    ins = nc.vector.tensor_scalar(core.diag[:, n, :], core.ident[:], core.w2[:, 2 * n + 1:2 * n + 2], None, ALU.mult)
                ins.then_inc(made, 1)
            for n, h in enumerate(on_dve):
                dve.wait_ge(relu_done, h + 1)
                if n == 0:
                    ins = nc.vector.tensor_scalar(acc[:], relu[:, h % RING, :], core.w2[:, h:h + 1], None, ALU.mult)
                else:
                    dve.wait_ge(dve_used, n)
                    ins = nc.vector.scalar_tensor_tensor(acc[:], relu[:, h % RING, :], core.w2[:, h:h + 1], acc[:],
                                                         ALU.mult, ALU.add)
                ins.then_inc(dve_used, 1)
            dve.wait_ge(dve_used, len(on_dve))
            dve.wait_ge(pe_used, len(on_pe))
            for i in range(2):
                nc.vector.scalar_tensor_tensor(mix[:, i * BANK:(i + 1) * BANK], ps_g[:, i * BANK:(i + 1) * BANK], core.b2[:],
                                               acc[:, i * BANK:(i + 1) * BANK], ALU.add, ALU.add).then_inc(mixed, 1)
            dve.wait_ge(xb_done, 1)
            for g in range(GROUPS):
                dve.wait_ge(out_done, g + 1)
                nc.vector.scalar_tensor_tensor(core.x[:, g * GROUP:(g + 1) * GROUP, :].rearrange("p a d -> p (a d)"),
                                               ps_o[:, g % 2, :], 0.5,
                                               xb[:, g * GROUP:(g + 1) * GROUP, :].rearrange("p a d -> p (a d)"),
                                               ALU.mult, ALU.add).then_inc(out_read, 1)

        @block.gpsimd
        def _(pool):
            if setup:
                setup.gpsimd(pool)
                core.landed(pool, "x0", "x1", "x2", "x3")
                pool.wait_ge(made, 2)
            nc.gpsimd.tensor_tensor(xb[:], core.x[:], core.bout_half[:].unsqueeze(1).to_broadcast([P, TILES, D]),
                                    ALU.add).then_inc(xb_done, 1)

        @block.scalar
        def _(act):
            if setup:
                setup.scalar(act)
                act.wait_ge(setup.set, 3)
            for i in range(GROUPS):
                ln.scalar_root(act, i)
            for i in range(GROUPS):
                ln.scalar_group(act, i)
            act.wait_ge(s_done, GROUPS)
            if setup:
                act.wait_ge(made, 1)
            for h in range(INNER):
                freed(act, h)
                nc.scalar.activation(relu[:, h % RING, :], ps_s[:], ACT.Relu, bias=core.b_pre[:, h:h + 1],
                                     scale=core.w1[:, h:h + 1]).then_inc(relu_done, 1)

        @block.tensor
        def _(pe):
            core.landed(pe, "ident", "win", "wout_0", "wout_1")
            for i in range(GROUPS):
                ln.tensor_group(pe, i)
                pe.wait_ge(ln.ready, i + 1)
                b, half = i // 2, i % 2
                nc.tensor.matmul(ps_s[M * b:M * b + M, half * GT:(half + 1) * GT], core.win[:], xT[:, i * GT:(i + 1) * GT],
                                 start=True, stop=True).then_inc(s_done, 1)
            if setup:
                pe.wait_ge(made, 3)
            for n, h in enumerate(on_pe):
                pe.wait_ge(relu_done, h + 1)
                for i in range(2):
                    ins = nc.tensor.matmul(ps_g[:, i * BANK:(i + 1) * BANK], core.diag[:, n, :],
                                           relu[:, h % RING, i * BANK:(i + 1) * BANK], start=(n == 0), stop=(n == len(on_pe) - 1))
                ins.then_inc(pe_used, 1)
            if setup:
                pe.wait_ge(setup.set, 3)
            for g in range(GROUPS):
                pe.wait_ge(mixed, 2 if g % 2 else 1)
                if g >= 2:
                    pe.wait_ge(out_read, g - 1)
                for j in range(GROUP):
                    t = (g % 2) * GROUP + j
                    ins = nc.tensor.matmul(ps_o[:, g % 2, j * D:(j + 1) * D], mix[:, t * P:(t + 1) * P],
                                           core.wout[:, g // 2, :], start=True, stop=True)
                ins.then_inc(out_done, 1)
    ctx.close()


class Attention:

    def __init__(self, core, name):
        nc = core.nc
        self.core, self.name, self.ctx = core, name, core.early
        dram = lambda n, shape, dt: nc.dram_tensor(f"{name}_{n}", shape, dt).ap()
        self.q_parts = dram("q_parts", (B, HEADS, PARTS, HD, T), BF16)
        self.k_parts = dram("k_parts", (B, HEADS, 2 * PARTS - 1, HD, T), BF16)
        self.shift = dram("shift", (B, HEADS, PARTS, T), BF16)
        self.v = core.sb(f"{name}_v", [P, TILES, HEADS, 32], ctx=self.ctx)
        self.flag = core.sb(f"{name}_flag", [1, 1], I32, ctx=self.ctx)
        sb, d = (lambda n, shape: core.sb(f"{name}_{n}", shape, ctx=self.ctx)), core.dram
        self.w, self.b_qk, self.b_v = sb("w", [D, 5, D]), sb("b_qk", [D, 4]), sb("b_v", [P, D])
        self.cos, self.sin, self.head_of_row = sb("cos", [D, T]), sb("sin", [D, T]), sb("head_of_row", [P, HEADS])
        self.loads = [("w_qkv", self.w[:], d["w_qkv"]), ("b_qk", self.b_qk[:], d["b_qk"]), ("rope_cos", self.cos[:], d["rope_cos"]),
                      ("rope_sin", self.sin[:], d["rope_sin"]), ("b_v", self.b_v[:], d["b_v"].to_broadcast([P, D])),
                      ("head_of_row", self.head_of_row[:], d["head_of_row"])]
        for n, _, _ in self.loads:
            core.loaded[n] = core.sem(f"ld_{n}")

    def sem(self, n, ctx):
        return self.core.sem(f"{self.name}_{n}", ctx)

    def prepare(self):
        core, nc, name = self.core, self.core.nc, self.name
        with ExitStack() as ctx:
            sb = lambda n, shape, dt=F32: core.sb(f"{name}_{n}", shape, dt, ctx)
            sem = lambda n: self.sem(n, ctx)
            psum = lambda n, shape: ctx.enter_context(nc.psum_tensor(f"{name}_{n}", shape, F32))
            xT = sb("xT", [D, B * T])
            w, b_qk, b_v, cos, sin, head_of_row = self.w, self.b_qk, self.b_v, self.cos, self.sin, self.head_of_row
            t_cos, t_sin, rot, rest = sb("t_cos", [D, 2, GT]), sb("t_sin", [D, 2, GT]), sb("rot", [D, 2, GT]), sb("rest", [D, 2, GT])
            parts = sb("parts", [D, 2, PARTS, B * T], BF16)
            zero = sb("zero", [P, PARTS * B * HEADS * T // P], BF16)
            peaks = sb("peaks", [D, 2, GROUPS])
            peak = sb("peak", [D, 2, B])
            bound_rows = sb("bound_rows", [D, B])
            bound = sb("bound", [1, 1])
            ps_t, ps_qk, ps_v = psum("ps_t", [P, 2, BANK]), psum("ps_qk", [P, 4, BANK]), psum("ps_v", [P, 2, BANK])
            ln = LayerNorm(core, f"{name}_ln", ctx, xT, ps_t)
            steps, qk_done, v_done, v_read, v_filled = sem("steps"), sem("qk_done"), sem("v_done"), sem("v_read"), sem("v_filled")
            qk_read, rot_done, part0, rest_done, part1, part2 = (sem(n) for n in ("qk_read", "rot_done", "part0", "rest_done",
                                                                                   "part1", "part2"))
            scratch, zeroed, shift_clear = sem("scratch"), sem("zeroed"), sem("shift_clear")
            rows_done, bound_done = sem("rows_done"), sem("bound_done")

            with nc.Block() as block:
                @block.sync
                def _(sp):
                    sp.wait_ge(zeroed, 1)
                    sp.dma_start(self.shift.rearrange("b h i t -> (b h i t)").rearrange("(p n) -> p n", p=P), zero[:])\
                      .then_inc(shift_clear, 16)
                    for b in range(B):
                        sp.wait_ge(part0, 4 * (b + 1))
                        sp.wait_ge(part1, 4 * (b + 1))
                        sp.wait_ge(part2, 4 * (b + 1))
                        for which, dst, n in ((0, self.q_parts, PARTS), (1, self.k_parts, 2 * PARTS - 1)):
                            for j in range(n):
                                sp.dma_start(dst[b, :, j, :, :], parts[:, which, j % PARTS, b * T:(b + 1) * T]).then_inc(scratch, 16)
                    sp.wait_ge(scratch, 16 * B * (3 * PARTS - 1))
                    sp.wait_ge(shift_clear, 16)

                @block.gpsimd
                def _(pool):
                    nc.gpsimd.memset(zero[:], 0.0).then_inc(zeroed, 1)
                    nc.gpsimd.memset(self.v[:], 0.0).then_inc(v_filled, 1)
                    pool.wait_ge(v_filled, 1)
                    nc.gpsimd.memset(self.v[:, :, :, HD:HD + 1], 1.0).then_inc(v_filled, 1)

                @block.vector
                def _(dve):
                    ch = Chain(dve, steps)
                    for i in range(GROUPS):
                        ln.vector_stats(dve, ch, i)
                    for i in range(GROUPS):
                        ln.vector_group(dve, ch, i)
                    core.landed(dve, "b_qk", "rope_cos", "rope_sin", "b_v")
                    dve.wait_ge(v_filled, 2)
                    for i in range(GROUPS):
                        at = slice((i % 2) * GT, (i % 2) * GT + GT)
                        to = slice(i * GT, (i + 1) * GT)
                        for k in range(2):
                            dve.wait_ge(qk_done, 2 * i + k + 1)
                            nc.vector.scalar_tensor_tensor(t_cos[:, k, :], ps_qk[:, 2 * k, :], b_qk[:, 2 * k:2 * k + 1], cos[:, at],
                                                           ALU.add, ALU.mult)
                            ins = nc.vector.scalar_tensor_tensor(t_sin[:, k, :], ps_qk[:, 2 * k + 1, :], b_qk[:, 2 * k + 1:2 * k + 2],
                                                                 sin[:, at], ALU.add, ALU.mult)
                            ins.then_inc(qk_read, 1)
                        dve.wait_ge(qk_read, 2 * i + 2)
                        for k in range(2):
                            nc.vector.tensor_tensor(rot[:, k, :], t_cos[:, k, :], t_sin[:, k, :], ALU.add).then_inc(rot_done, 1)
                        dve.wait_ge(v_done, i + 1)
                        nc.vector.tensor_tensor(self.v[:, i * GROUP:(i + 1) * GROUP, :, 0:HD],
                                                ps_v[:, i % 2, :].rearrange("p (j h d) -> p j h d", j=GROUP, h=HEADS),
                                                b_v[:].rearrange("p (h d) -> p h d", h=HEADS).unsqueeze(1)
                                                .to_broadcast([P, GROUP, HEADS, HD]), ALU.add).then_inc(v_read, 1)
                        dve.wait_ge(rot_done, 2 * i + 2)
                        nc.vector.tensor_reduce(peaks[:, :, i:i + 1], rot[:], AX_X, ALU.max, apply_absolute_value=True)
                        for k in range(2):
                            dve.wait_ge(part0, 2 * i + k + 1)
                            nc.vector.tensor_tensor(rest[:, k, :], rot[:, k, :], parts[:, k, 0, to], ALU.subtract).then_inc(rest_done, 1)
                        dve.wait_ge(rest_done, 2 * i + 2)
                        for k in range(2):
                            dve.wait_ge(part1, 2 * i + k + 1)
                            nc.vector.tensor_tensor(parts[:, k, 2, to], rest[:, k, :], parts[:, k, 1, to], ALU.subtract).then_inc(part2, 1)
                    dve.wait_ge(part2, 2 * GROUPS)
                    ch.step(nc.vector.tensor_reduce(peak[:].rearrange("p k b -> p (k b)").unsqueeze(2),
                                                    peaks[:].rearrange("p k (b g) -> p (k b) g", b=B), AX_X, ALU.max))
                    ch.wait()
                    nc.vector.tensor_tensor(bound_rows[:], peak[:, 0, :], peak[:, 1, :], ALU.mult).then_inc(rows_done, 1)
                    dve.wait_ge(bound_done, 1)
                    ch.step(nc.vector.reduce_max(bound[:], ps_v[0:1, 0, 0:B * HEADS], AX_X))
                    ch.wait()
                    nc.vector.tensor_scalar(self.flag[:], bound[:], NO_SHIFT_BOUND * HD ** 0.5, None, ALU.is_gt)

                @block.scalar
                def _(act):
                    for i in range(GROUPS):
                        ln.scalar_root(act, i)
                    for i in range(GROUPS):
                        ln.scalar_group(act, i)
                    for i in range(GROUPS):
                        to = slice(i * GT, (i + 1) * GT)
                        for k in range(2):
                            act.wait_ge(rot_done, 2 * i + k + 1)
                            nc.scalar.copy(parts[:, k, 0, to], rot[:, k, :]).then_inc(part0, 1)
                        for k in range(2):
                            act.wait_ge(rest_done, 2 * i + k + 1)
                            nc.scalar.copy(parts[:, k, 1, to], rest[:, k, :]).then_inc(part1, 1)

                @block.tensor
                def _(pe):
                    core.landed(pe, "ident")
                    for i in range(GROUPS):
                        ln.tensor_group(pe, i)
                    core.landed(pe, "w_qkv")
                    for i in range(GROUPS):
                        pe.wait_ge(ln.ready, i + 1)
                        for k in range(2):
                            if i >= 1:
                                pe.wait_ge(qk_read, 2 * (i - 1) + k + 1)
                            for s in range(2):
                                ins = nc.tensor.matmul(ps_qk[:, 2 * k + s, :], w[:, 2 * k + s, :], xT[:, i * GT:(i + 1) * GT],
                                                       start=True, stop=True)
                            ins.then_inc(qk_done, 1)
                        if i >= 2:
                            pe.wait_ge(v_read, i - 1)
                        for j in range(GROUP):
                            n = i * GROUP + j
                            ins = nc.tensor.matmul(ps_v[:, i % 2, j * D:(j + 1) * D], xT[:, n * P:(n + 1) * P], w[:, 4, :],
                                                   start=True, stop=True)
                        ins.then_inc(v_done, 1)
                    core.landed(pe, "head_of_row")
                    pe.wait_ge(rows_done, 1)
                    pe.wait_ge(v_read, GROUPS)
                    for b in range(B):
                        ins = nc.tensor.matmul(ps_v[0:1, 0, b * HEADS:(b + 1) * HEADS], bound_rows[:, b:b + 1], head_of_row[:],
                                               start=True, stop=True)
                    ins.then_inc(bound_done, 1)

    def load_heads(self, eng, q, k, b, hg, landed):
        heads = slice(hg * HG, (hg + 1) * HG)
        for r in range(PARTS):
            rows = slice(r * PARTS * HD, (r + 1) * PARTS * HD)
            eng.dma_start(q[rows, :, :], self.q_parts[b, heads].rearrange("h i d t -> (i d) h t")).then_inc(landed, 16)
            eng.dma_start(k[rows, :, :], self.k_parts[b, heads, r:r + PARTS].rearrange("h i d t -> (i d) h t")).then_inc(landed, 16)

    def find_shift(self):
        core, nc, name = self.core, self.core.nc, self.name
        STEPS = HG * TPB
        NG = B * HGROUPS
        LOADS = 2 * PARTS
        with ExitStack() as ctx:
            sb = lambda n, shape, dt=F32: core.sb(f"{name}_{n}", shape, dt, ctx)
            sem = lambda n: self.sem(n, ctx)
            q, k = sb("shift_q", [QK_ROWS, HG, T], BF16), sb("shift_k", [QK_ROWS, HG, T], BF16)
            peak, rest = sb("shift_peak", [P, HG, TPB]), sb("shift_rest", [P, HG, TPB])
            parts = sb("shift_parts", [P, PARTS, HG, TPB], BF16)
            ps = ctx.enter_context(nc.psum_tensor(f"{name}_shift_ps", [P, 2, T], F32))
            free, landed, scored, maxed, own, split, stored = (
                sem(f"shift_{n}") for n in ("free", "landed", "scored", "maxed", "own", "split", "stored"))
            groups = lambda ap: ap.rearrange("b (g h) i d t -> (b g) h i d t", h=HG)

            def needed(eng):
                flag = eng.alloc_register(f"{name}_needs_shift")
                eng.reg_load(flag, self.flag[0:1, 0:1])
                return eng.If_ne(flag, 0)

            with nc.Block() as block:
                @block.sync
                def _(sp):
                    with needed(sp):
                        sp.sem_inc(free, 1)
                        with sp.Fori(0, NG) as g:
                            sp.wait_ge(free, g + 1)
                            for r in range(PARTS):
                                rows = slice(r * PARTS * HD, (r + 1) * PARTS * HD)
                                sp.dma_start(q[rows, :, :], groups(self.q_parts)[bass.ds(g, 1)].rearrange("g h i d t -> (g i d) h t"))\
                                  .then_inc(landed, 16)
                                sp.dma_start(k[rows, :, :], groups(self.k_parts)[bass.ds(g, 1), :, r:r + PARTS]
                                             .rearrange("g h i d t -> (g i d) h t")).then_inc(landed, 16)
                            sp.wait_ge(split, g + 1)
                            dst = self.shift.rearrange("b (g h) i t -> (b g) h i t", h=HG)[bass.ds(g, 1)]
                            for i in range(PARTS):
                                for h in range(HG):
                                    with nc.allow_non_contiguous_dma("one value of a query to a row"):
                                        sp.dma_start(dst[:, h, i, :].rearrange("g (j p) -> (g p) j", p=P), parts[:, i, h, :]).then_inc(stored, 16)
                            sp.wait_ge(stored, 16 * PARTS * HG * (g + 1))
                            sp.sem_inc(free, 1)

                @block.tensor
                def _(pe):
                    with needed(pe):
                        with pe.Fori(0, NG) as g:
                            pe.wait_ge(landed, 16 * LOADS * (g + 1))
                            for n in range(STEPS):
                                pe.wait_ge(maxed, STEPS * g + n + 1)
                                for half in range(2):
                                    ins = nc.tensor.matmul(ps[:, n % 2, half * BANK:(half + 1) * BANK], q[:, n // TPB, n % TPB * P:n % TPB * P + P],
                                                           k[:, n // TPB, half * BANK:(half + 1) * BANK], start=True, stop=True)
                                ins.then_inc(scored, 1)

                @block.vector
                def _(dve):
                    with needed(dve):
                        dve.sem_inc(maxed, 2)
                        with dve.Fori(0, NG) as g:
                            for n in range(STEPS):
                                dve.wait_ge(scored, STEPS * g + n + 1)
                                nc.vector.reduce_max(peak[:, n // TPB, n % TPB:n % TPB + 1], ps[:, n % 2, :], AX_X).then_inc(maxed, 1)
                            dve.wait_ge(maxed, STEPS * (g + 1) + 2)
                            dve.wait_ge(free, g + 1)
                            nc.vector.tensor_scalar(parts[:, 0, :, :], peak[:], -1.0, None, ALU.mult).then_inc(own, 1)
                            dve.wait_ge(own, 3 * g + 1)
                            nc.vector.scalar_tensor_tensor(rest[:], peak[:], -1.0, parts[:, 0, :, :], ALU.mult, ALU.subtract).then_inc(own, 1)
                            dve.wait_ge(own, 3 * g + 2)
                            nc.vector.tensor_copy(parts[:, 1, :, :], rest[:]).then_inc(own, 1)
                            dve.wait_ge(own, 3 * g + 3)
                            nc.vector.tensor_tensor(parts[:, 2, :, :], rest[:], parts[:, 1, :, :], ALU.subtract).then_inc(split, 1)

    def attend(self):
        core, nc, name = self.core, self.core.nc, self.name
        UNITS = 2 * TPB
        SB_, PB = 3, 3
        blocks = [(b, hg, half) for b in range(B) for hg in range(HGROUPS) for half in range(2)]
        LOADS = 2 * PARTS + 1
        with ExitStack() as ctx:
            sb = lambda n, shape, dt=F32: core.sb(f"{name}_{n}", shape, dt, ctx)
            sem = lambda n: self.sem(n, ctx)
            psum = lambda n, shape: ctx.enter_context(nc.psum_tensor(f"{name}_{n}", shape, F32))
            q = [sb(f"q{i}", [QK_PAD, HG, T], BF16) for i in range(2)]
            k = [sb(f"k{i}", [QK_PAD, HG, T], BF16) for i in range(2)]
            p = sb("p", [P, PB, 2, BANK])
            mixed = sb("mixed", [P, 2, BANK])
            rden = sb("rden", [P, GROUP, HG])
            scaled = sb("scaled", [P, GROUP, HG, HD])
            ps_s, ps_av, ps_o = psum("ps_s", [P, SB_, 2, BANK]), psum("ps_av", [P, BANK]), psum("ps_o", [P, BANK])
            padded = sem("padded")
            landed = [sem(f"heads{i}") for i in range(2)]
            scored, exped, summed, av_read, turned, den_done, out_done, o_read = (
                sem(n) for n in ("scored", "exped", "summed", "av_read", "turned", "den_done", "out_done", "o_read"))

            with nc.Block() as block:
                @block.sync
                def _(sp):
                    sp.wait_ge(padded, 4)
                    for n, (b, hg) in enumerate((b, hg) for b in range(B) for hg in range(HGROUPS)):
                        if n >= 2:
                            sp.wait_ge(scored, 2 * UNITS * (n - 1))
                        self.load_heads(sp, q[n % 2], k[n % 2], b, hg, landed[n % 2])
                        sp.dma_start(q[n % 2][QK_ROWS:QK_ROWS + PARTS, :, :],
                                     self.shift[b, hg * HG:(hg + 1) * HG].rearrange("h i t -> i h t")).then_inc(landed[n % 2], 16)
                    sp.wait_ge(core.moe.cleared, 16 * 2 * 2 * B)

                @block.gpsimd
                def _(pool):
                    for i in range(2):
                        nc.gpsimd.memset(q[i][64:QK_PAD, :, :], 0.0).then_inc(padded, 1)
                        nc.gpsimd.memset(k[i][64:QK_PAD, :, :], 1.0).then_inc(padded, 1)

                @block.tensor
                def _(pe):
                    def scores(n, u):
                        b, hg, half = blocks[n]
                        w, i = n * UNITS + u, n // 2
                        kt, pair = u // 2, u % 2
                        if u == 0:
                            pe.wait_ge(landed[i % 2], 16 * LOADS * (i // 2 + 1))
                        if w >= SB_:
                            pe.wait_ge(exped, w - SB_ + 1)
                        for j in range(2):
                            h = 2 * pair + j
                            ins = nc.tensor.matmul(ps_s[:, w % SB_, j, :], k[i % 2][:, h, kt * P:(kt + 1) * P],
                                                   q[i % 2][:, h, half * BANK:(half + 1) * BANK], start=True, stop=True)
                        ins.then_inc(scored, 1)

                    def weigh(n, u):
                        b, hg, half = blocks[n]
                        w = n * UNITS + u
                        kt, pair = u // 2, u % 2
                        if u == 0 and n >= 1:
                            pe.wait_ge(av_read, n)
                        pe.wait_ge(exped, w + 1)
                        for j in range(2):
                            h = 2 * pair + j
                            ins = nc.tensor.matmul(ps_av[32 * h:32 * h + 32, :], self.v[:, b * TPB + kt, hg * HG + h, :],
                                                   p[:, w % PB, j, :], start=(kt == 0), stop=(kt == TPB - 1))
                        ins.then_inc(summed, 1)

                    def turn(n):
                        pe.wait_ge(av_read, n + 1)
                        if n >= 1:
                            pe.wait_ge(o_read, n)
                        for j in range(GROUP):
                            ins = nc.tensor.transpose(ps_o[:, j * P:(j + 1) * P], mixed[:, n % 2, j * P:(j + 1) * P], core.ident[:])
                        ins.then_inc(turned, 1)

                    AHEAD = 2
                    total = len(blocks) * UNITS
                    for w in range(total + AHEAD):
                        if w < total:
                            scores(w // UNITS, w % UNITS)
                        if w >= AHEAD:
                            weigh((w - AHEAD) // UNITS, (w - AHEAD) % UNITS)
                        if w >= UNITS + 5 and (w - 5) % UNITS == 0:
                            turn((w - 5) // UNITS - 1)
                    turn(len(blocks) - 1)

                @block.scalar
                def _(act):
                    for w in range(len(blocks) * UNITS):
                        act.wait_ge(scored, w + 1)
                        if w >= PB:
                            act.wait_ge(summed, w - PB + 1)
                        nc.scalar.activation(p[:, w % PB, :, :].rearrange("p a n -> p (a n)"),
                                             ps_s[:, w % SB_, :, :].rearrange("p a n -> p (a n)"), ACT.Exp,
                                             scale=float(HD) ** -0.5).then_inc(exped, 1)

                @block.vector
                def _(dve):
                    for n, (b, hg, half) in enumerate(blocks):
                        dve.wait_ge(summed, UNITS * (n + 1))
                        if n >= 2:
                            dve.wait_ge(turned, n - 1)
                        nc.vector.tensor_copy(mixed[:, n % 2, :], ps_av[:]).then_inc(av_read, 1)
                        dve.wait_ge(turned, n + 1)
                        o = ps_o[:].rearrange("p (j h c) -> p j h c", j=GROUP, h=HG)
                        nc.vector.reciprocal(rden[:], o[:, :, :, HD]).then_inc(den_done, 1)
                        dve.wait_ge(den_done, n + 1)
                        nc.vector.tensor_tensor(scaled[:], o[:, :, :, 0:HD], rden[:].unsqueeze(3).to_broadcast([P, GROUP, HG, HD]),
                                                ALU.mult).then_inc(o_read, 1)
                        dve.wait_ge(o_read, n + 1)
                        n0 = b * TPB + half * GROUP
                        xs = core.x[:, n0:n0 + GROUP, hg * HG * HD:(hg + 1) * HG * HD]
                        nc.vector.tensor_tensor(xs, xs, scaled[:].rearrange("p j h d -> p j (h d)"), ALU.add).then_inc(out_done, 1)


def attention(core):
    a = core.attention
    a.prepare()
    core.end_stage()
    a.find_shift()
    core.end_stage()
    a.attend()


class SideBanks:

    def __init__(self, psum):
        self.psum, self.bank, self.reader, self.uses = psum, {}, [None, None], 0

    def take(self, pe, use, read, count):
        n = self.uses % 2
        if self.reader[n] is not None:
            pe.wait_ge(*self.reader[n])
        self.bank[use], self.reader[n], self.uses = n, (read, count), self.uses + 1
        return self.psum[:, n, :]

    def of(self, use):
        return self.psum[:, self.bank[use], :]


class Norm:

    def __init__(self, core, name, ctx, xn, xT, side, groups):
        self.core, self.xn, self.xT, self.side, self.groups = core, xn, xT, side, groups
        small = lambda n, shape: core.sb(f"{name}_{n}", shape, ctx=ctx)
        self.stats, self.mv = small("stats", [P, TILES, 6]), small("mv", [P, TILES, 2])
        self.std, self.rstd = small("std", [P, TILES]), small("rstd", [P, TILES])
        sem = lambda n: core.sem(f"{name}_{n}", ctx)
        self.aggregated, self.rooted = sem("aggregated"), sem("rooted")
        self.normed, self.turned, self.ready = sem("normed"), sem("turned"), sem("ready")

    def tiles(self, i):
        return slice(self.groups[i] * GROUP, (self.groups[i] + 1) * GROUP)

    def stats_of(self, dve, ch, i):
        nc, tiles = self.core.nc, range(TILES)[self.tiles(i)]
        for n in tiles:
            ch.step(nc.vector.bn_stats(self.stats[:, n, :], self.core.x[:, n, :]))
        ch.wait()
        for n in tiles:
            ins = nc.vector.bn_aggr(self.mv[:, n, :], self.stats[:, n, :])
        ins.then_inc(self.aggregated, 1)

    def root(self, act, i):
        act.wait_ge(self.aggregated, i + 1)
        self.core.nc.scalar.activation(self.std[:, self.tiles(i)], self.mv[:, self.tiles(i), 1], ACT.Sqrt,
                                       bias=self.core.eps[:]).then_inc(self.rooted, 1)

    def normalise(self, dve, ch, i):
        nc = self.core.nc
        dve.wait_ge(self.aggregated, i + 1)
        dve.wait_ge(self.rooted, i + 1)
        ch.step(nc.vector.reciprocal(self.rstd[:, self.tiles(i)], self.std[:, self.tiles(i)]))
        ch.wait()
        if i in self.groups and self.groups.index(self.groups[i]) != i:
            dve.wait_ge(self.turned, i)
        for n in range(TILES)[self.tiles(i)]:
            ins = nc.vector.tensor_scalar(self.xn(n), self.core.x[:, n, :], self.mv[:, n, 0:1], self.rstd[:, n:n + 1],
                                          ALU.subtract, ALU.mult)
        ins.then_inc(self.normed, 1)

    def turn(self, pe, i):
        pe.wait_ge(self.normed, i + 1)
        bank = self.side.take(pe, ("turn", i), self.ready, i + 1)
        for j, n in enumerate(range(TILES)[self.tiles(i)]):
            ins = self.core.nc.tensor.transpose(bank[:, j * P:(j + 1) * P], self.xn(n), self.core.ident[:])
        ins.then_inc(self.turned, 1)

    def copy(self, act, i):
        act.wait_ge(self.turned, i + 1)
        g = self.groups[i]
        self.core.nc.scalar.copy(self.xT[:, g * GT:(g + 1) * GT], self.side.of(("turn", i))).then_inc(self.ready, 1)


class Moe:

    PROB, TOKEN, FIRST, ROW = D, D + E_, D + E_ + 1, D + E_ + 2
    NOWHERE = float(16 * T)
    RING = 3

    def __init__(self, core):
        nc, d = core.nc, core.dram
        self.core = core
        self.w1 = core.sb("moe_w1", [D, E_, FF])
        self.w3 = core.sb("moe_w3", [D, E_, FF])
        self.w2 = core.sb("moe_w2", [FC, E_, FCH, D])
        self.gate = core.sb("moe_gate", [D, E_])
        self.iota = core.sb("moe_iota", [P, E_])
        self.token = core.sb("moe_token", [P, TPB])
        self.tri = core.sb("moe_tri", [P, 2, P], BF16)
        per_batch = lambda n, rows, cols: [nc.dram_tensor(f"moe_{n}{i}", (rows, cols), F32).ap() for i in range(2 * B)]
        self.slots, self.rows = per_batch("slots", SLOTS, self.ROW), per_batch("rows", TOPK * T, D)
        self.loads = [("moe_gate", self.gate[:], d["gate"]), ("moe_iota", self.iota[:], d["expert_iota"].to_broadcast([P, E_])),
                      ("moe_token", self.token[:], d["token"]),
                      ("moe_w1", self.w1[:], d["w1"]), ("moe_w3", self.w3[:], d["w3"]), ("moe_w2", self.w2[:], d["w2"])]
        for n, _, _ in self.loads:
            core.loaded[n] = core.sem(f"ld_{n}")
        self.cleared = core.sem("moe_cleared")

    def open(self, ctx, name, rows, xT, norm, side, main):
        core, nc = self.core, self.core.nc
        self.row_of, self.xT, self.norm, self.side = rows, xT, norm, side
        sb = lambda n, shape, dt=F32: core.sb(f"{name}_{n}", shape, dt, ctx)
        sem = lambda n: core.sem(f"{name}_{n}", ctx)
        NT = TPB
        self.e0, self.e1, self.pr = sb("e0", [P, NT, E_]), sb("e1", [P, NT, E_]), sb("pr", [P, NT, E_])
        self.mx, self.den, self.rden = sb("mx", [P, NT]), sb("den", [P, NT]), sb("rden", [P, NT])
        self.top, self.at, self.atf = sb("top", [P, NT, 8]), sb("at", [P, NT, 8], U32), sb("atf", [P, TOPK, NT])
        self.hot, self.tmp = sb("hot", [P, TOPK, NT, E_]), sb("tmp", [P, TOPK, NT, E_])
        self.picked = sb("picked", [P, NT, E_], BF16)
        self.mine, self.place, self.over = (sb(n, [P, TOPK, NT]) for n in ("mine", "place", "over"))
        self.scatter_at = sb("scatter_at", [P, B, TOPK, NT], U32)
        self.xs, self.xsT = sb("xs", [P, self.RING, 3, self.ROW]), sb("xsT", [D, 2, CAP])
        self.act_h, self.hid = sb("act_h", [FC, 2, CAP]), sb("hid", [FC, 2, FCH, CAP])
        self.y = sb("y", [P, 2, 3, D])
        self.second, self.dest, self.weight = sb("second", [P, 2, 3]), sb("dest", [P, 2, 3], U32), sb("weight", [P, 2, 3])
        self.back = sb("back", [P, TOPK, NT, D])
        self.ps_t, self.ps_h1, self.ps_h3, self.ps_y = main[:, 0, :], main[:, 1:3, :], main[:, 3:5, :], main[:, 5, :]
        (self.logits_done, self.shifted, self.exped, self.picked_done, self.counted, self.placed, self.routed) = (
            sem(n) for n in ("logits_done", "shifted", "exped", "picked_done", "counted", "placed", "routed"))
        self.tail_clear, self.chain = sem("tail_clear"), sem("chain")
        self.scattered = [sem(f"scattered{b}") for b in range(B)]
        self.slots_in = [sem(f"slots_in{i}") for i in range(self.RING)]
        self.y_out = [sem(f"y_out{i}") for i in range(2)]
        self.back_in = sem("back_in")
        (self.turned, self.t_read, self.h_done, self.silu_done, self.gated, self.y_done, self.y_read, self.sent, self.combined) = (
            sem(n) for n in ("turned", "t_read", "h_done", "silu_done", "gated", "y_done", "y_read", "sent", "combined"))

    UNITS = 2 * B * E_
    FULL = CAP // P
    REST = CAP - FULL * P
    CHUNKS = [(s * P, min(P, CAP - s * P)) for s in range(FULL + 1)]


    def logits(self, pe, r):
        nc, b = self.core.nc, r % B
        bank = self.side.take(pe, ("logits", r), self.shifted, r + 1)
        for j in range(TPB):
            n = b * TPB + j
            ins = nc.tensor.matmul(bank[:, j * E_:(j + 1) * E_], self.xT[:, n * P:(n + 1) * P], self.gate[:], start=True, stop=True)
        ins.then_inc(self.logits_done, 1)

    def counts(self, pe, r):
        pe.wait_ge(self.picked_done, r + 1)
        bank = self.side.take(pe, ("counts", r), self.placed, r + 1)
        for step in range(TPB):
            ins = self.core.nc.tensor.matmul(bank[:, step * E_:TPB * E_], self.tri[:, min(step, 1), :],
                                             self.picked[:, 0:TPB - step, :].rearrange("p j e -> p (j e)"),
                                             start=(step == 0), stop=(step == TPB - 1))
        ins.then_inc(self.counted, 1)

    def shift(self, dve, ch, r):
        nc = self.core.nc
        dve.wait_ge(self.logits_done, r + 1)
        logits = self.side.of(("logits", r))[:, 0:TPB * E_].rearrange("p (j e) -> p j e", e=E_)
        ch.step(nc.vector.reduce_max(self.mx[:], logits, AX_X))
        ch.wait()
        nc.vector.tensor_tensor(self.e0[:], logits, self.mx[:].unsqueeze(2).to_broadcast([P, TPB, E_]), ALU.subtract).then_inc(self.shifted, 1)

    def exp(self, act, r):
        act.wait_ge(self.shifted, r + 1)
        self.core.nc.scalar.activation(self.e1[:], self.e0[:], ACT.Exp).then_inc(self.exped, 1)

    def pick(self, dve, ch, r):
        nc, b = self.core.nc, r % B
        over_e = lambda v: v.unsqueeze(2).to_broadcast([P, TPB, E_])
        tiles = slice(b * TPB, (b + 1) * TPB)

        def then(ins):
            ch.step(ins)
            ch.wait()

        dve.wait_ge(self.exped, r + 1)
        then(nc.vector.reduce_sum(self.den[:], self.e1[:], AX_X))
        then(nc.vector.reciprocal(self.rden[:], self.den[:]))
        then(nc.vector.tensor_tensor(self.pr[:], self.e1[:], over_e(self.rden[:]), ALU.mult))
        for j in range(TPB):
            ch.step(nc.vector.max(self.top[:, j, :], self.pr[:, j, :]))
        ch.wait()
        for j in range(TPB):
            ch.step(nc.vector.max_index(self.at[:, j, :], self.top[:, j, :], self.pr[:, j, :]))
        ch.wait()
        then(nc.vector.tensor_copy(self.atf[:].rearrange("p k j -> p j k"), self.at[:, :, 0:TOPK]))
        for k in range(TOPK):
            ch.step(nc.vector.tensor_tensor(self.hot[:, k, :, :], self.iota[:].unsqueeze(1).to_broadcast([P, TPB, E_]),
                                            over_e(self.atf[:, k, :]), ALU.is_equal))
        ch.wait()
        nc.vector.tensor_tensor(self.picked[:], self.hot[:, 0, :, :], self.hot[:, 1, :, :], ALU.add).then_inc(self.picked_done, 1)
        ch.step(nc.vector.tensor_scalar(self.row_of[:, tiles, self.PROB:self.PROB + E_], self.pr[:], 0.5, None, ALU.mult))
        ch.step(nc.vector.tensor_copy(self.row_of[:, tiles, self.FIRST], self.atf[:, 0, :]))

    def put(self, dve, ch, r):
        nc, b = self.core.nc, r % B

        def then(ins):
            ch.step(ins)
            ch.wait()

        dve.wait_ge(self.counted, r + 1)
        seen = self.side.of(("counts", r))[:, 0:TPB * E_].rearrange("p (j e) -> p j e", e=E_)
        ch.step(nc.vector.tensor_tensor(self.tmp[:, 0, :, :], self.hot[:, 0, :, :], seen, ALU.mult))
        nc.vector.tensor_tensor(self.tmp[:, 1, :, :], self.hot[:, 1, :, :], seen, ALU.mult).then_inc(self.placed, 1)
        ch.wait()
        dve.wait_ge(self.placed, r + 1)
        then(nc.vector.reduce_sum(self.mine[:], self.tmp[:], AX_X))
        ch.step(nc.vector.scalar_tensor_tensor(self.place[:], self.atf[:], float(CAP), self.mine[:], ALU.mult, ALU.add))
        then(nc.vector.tensor_scalar(self.over[:], self.mine[:], float(CAP), float(4 * SLOTS), ALU.is_gt, ALU.mult))
        nc.vector.scalar_tensor_tensor(self.scatter_at[:, b, :, :], self.place[:], -1.0, self.over[:], ALU.add, ALU.add)\
          .then_inc(self.routed, 1)

    def scatter(self, pool, r, first=0, last=TOPK * TPB):
        nc, b = self.core.nc, r % B
        if first == 0:
            pool.wait_ge(self.routed, r + 1)
        for n in range(first, last):
            k, j = n // TPB, n % TPB
            nc.gpsimd.indirect_dma_start(self.slots[r], bass.IndirectOffsetOnAxis(self.scatter_at[:, b, k, j:j + 1], 0),
                                         self.row_of[:, b * TPB + j, :], None, bounds_check=SLOTS - 1, oob_is_err=False)\
              .then_inc(self.scattered[b], 16)


    def load(self, sp, u):
        r, e = u // E_, u % E_
        if e == 0:
            sp.wait_ge(self.scattered[r % B], 16 * TOPK * TPB * (r // B + 1))
        if u == 0:
            sp.wait_ge(self.tail_clear, 1)
        if u >= self.RING:
            sp.wait_ge(self.turned, u - self.RING + 1)
            sp.wait_ge(self.sent, u - self.RING + 1)
        src, r0 = self.slots[r], e * CAP
        sp.dma_start(self.xs[:, u % self.RING, 0:self.FULL, :], src[r0:r0 + self.FULL * P, :].rearrange("(s p) d -> p s d", p=P))\
          .then_inc(self.slots_in[u % self.RING], 16)
        sp.dma_start(self.xs[0:self.REST, u % self.RING, self.FULL, :], src[r0 + self.FULL * P:r0 + CAP, :])\
          .then_inc(self.slots_in[u % self.RING], 16)

    def loaded(self, eng, u):
        eng.wait_ge(self.slots_in[u % self.RING], 32 * (u // self.RING + 1))

    def turn(self, pe, u):
        self.loaded(pe, u)
        if u >= 1:
            pe.wait_ge(self.t_read, u)
        for s, (c0, n) in enumerate(self.CHUNKS):
            ins = self.core.nc.tensor.transpose(self.ps_t[:, c0:c0 + n], self.xs[0:n, u % self.RING, s, 0:D], self.core.ident[0:n, 0:n])
        ins.then_inc(self.turned, 1)

    def take(self, dve, u):
        nc = self.core.nc
        dve.wait_ge(self.turned, u + 1)
        if u >= 2:
            dve.wait_ge(self.h_done, 2 * FCH * (u - 1))
        nc.vector.tensor_copy(self.xsT[:, u % 2, :], self.ps_t[:, 0:CAP]).then_inc(self.t_read, 1)

    def address(self, dve, u):
        nc, e = self.core.nc, u % E_
        self.loaded(dve, u)
        if u >= 2:
            dve.wait_ge(self.y_out[u % 2], 48 * (u // 2))
        row = self.xs[:, u % self.RING, :, :]
        nc.vector.tensor_scalar(self.second[:, u % 2, :], row[:, :, self.FIRST], float(e), float(T), ALU.not_equal, ALU.mult).then_inc(self.chain, 1)
        nc.vector.tensor_copy(self.weight[:, u % 2, :], row[:, :, self.PROB + e]).then_inc(self.chain, 1)
        dve.wait_ge(self.chain, 2 * u + 2)
        nc.vector.tensor_tensor(self.dest[:, u % 2, :], self.second[:, u % 2, :], row[:, :, self.TOKEN], ALU.add).then_inc(self.sent, 1)

    def hidden(self, pe, u):
        e = u % E_
        pe.wait_ge(self.t_read, u + 1)
        for c in range(FCH):
            w = u * FCH + c
            for ps, wt in ((self.ps_h1, self.w1), (self.ps_h3, self.w3)):
                if w >= 2:
                    pe.wait_ge(self.gated, w - 1)
                self.core.nc.tensor.matmul(ps[0:FC, w % 2, 0:CAP], wt[:, e, c * FC:(c + 1) * FC], self.xsT[:, u % 2, :],
                                           start=True, stop=True).then_inc(self.h_done, 1)

    def silu(self, act, u):
        for w in range(u * FCH, (u + 1) * FCH):
            act.wait_ge(self.h_done, 2 * w + 1)
            if w >= 2:
                act.wait_ge(self.gated, w - 1)
            self.core.nc.scalar.activation(self.act_h[:, w % 2, :], self.ps_h1[0:FC, w % 2, 0:CAP], ACT.Silu).then_inc(self.silu_done, 1)

    def gating(self, dve, u):
        for c in range(FCH):
            w = u * FCH + c
            dve.wait_ge(self.silu_done, w + 1)
            dve.wait_ge(self.h_done, 2 * (w + 1))
            if u >= 2 and c == 0:
                dve.wait_ge(self.y_done, u - 1)
            self.core.nc.vector.tensor_tensor(self.hid[:, u % 2, c, :], self.act_h[:, w % 2, :], self.ps_h3[0:FC, w % 2, 0:CAP], ALU.mult)\
                .then_inc(self.gated, 1)

    def results(self, pe, u):
        pe.wait_ge(self.gated, FCH * (u + 1))
        if u >= 1:
            pe.wait_ge(self.y_read, 3 * u)
        for s, (c0, n) in enumerate(self.CHUNKS):
            for c in range(FCH):
                ins = self.core.nc.tensor.matmul(self.ps_y[0:n, s * D:(s + 1) * D], self.hid[:, u % 2, c, c0:c0 + n], self.w2[:, u % E_, c, :],
                                                 start=(c == 0), stop=(c == FCH - 1))
        ins.then_inc(self.y_done, 1)

    def weigh(self, act, u):
        act.wait_ge(self.y_done, u + 1)
        act.wait_ge(self.sent, u + 1)
        for s, (c0, n) in enumerate(self.CHUNKS):
            self.core.nc.scalar.activation(self.y[0:n, u % 2, s, :], self.ps_y[0:n, s * D:(s + 1) * D], ACT.Copy,
                                           scale=self.weight[0:n, u % 2, s:s + 1]).then_inc(self.y_read, 1)

    def send(self, pool, u):
        pool.wait_ge(self.y_read, 3 * (u + 1))
        pool.wait_ge(self.sent, u + 1)
        for s, (c0, n) in enumerate(self.CHUNKS):
            self.core.nc.gpsimd.indirect_dma_start(self.rows[u // E_], bass.IndirectOffsetOnAxis(self.dest[0:n, u % 2, s:s + 1], 0),
                                                   self.y[0:n, u % 2, s, :], None, bounds_check=TOPK * T - 1, oob_is_err=False)\
                .then_inc(self.y_out[u % 2], 16)

    def fetch(self, sp, r):
        for i in range(2):
            sp.wait_ge(self.y_out[i], 48 * E_ // 2 * (r + 1))
        if r >= 1:
            sp.wait_ge(self.combined, r)
        sp.dma_start(self.back[:], self.rows[r].rearrange("(k j p) d -> p k j d", k=TOPK, p=P)).then_inc(self.back_in, 16)

    def combine(self, dve, ch, r):
        nc, tiles = self.core.nc, slice(r % B * TPB, (r % B + 1) * TPB)
        dve.wait_ge(self.back_in, 16 * (r + 1))
        x = self.core.x[:, tiles, :]
        ch.step(nc.vector.tensor_tensor(x, x, self.back[:, 0, :, :], ALU.add))
        ch.wait()
        nc.vector.tensor_tensor(x, x, self.back[:, 1, :, :], ALU.add).then_inc(self.combined, 1)
        dve.wait_ge(self.combined, r + 1)


class Mamba:

    UNITS = [(di, b) for b in range(B) for di in range(2)]
    NC = TPB
    N = len(UNITS) * NC
    PIECES = 6
    LOG_TERMS = 8
    PARTS_OUT = [range(0, 3), range(3, 6), range(6, 8)]
    TAPS_AT = [range(0, 2), range(2, 5), range(5, 8), range(8, 11), range(11, 14), range(14, 16), (), ()]

    def __init__(self, core):
        d = core.dram
        self.core = core
        sb = core.sb
        self.w_xbc, self.w_z, self.w_dt = sb("mb_w_xbc", [D, 2, 4, P]), sb("mb_w_z", [D, 2, 2, P]), sb("mb_w_dt", [D, 2 * NH])
        self.taps, self.conv_b = sb("mb_taps", [P, 2, 4, TAPS]), sb("mb_conv_b", [P, 2, 4])
        self.skip, self.norm_w, self.wo = sb("mb_skip", [P, 2, 2]), sb("mb_norm_w", [P, 2, 2]), sb("mb_wo", [P, 2, 2, D])
        self.dt_bias, self.a_log = sb("mb_dt_bias", [P, 2 * NH]), sb("mb_a_log", [P, 2 * NH])
        self.loads = [("mb_w_xbc", self.w_xbc[:], d["mb_w_xbc"]), ("mb_w_z", self.w_z[:], d["mb_w_z"]), ("mb_w_dt", self.w_dt[:], d["mb_w_dt"]),
                      ("mb_taps", self.taps[:], d["mb_taps"]), ("mb_conv_b", self.conv_b[:], d["mb_conv_b"]),
                      ("mb_skip", self.skip[:], d["mb_skip"]), ("mb_norm_w", self.norm_w[:], d["mb_norm_w"]), ("mb_wo", self.wo[:], d["mb_wo"]),
                      ("mb_dt_bias", self.dt_bias[:], d["mb_dt_bias"].to_broadcast([P, 2 * NH])),
                      ("mb_a_log", self.a_log[:], d["mb_a_log"].to_broadcast([P, 2 * NH]))]
        for n, _, _ in self.loads:
            core.loaded[n] = core.sem(f"ld_{n}")

    def open(self, ctx, name, xT, side, main):
        core = self.core
        self.xT, self.side = xT, side
        sb = lambda n, shape, dt=F32: core.sb(f"{name}_{n}", shape, dt, ctx)
        sem = lambda n: core.sem(f"{name}_{n}", ctx)
        XP = T + 2 * (TAPS - 1)
        self.padded = sb("padded", [P, 2, XP])
        self.act_t = sb("act", [P, 2, 4, T])
        self.z = sb("z", [P, 2, 2, T])
        self.strict, self.incl, self.ones = sb("strict", [P, 2, P]), sb("incl", [P, 2, P]), sb("ones", [P, P])
        small = lambda n: sb(n, [P, TILES, 2 * NH])
        self.dt, self.a, self.whole = small("dt"), small("a"), small("whole")
        self.v, self.ab, self.ex, self.sq, self.poly = (sb(n, [P, TPB, 2 * NH]) for n in ("v", "ab", "ex", "sq", "poly"))
        self.a_exp, self.to_end = sb("a_exp", [P, 2 * NH]), sb("to_end", [P, 2, TILES, NH])
        self.cut, self.e_seg, self.mt = (sb(n, [P, 2, NH, P]) for n in ("cut", "e_seg", "mt"))
        self.e_cum, self.gm, self.bs = sb("e_cum", [P, 2, 2, P]), sb("gm", [P, 2, P]), sb("bs", [P, 2, P])
        self.xdt, self.xw, self.h, self.h_dec = sb("xdt", [P, 2, DIN]), sb("xw", [P, 2, DIN]), sb("h", [P, 2, DIN]), sb("h_dec", [P, DIN])
        self.y_in, self.y_old, self.y2 = sb("y_in", [P, 2, 2, P]), sb("y_old", [P, 2, 2, P]), sb("y2", [P, 2, 2, P])
        self.var, self.std, self.rstd = (sb(n, [P, self.NC]) for n in ("var", "std", "rstd"))
        self.ps_seg, self.ps_cb, self.ps_x, self.ps_y, self.ps_st, self.ps_o = (main[:, i, :] for i in range(6))
        (self.masks, self.pads, self.dt_done, self.dt_in, self.dt_exp, self.a_exped, self.a_done, self.sums_done, self.decays, self.norm_done) = (
            sem(n) for n in ("masks", "pads", "dt_done", "dt_in", "dt_exp", "a_exped", "a_done", "sums_done", "decays", "norm_done"))
        self.proj_done, self.proj_read, self.conv_done, self.act_ready = (sem(n) for n in ("proj_done", "proj_read", "conv_done", "act_ready"))
        (self.cut_done, self.seg_done, self.cb_done, self.xg_done, self.y_done, self.st_done, self.seg_exp, self.cb_read, self.x_read) = (
            sem(n) for n in ("cut_done", "seg_done", "cb_done", "xg_done", "y_done", "st_done", "seg_exp", "cb_read", "x_read"))
        (self.gm_done, self.mt_done, self.xw_done, self.h_decayed, self.h_ready, self.y_read, self.y_sum, self.gate_done) = (
            sem(n) for n in ("gm_done", "mt_done", "xw_done", "h_decayed", "h_ready", "y_read", "y_sum", "gate_done"))
        (self.squared, self.ss_done, self.ss_read, self.std_done, self.rms_done, self.out_done, self.out_read) = (
            sem(n) for n in ("squared", "ss_done", "ss_read", "std_done", "rms_done", "out_done", "out_read"))

    def at(self, g):
        u, i = g // self.NC, g % self.NC
        di, b = self.UNITS[u]
        j = i if di == 0 else self.NC - 1 - i
        return u, di, b, i, b * TPB + j, slice(j * P, (j + 1) * P)

    def carried(self, g):
        return (g // self.NC) * (self.NC - 1) + g % self.NC

    def passes_on(self, g):
        return g % self.NC < self.NC - 1


    def make_masks(self, pool):
        nc = self.core.nc
        for m in (self.ones, self.strict, self.incl):
            nc.gpsimd.memset(m[:], 1.0).then_inc(self.masks, 1)
        nc.gpsimd.memset(self.padded[:], 0.0).then_inc(self.pads, 1)
        pool.wait_ge(self.masks, 3)
        for m, di, op, sign in ((self.strict, 0, ALU.is_gt, 1), (self.strict, 1, ALU.is_gt, -1), (self.incl, 0, ALU.is_ge, -1), (self.incl, 1, ALU.is_ge, 1)):
            nc.gpsimd.affine_select(out=m[:, di, :], in_=m[:, di, :], compare_op=op, fill=0.0, base=0,
                                    pattern=[[-sign, P]], channel_multiplier=sign).then_inc(self.masks, 1)
        pool.wait_ge(self.masks, 7)

    def steps(self, pe, b):
        bank = self.side.take(pe, ("dt", b), self.dt_in, b + 1)
        for j in range(TPB):
            n = b * TPB + j
            ins = self.core.nc.tensor.matmul(bank[:, j * 2 * NH:(j + 1) * 2 * NH], self.xT[:, n * P:(n + 1) * P], self.w_dt[:], start=True, stop=True)
        ins.then_inc(self.dt_done, 1)

    def sums(self, pe, b):
        nc, tiles = self.core.nc, slice(b * TPB, (b + 1) * TPB)
        pe.wait_ge(self.a_done, b + 1)
        pe.wait_ge(self.masks, 7)
        bank = self.side.take(pe, ("sums", b), self.decays, 3 * (b + 1))
        n = TPB * NH
        for di in range(2):
            nc.tensor.matmul(bank[:, di * n:(di + 1) * n], self.strict[:, di, :], self.a[:, tiles, di * NH:(di + 1) * NH], start=True, stop=True)
        nc.tensor.matmul(bank[:, 2 * n:4 * n], self.ones[:], self.a[:, tiles, :], start=True, stop=True).then_inc(self.sums_done, 1)

    def exp_a(self, act):
        self.core.landed(act, "mb_a_log", "mb_conv_b")
        self.core.nc.scalar.activation(self.a_exp[:], self.a_log[:], ACT.Exp).then_inc(self.a_exped, 1)

    def exp_dt(self, act, b):
        act.wait_ge(self.dt_in, b + 1)
        self.core.nc.scalar.activation(self.ex[:], self.ab[:], ACT.Exp, scale=-1.0).then_inc(self.dt_exp, 1)

    def exp_sums(self, act, b):
        nc, tiles, n = self.core.nc, slice(b * TPB, (b + 1) * TPB), TPB * NH
        act.wait_ge(self.sums_done, b + 1)
        bank = self.side.of(("sums", b))
        for di in range(2):
            nc.scalar.activation(self.to_end[:, di, tiles, :], bank[:, di * n:(di + 1) * n].rearrange("p (j h) -> p j h", h=NH), ACT.Exp)\
              .then_inc(self.decays, 1)
        nc.scalar.activation(self.whole[:, tiles, :], bank[:, 2 * n:4 * n].rearrange("p (j h) -> p j h", h=2 * NH), ACT.Exp).then_inc(self.decays, 1)

    def weigh_out(self, dve):
        self.core.landed(dve, "mb_norm_w", "mb_wo", "mb_dt_bias", "mb_taps", "mb_skip")
        for di in range(2):
            for c in range(2):
                ins = self.core.nc.vector.tensor_scalar(self.wo[:, di, c, :], self.wo[:, di, c, :], self.norm_w[:, di, c:c + 1], None, ALU.mult)
        ins.then_inc(self.norm_done, 1)

    def step_sizes(self, dve, ch, b):
        nc, tiles, every = self.core.nc, slice(b * TPB, (b + 1) * TPB), [P, TPB, 2 * NH]
        v, ab, ex, sq, poly = self.v, self.ab, self.ex, self.sq, self.poly

        def then(ins):
            ch.step(ins)
            ch.wait()

        dve.wait_ge(self.dt_done, b + 1)
        then(nc.vector.tensor_tensor(v[:], self.side.of(("dt", b))[:, 0:TPB * 2 * NH].rearrange("p (j h) -> p j h", h=2 * NH),
                                     self.dt_bias[:].unsqueeze(1).to_broadcast(every), ALU.add))
        nc.vector.scalar_tensor_tensor(ab[:], v[:], -1.0, v[:], ALU.mult, ALU.max).then_inc(self.dt_in, 1)
        dve.wait_ge(self.dt_exp, b + 1)
        then(nc.vector.tensor_scalar(poly[:], ex[:], 2.0, None, ALU.add))
        then(nc.vector.reciprocal(poly[:], poly[:]))
        then(nc.vector.tensor_tensor(ex[:], ex[:], poly[:], ALU.mult))
        then(nc.vector.tensor_tensor(sq[:], ex[:], ex[:], ALU.mult))
        then(nc.vector.tensor_scalar(poly[:], sq[:], 1.0 / (2 * self.LOG_TERMS + 1), None, ALU.mult))
        for k in range(self.LOG_TERMS - 1, 0, -1):
            then(nc.vector.scalar_tensor_tensor(poly[:], poly[:], 1.0 / (2 * k + 1), sq[:], ALU.add, ALU.mult))
        then(nc.vector.scalar_tensor_tensor(poly[:], poly[:], 1.0, ex[:], ALU.add, ALU.mult))
        then(nc.vector.tensor_scalar(v[:], v[:], 0.0, None, ALU.max))
        then(nc.vector.scalar_tensor_tensor(self.dt[:, tiles, :], poly[:], 2.0, v[:], ALU.mult, ALU.add))
        dve.wait_ge(self.a_exped, 1)
        nc.vector.scalar_tensor_tensor(self.a[:, tiles, :], self.dt[:, tiles, :], -1.0, self.a_exp[:].unsqueeze(1).to_broadcast(every), ALU.mult, ALU.mult)\
          .then_inc(self.a_done, 1)


    def project(self, pe, u, c):
        di, b = self.UNITS[u]
        weight = self.w_xbc[:, di, c, :] if c < 4 else self.w_z[:, di, c - 4, :]
        for half in range(2):
            w = (u * self.PIECES + c) * 2 + half
            bank = self.side.take(pe, ("proj", w), self.proj_read, w + 1)
            t0 = b * T + half * BANK
            self.core.nc.tensor.matmul(bank[:], weight, self.xT[:, t0:t0 + BANK], start=True, stop=True).then_inc(self.proj_done, 1)

    def take(self, act, u, c):
        if c < 4:
            if u >= 1 or c >= 2:
                act.wait_ge(self.conv_done, 4 * u + c - 1)
        elif u >= 2:
            act.wait_ge(self.out_done, len(self.PARTS_OUT) * (u - 1))
        for half in range(2):
            w = (u * self.PIECES + c) * 2 + half
            act.wait_ge(self.proj_done, w + 1)
            t0 = half * BANK
            dst = self.padded[:, c % 2, TAPS - 1 + t0:TAPS - 1 + t0 + BANK] if c < 4 else self.z[:, u % 2, c - 4, t0:t0 + BANK]
            self.core.nc.scalar.copy(dst, self.side.of(("proj", w))).then_inc(self.proj_read, 1)

    def convolve(self, dve, ch, u, n):
        nc, (di, b), c, k = self.core.nc, self.UNITS[u], n // TAPS, n % TAPS
        out = self.act_t[:, u % 2, c, :]
        t0 = k if di == 0 else 2 * (TAPS - 1) - k
        src, tap = self.padded[:, c % 2, t0:t0 + T], self.taps[:, di, c, k:k + 1]
        if k == 0:
            dve.wait_ge(self.proj_read, (u * self.PIECES + c) * 2 + 2)
            ch.step(nc.vector.tensor_scalar(out, src, tap, None, ALU.mult))
            return
        ch.wait()
        ins = nc.vector.scalar_tensor_tensor(out, src, tap, out, ALU.mult, ALU.add)
        ch.step(ins) if k < TAPS - 1 else ins.then_inc(self.conv_done, 1)

    def silus(self, act, u):
        di, b = self.UNITS[u]
        for c in range(4):
            act.wait_ge(self.conv_done, 4 * u + c + 1)
            self.core.nc.scalar.activation(self.act_t[:, u % 2, c, :], self.act_t[:, u % 2, c, :], ACT.Silu, bias=self.conv_b[:, di, c:c + 1])\
                .then_inc(self.act_ready, 1)
        act.wait_ge(self.proj_read, (u + 1) * self.PIECES * 2)
        for c in range(2):
            self.core.nc.scalar.activation(self.z[:, u % 2, c, :], self.z[:, u % 2, c, :], ACT.Silu).then_inc(self.act_ready, 1)


    def cut_a(self, pool, g):
        u, di, b, i, n, cols = self.at(g)
        pool.wait_ge(self.a_done, b + 1)
        if g >= 2:
            pool.wait_ge(self.seg_done, g - 1)
        self.core.nc.gpsimd.tensor_tensor(self.cut[:, g % 2, :, :], self.strict[:, di, :].unsqueeze(1).to_broadcast([P, NH, P]),
                                          self.a[:, n, di * NH:(di + 1) * NH].unsqueeze(2).to_broadcast([P, NH, P]), ALU.mult)\
            .then_inc(self.cut_done, 1)

    def before(self, pe, g):
        nc = self.core.nc
        u, di, b, i, n, cols = self.at(g)
        act = self.act_t[:, u % 2, :, :]
        pe.wait_ge(self.cut_done, g + 1)
        if g >= 1:
            pe.wait_ge(self.seg_exp, g)
        for hh in range(NH):
            ins = nc.tensor.matmul(self.ps_seg[:, hh * P:(hh + 1) * P], self.cut[:, g % 2, hh, :], self.incl[:, di, :], start=True, stop=True)
        ins.then_inc(self.seg_done, 1)
        pe.wait_ge(self.act_ready, self.PIECES * (u + 1))
        if g >= 1:
            pe.wait_ge(self.cb_read, g)
        if i:
            for hh in range(NH):
                nc.tensor.matmul(self.ps_cb[HP * (hh % 2):HP * (hh % 2) + HP, hh // 2 * P:hh // 2 * P + P],
                                 self.a[:, n, di * NH + hh:di * NH + hh + 1].to_broadcast([P, HP]), self.incl[:, di, :], start=True, stop=True)
        nc.tensor.transpose(self.ps_cb[:, 2 * P:3 * P], act[:, 2, cols], self.core.ident[:]).then_inc(self.cb_done, 1)
        if g >= 1:
            pe.wait_ge(self.x_read, g)
            pe.wait_ge(self.gm_done, g)
        for c in range(2):
            nc.tensor.transpose(self.ps_x[:, c * P:(c + 1) * P], act[:, c, cols], self.core.ident[:])
        nc.tensor.matmul(self.ps_x[:, 2 * P:3 * P], act[:, 2, cols], act[:, 3, cols], start=True, stop=True).then_inc(self.xg_done, 1)

    def exps(self, act, g):
        nc = self.core.nc
        i = g % self.NC
        act.wait_ge(self.seg_done, g + 1)
        if g >= 2:
            act.wait_ge(self.mt_done, g - 1)
        nc.scalar.activation(self.e_seg[:, g % 2, :, :], self.ps_seg.rearrange("p (h t) -> p h t", h=NH), ACT.Exp).then_inc(self.seg_exp, 1)
        act.wait_ge(self.cb_done, g + 1)
        if g >= 2:
            act.wait_ge(self.y_read, g - 1)
            act.wait_ge(self.st_done, min(self.carried(g - 2) + 1, self.carried(g - 1)))
        if i:
            nc.scalar.activation(self.e_cum[:, g % 2, :, :], self.ps_cb[:, 0:2 * P].rearrange("p (c t) -> p c t", c=2), ACT.Exp)
        nc.scalar.copy(self.bs[:, g % 2, :], self.ps_cb[:, 2 * P:3 * P]).then_inc(self.cb_read, 1)

    def by_head(self, ap):
        return ap.rearrange("p (h c) -> p h c", h=NH)

    def heads(self, ap):
        return ap.unsqueeze(2).to_broadcast([P, NH, HP])

    def front(self, dve, g):
        nc = self.core.nc
        u, di, b, i, n, cols = self.at(g)
        dve.wait_ge(self.xg_done, g + 1)
        if g >= 2:
            dve.wait_ge(self.y_done, g - 1)
            if self.passes_on(g - 2):
                dve.wait_ge(self.xw_done, self.carried(g - 2) + 1)
        nc.vector.tensor_tensor(self.by_head(self.xdt[:, g % 2, :]), self.by_head(self.ps_x[:, 0:DIN]), self.heads(self.dt[:, n, di * NH:(di + 1) * NH]), ALU.mult)\
          .then_inc(self.x_read, 1)
        if g >= 2:
            dve.wait_ge(self.mt_done, g - 1)
        nc.vector.tensor_tensor(self.gm[:, g % 2, :], self.ps_x[:, 2 * P:3 * P], self.incl[:, di, :], ALU.mult).then_inc(self.gm_done, 1)
        dve.wait_ge(self.seg_exp, g + 1)
        dve.wait_ge(self.gm_done, g + 1)
        nc.vector.tensor_tensor(self.mt[:, g % 2, :, :], self.e_seg[:, g % 2, :, :], self.gm[:, g % 2, :].unsqueeze(1).to_broadcast([P, NH, P]),
                                ALU.mult).then_inc(self.mt_done, 1)

    def to_state(self, pool, g):
        u, di, b, i, n, cols = self.at(g)
        if not self.passes_on(g):
            return
        pool.wait_ge(self.x_read, g + 1)
        pool.wait_ge(self.decays, 3 * (b + 1))
        if self.carried(g) >= 2:
            pool.wait_ge(self.st_done, self.carried(g) - 1)
        self.core.nc.gpsimd.tensor_tensor(self.by_head(self.xw[:, g % 2, :]), self.by_head(self.xdt[:, g % 2, :]), self.heads(self.to_end[:, di, n, :]), ALU.mult)\
            .then_inc(self.xw_done, 1)

    def state(self, pe, g):
        if not self.passes_on(g):
            return
        n = self.carried(g)
        pe.wait_ge(self.cb_read, g + 1)
        pe.wait_ge(self.xw_done, n + 1)
        if n >= 1:
            pe.wait_ge(self.h_ready, n)
        self.core.nc.tensor.matmul(self.ps_st[:, 0:DIN], self.bs[:, g % 2, :], self.xw[:, g % 2, :], start=True, stop=True).then_inc(self.st_done, 1)

    def decay(self, pool, g):
        u, di, b, i, n, cols = self.at(g)
        if i == 0 or not self.passes_on(g):
            return
        pool.wait_ge(self.h_ready, self.carried(g))
        self.core.nc.gpsimd.tensor_tensor(self.by_head(self.h_dec[:]), self.by_head(self.h[:, (g - 1) % 2, :]),
                                          self.heads(self.whole[:, n, di * NH:(di + 1) * NH]), ALU.mult).then_inc(self.h_decayed, 1)

    def pass_state(self, dve, g):
        u, di, b, i, n, cols = self.at(g)
        if not self.passes_on(g):
            return
        if g >= 1:
            dve.wait_ge(self.y_done, g)
        dve.wait_ge(self.st_done, self.carried(g) + 1)
        if i == 0:
            self.core.nc.vector.tensor_copy(self.h[:, g % 2, :], self.ps_st[:, 0:DIN]).then_inc(self.h_ready, 1)
            return
        dve.wait_ge(self.h_decayed, u * (self.NC - 2) + i)
        self.core.nc.vector.tensor_tensor(self.h[:, g % 2, :], self.h_dec[:], self.ps_st[:, 0:DIN], ALU.add).then_inc(self.h_ready, 1)

    def outputs(self, pe, g):
        nc = self.core.nc
        u, di, b, i, n, cols = self.at(g)
        if g >= 1:
            pe.wait_ge(self.y_read, g)
        if i:
            pe.wait_ge(self.h_ready, self.carried(g))
            for c in range(2):
                nc.tensor.matmul(self.ps_y[:, (2 + c) * P:(3 + c) * P], self.h[:, (g - 1) % 2, c * P:(c + 1) * P], self.act_t[:, u % 2, 3, cols],
                                 start=True, stop=True)
        pe.wait_ge(self.mt_done, g + 1)
        pe.wait_ge(self.x_read, g + 1)
        for hh in range(NH):
            out = self.ps_y[HP * (hh % 2):HP * (hh % 2) + HP, hh // 2 * P:hh // 2 * P + P]
            ins = nc.tensor.matmul(out, self.xdt[:, g % 2, hh * HP:(hh + 1) * HP], self.mt[:, g % 2, hh, :], start=True, stop=True)
        ins.then_inc(self.y_done, 1)

    def back(self, dve, g):
        nc = self.core.nc
        u, di, b, i, n, cols = self.at(g)
        dve.wait_ge(self.y_done, g + 1)
        if g >= 2:
            dve.wait_ge(self.gate_done, g - 1)
        if i:
            dve.wait_ge(self.cb_read, g + 1)
            nc.vector.tensor_tensor(self.y_old[:, g % 2, :, :], self.e_cum[:, g % 2, :, :], self.ps_y[:, 2 * P:4 * P].rearrange("p (c t) -> p c t", c=2), ALU.mult)
        for c in range(2):
            ins = nc.vector.scalar_tensor_tensor(self.y_in[:, g % 2, c, :], self.act_t[:, u % 2, c, cols], self.skip[:, di, c:c + 1], self.ps_y[:, c * P:(c + 1) * P],
                                                 ALU.mult, ALU.add)
        ins.then_inc(self.y_read, 1)

    def gate(self, pool, g):
        nc = self.core.nc
        u, di, b, i, n, cols = self.at(g)
        pool.wait_ge(self.y_read, g + 1)
        pool.wait_ge(self.act_ready, self.PIECES * (u + 1))
        if i:
            nc.gpsimd.tensor_tensor(self.y_in[:, g % 2, :, :], self.y_in[:, g % 2, :, :], self.y_old[:, g % 2, :, :], ALU.add).then_inc(self.y_sum, 1)
            pool.wait_ge(self.y_sum, self.carried(g))
        nc.gpsimd.tensor_tensor(self.z[:, u % 2, :, cols], self.y_in[:, g % 2, :, :], self.z[:, u % 2, :, cols], ALU.mult).then_inc(self.gate_done, 1)


    def square(self, act, g):
        u, di, b, i, n, cols = self.at(g)
        act.wait_ge(self.gate_done, g + 1)
        if g >= 2:
            act.wait_ge(self.ss_done, g - 1)
        self.core.nc.scalar.activation(self.y2[:, g % 2, :, :], self.z[:, u % 2, :, cols], ACT.Square).then_inc(self.squared, 1)

    def squares(self, pe, g, parts):
        u, di, b, i, n, cols = self.at(g)
        pe.wait_ge(self.squared, g + 1)
        if parts:
            pe.wait_ge(self.out_read, parts)
        if i == 0 and u >= 1:
            pe.wait_ge(self.ss_read, u)
        col = 3 * D + n % TPB
        for c in range(2):
            ins = self.core.nc.tensor.matmul(self.ps_o[:, col:col + 1], self.y2[:, g % 2, c, :], self.ones[:, 0:1], start=(c == 0), stop=(c == 1))
        ins.then_inc(self.ss_done, 1)

    def variance(self, dve, u):
        dve.wait_ge(self.ss_done, self.NC * (u + 1))
        if u >= 1:
            dve.wait_ge(self.std_done, u)
        self.core.nc.vector.tensor_scalar(self.var[:], self.ps_o[:, 3 * D:3 * D + self.NC], 1.0 / DIN, None, ALU.mult).then_inc(self.ss_read, 1)

    def deviation(self, act, u):
        act.wait_ge(self.ss_read, u + 1)
        if u >= 1:
            act.wait_ge(self.rms_done, u)
        self.core.nc.scalar.activation(self.std[:], self.var[:], ACT.Sqrt, bias=self.core.eps[:]).then_inc(self.std_done, 1)

    def output(self, pe, u, part):
        parts = len(self.PARTS_OUT)
        pe.wait_ge(self.gate_done, self.NC * (u + 1))
        pe.wait_ge(self.ss_read, u + 1)
        if u or part:
            pe.wait_ge(self.out_read, parts * u + part)
        for q, j in enumerate(self.PARTS_OUT[part]):
            for c in range(2):
                ins = self.core.nc.tensor.matmul(self.ps_o[:, q * D:(q + 1) * D], self.z[:, u % 2, c, j * P:(j + 1) * P],
                                                 self.wo[:, self.UNITS[u][0], c, :], start=(c == 0), stop=(c == 1))
        ins.then_inc(self.out_done, 1)

    def add(self, dve, ch, u, part):
        nc, core, (di, b) = self.core.nc, self.core, self.UNITS[u]
        if part == 0:
            dve.wait_ge(self.std_done, u + 1)
            nc.vector.reciprocal(self.rstd[:], self.std[:]).then_inc(self.rms_done, 1)
            dve.wait_ge(self.rms_done, u + 1)
            ch.step(nc.vector.tensor_scalar(self.rstd[:], self.rstd[:], 0.5, None, ALU.mult))
            ch.wait()
        dve.wait_ge(self.out_done, len(self.PARTS_OUT) * u + part + 1)
        for q, j in enumerate(self.PARTS_OUT[part]):
            n = b * TPB + j
            ins = nc.vector.scalar_tensor_tensor(core.x[:, n, :], self.ps_o[:, q * D:(q + 1) * D], self.rstd[:, j:j + 1], core.x[:, n, :], ALU.mult, ALU.add)
        ins.then_inc(self.out_read, 1)
        if part == len(self.PARTS_OUT) - 1:
            dve.wait_ge(self.out_read, len(self.PARTS_OUT) * (u + 1))


def moe_mamba_moe(core):
    nc, moe, mamba = core.nc, core.moe, core.mamba
    NC, N, UNITS = mamba.NC, mamba.N, len(mamba.UNITS)
    HALF = B * E_
    with ExitStack() as ctx:
        rows = core.sb("rows", [P, TILES, moe.ROW], ctx=ctx)
        xT = core.sb("xT", [D, B * T], ctx=ctx)
        side = SideBanks(ctx.enter_context(nc.psum_tensor("ps_side", [P, 2, BANK], F32)))
        main = ctx.enter_context(nc.psum_tensor("ps_main", [P, 6, BANK], F32))
        norm = Norm(core, "norm", ctx, lambda n: rows[:, n, 0:D], xT, side, [0, 1, 2, 3] * 3)
        moe.open(ctx, "moe", rows, xT, norm, side, main)
        mamba.open(ctx, "mb", xT, side, main)
        chain, numbered = core.sem("dve_chain", ctx), core.sem("numbered", ctx)
        PARTS_OUT = len(mamba.PARTS_OUT)

        with nc.Block() as block:
            @block.tensor
            def _(pe):
                def experts(u, last):
                    if u + 1 < last:
                        moe.turn(pe, u + 1)
                    moe.hidden(pe, u)
                    if u > last - HALF:
                        moe.results(pe, u - 1)

                core.landed(pe, "moe_gate", "ident")
                for r in range(B):
                    for half in range(2):
                        norm.turn(pe, 2 * r + half)
                    pe.wait_ge(norm.ready, 2 * r + 2)
                    moe.logits(pe, r)
                    moe.counts(pe, r)
                core.landed(pe, "moe_w1", "moe_w3", "moe_w2", "mb_w_dt", "mb_w_xbc", "mb_w_z")
                moe.turn(pe, 0)
                for u in range(HALF):
                    experts(u, HALF)
                    if u == 11:
                        norm.turn(pe, 4)
                        norm.turn(pe, 5)
                    if u == 12:
                        pe.wait_ge(norm.ready, 6)
                        mamba.steps(pe, 0)
                    if u == 14:
                        mamba.sums(pe, 0)
                    if u >= 12:
                        mamba.project(pe, 0, u - 12)
                moe.results(pe, HALF - 1)
                for c in (4, 5):
                    mamba.project(pe, 0, c)
                pe.wait_ge(moe.y_read, 3 * HALF)
                pe.wait_ge(mamba.norm_done, 1)
                mamba.before(pe, 0)
                for g in range(N):
                    u, i = g // NC, g % NC
                    if g + 1 < N and i < NC - 1:
                        mamba.before(pe, g + 1)
                    mamba.state(pe, g)
                    mamba.outputs(pe, g)
                    if g >= 1:
                        mamba.squares(pe, g - 1, 0 if u == 0 else PARTS_OUT * (u - 1) + min(max(i - 2, 0), PARTS_OUT))
                    if u >= 1 and i in (2, 3, 4):
                        mamba.output(pe, u - 1, i - 2)
                    if u + 1 < UNITS and i < mamba.PIECES:
                        if u == 1 and i == 0:
                            pe.wait_ge(norm.ready, 8)
                        mamba.project(pe, u + 1, i)
                    if u == 0 and i == 7:
                        norm.turn(pe, 6)
                        norm.turn(pe, 7)
                    if u == 1 and i == 1:
                        mamba.steps(pe, 1)
                    if u == 1 and i == 4:
                        mamba.sums(pe, 1)
                    if u == 2 and i == 7:
                        norm.turn(pe, 8)
                        norm.turn(pe, 9)
                    if u == 3 and i == 0:
                        pe.wait_ge(norm.ready, 10)
                        moe.logits(pe, 2)
                    if u == 3 and i == 2:
                        moe.counts(pe, 2)
                    if g + 1 < N and i == NC - 1:
                        mamba.before(pe, g + 1)
                pe.wait_ge(mamba.seg_exp, N)
                pe.wait_ge(mamba.cb_read, N)
                pe.wait_ge(mamba.x_read, N)
                pe.wait_ge(mamba.gm_done, N)
                pe.wait_ge(mamba.y_read, N)
                pe.wait_ge(mamba.h_ready, UNITS * (NC - 1))
                moe.turn(pe, HALF)
                for u in range(HALF, 2 * HALF):
                    if u == HALF + 1:
                        pe.wait_ge(mamba.out_read, PARTS_OUT * UNITS)
                    experts(u, 2 * HALF)
                    if u == HALF:
                        mamba.squares(pe, N - 1, PARTS_OUT * (UNITS - 1))
                        for part in range(PARTS_OUT):
                            mamba.output(pe, UNITS - 1, part)
                    if u == HALF + 1:
                        norm.turn(pe, 10)
                        norm.turn(pe, 11)
                    if u == HALF + 2:
                        pe.wait_ge(norm.ready, 12)
                        moe.logits(pe, 3)
                    if u == HALF + 3:
                        moe.counts(pe, 3)
                moe.results(pe, 2 * HALF - 1)

            @block.sync
            def _(sp):
                for u in range(2 * HALF):
                    moe.load(sp, u)
                    if u in (E_ + 4, HALF + E_ + 4):
                        moe.fetch(sp, u // E_ - 1)
                    if u == HALF - 1:
                        moe.fetch(sp, 1)
                sp.wait_ge(moe.combined, 3)
                sp.dma_start(core.stored_rows(0), core.x[:, 0:TPB, :]).then_inc(core.stored, 16)
                moe.fetch(sp, 3)
                sp.wait_ge(moe.combined, 4)
                sp.dma_start(core.stored_rows(1), core.x[:, TPB:TILES, :]).then_inc(core.stored, 16)
                sp.wait_ge(core.stored, 16 * B)

            @block.gpsimd
            def _(pool):
                core.landed(pool, "moe_token")
                for b in range(B):
                    nc.gpsimd.tensor_copy(rows[:, b * TPB:(b + 1) * TPB, moe.TOKEN], moe.token[:]).then_inc(numbered, 1)
                mamba.make_masks(pool)
                pool.wait_ge(moe.cleared, 16 * 2 * 2 * B)
                pool.wait_ge(numbered, B)
                for r in range(B):
                    moe.scatter(pool, r)
                for u in range(HALF):
                    moe.send(pool, u)
                for g in range(2):
                    mamba.cut_a(pool, g)
                mamba.to_state(pool, 0)
                for g in range(N):
                    u, i = g // NC, g % NC
                    if g + 2 < N:
                        mamba.cut_a(pool, g + 2)
                    if i < NC - 1:
                        mamba.to_state(pool, g + 1)
                    mamba.gate(pool, g)
                    if i < NC - 1:
                        mamba.decay(pool, g + 1)
                    elif g + 1 < N:
                        mamba.to_state(pool, g + 1)
                    if u == 3 and i >= 4:
                        moe.scatter(pool, 2, 2 * (i - 4), 2 * (i - 3))
                moe.scatter(pool, 2, 8)
                for u in range(HALF, 2 * HALF):
                    moe.send(pool, u)
                    if u == HALF + 3:
                        moe.scatter(pool, 3)

            @block.vector
            def _(dve):
                ch = Chain(dve, chain)

                def experts(u, last):
                    if u + 1 < last:
                        moe.take(dve, u + 1)
                    moe.gating(dve, u)
                    moe.address(dve, u)

                nc.vector.memset(moe.xs[64:P, :, moe.FULL, :], 0.0).then_inc(moe.tail_clear, 1)
                core.landed(dve, "moe_iota")
                for i in range(GROUPS):
                    norm.stats_of(dve, ch, i)
                for r in range(B):
                    for half in range(2):
                        norm.normalise(dve, ch, 2 * r + half)
                    moe.shift(dve, ch, r)
                    moe.pick(dve, ch, r)
                    moe.put(dve, ch, r)
                mamba.weigh_out(dve)
                moe.take(dve, 0)
                for u in range(HALF):
                    experts(u, HALF)
                    if u == 10:
                        moe.combine(dve, ch, 0)
                        norm.stats_of(dve, ch, 4)
                        norm.stats_of(dve, ch, 5)
                        norm.normalise(dve, ch, 4)
                        norm.normalise(dve, ch, 5)
                    if u == 12:
                        mamba.step_sizes(dve, ch, 0)
                    if u >= 13:
                        for n in range(4 * (u - 13), 4 * (u - 12)):
                            mamba.convolve(dve, ch, 0, n)
                for n in range(12, 16):
                    mamba.convolve(dve, ch, 0, n)
                dve.wait_ge(mamba.decays, 3)
                mamba.front(dve, 0)
                for g in range(N):
                    u, i = g // NC, g % NC
                    if u >= 1 and i == 1:
                        mamba.variance(dve, u - 1)
                    if g + 1 < N and i < NC - 1:
                        mamba.front(dve, g + 1)
                    mamba.pass_state(dve, g)
                    mamba.back(dve, g)
                    if u >= 1 and i in (2, 3, 4):
                        mamba.add(dve, ch, u - 1, i - 2)
                    if u + 1 < UNITS:
                        for n in mamba.TAPS_AT[i]:
                            mamba.convolve(dve, ch, u + 1, n)
                    if u == 0 and i == 6:
                        moe.combine(dve, ch, 1)
                        norm.stats_of(dve, ch, 6)
                        norm.stats_of(dve, ch, 7)
                    if u == 0 and i == 7:
                        norm.normalise(dve, ch, 6)
                        norm.normalise(dve, ch, 7)
                    if u == 1 and i == 2:
                        mamba.step_sizes(dve, ch, 1)
                    if u == 2 and i == 5:
                        norm.stats_of(dve, ch, 8)
                        norm.stats_of(dve, ch, 9)
                    if u == 2 and i == 6:
                        norm.normalise(dve, ch, 8)
                        norm.normalise(dve, ch, 9)
                    if u == 3 and i == 0:
                        moe.shift(dve, ch, 2)
                    if u == 3 and i == 1:
                        moe.pick(dve, ch, 2)
                    if u == 3 and i == 2:
                        moe.put(dve, ch, 2)
                    if g + 1 < N and i == NC - 1:
                        mamba.front(dve, g + 1)
                moe.take(dve, HALF)
                for u in range(HALF, 2 * HALF):
                    experts(u, 2 * HALF)
                    if u == HALF:
                        mamba.variance(dve, UNITS - 1)
                        for part in range(PARTS_OUT):
                            mamba.add(dve, ch, UNITS - 1, part)
                        norm.stats_of(dve, ch, 10)
                        norm.stats_of(dve, ch, 11)
                        norm.normalise(dve, ch, 10)
                        norm.normalise(dve, ch, 11)
                    if u == HALF + 2:
                        moe.shift(dve, ch, 3)
                        moe.pick(dve, ch, 3)
                    if u == HALF + 3:
                        moe.put(dve, ch, 3)
                    if u == HALF + 13:
                        moe.combine(dve, ch, 2)
                moe.combine(dve, ch, 3)

            @block.scalar
            def _(act):
                def experts(u, last):
                    moe.silu(act, u)
                    if u > last - HALF:
                        moe.weigh(act, u - 1)

                for i in range(GROUPS):
                    norm.root(act, i)
                for r in range(B):
                    for half in range(2):
                        norm.copy(act, 2 * r + half)
                    moe.exp(act, r)
                mamba.exp_a(act)
                act.wait_ge(mamba.pads, 1)
                for u in range(HALF):
                    experts(u, HALF)
                    if u == 10:
                        norm.root(act, 4)
                        norm.root(act, 5)
                    if u == 11:
                        norm.copy(act, 4)
                        norm.copy(act, 5)
                    if u == 12:
                        mamba.exp_dt(act, 0)
                    if u == 14:
                        mamba.exp_sums(act, 0)
                    if u >= 12:
                        mamba.take(act, 0, u - 12)
                moe.weigh(act, HALF - 1)
                mamba.take(act, 0, 4)
                mamba.take(act, 0, 5)
                mamba.silus(act, 0)
                mamba.exps(act, 0)
                for g in range(N):
                    u, i = g // NC, g % NC
                    if g + 1 < N and i < NC - 1:
                        mamba.exps(act, g + 1)
                    if u >= 1 and i == 1:
                        mamba.deviation(act, u - 1)
                    if g >= 1:
                        mamba.square(act, g - 1)
                    if u + 1 < UNITS and i < mamba.PIECES:
                        mamba.take(act, u + 1, i)
                    if u + 1 < UNITS and i == 6:
                        mamba.silus(act, u + 1)
                    if u == 0 and i == 6:
                        norm.root(act, 6)
                        norm.root(act, 7)
                    if u == 0 and i == 7:
                        norm.copy(act, 6)
                        norm.copy(act, 7)
                    if u == 1 and i == 2:
                        mamba.exp_dt(act, 1)
                    if u == 1 and i == 4:
                        mamba.exp_sums(act, 1)
                    if u == 2 and i == 6:
                        norm.root(act, 8)
                        norm.root(act, 9)
                    if u == 2 and i == 7:
                        norm.copy(act, 8)
                        norm.copy(act, 9)
                    if u == 3 and i == 1:
                        moe.exp(act, 2)
                    if g + 1 < N and i == NC - 1:
                        mamba.exps(act, g + 1)
                mamba.square(act, N - 1)
                for u in range(HALF, 2 * HALF):
                    experts(u, 2 * HALF)
                    if u == HALF:
                        mamba.deviation(act, UNITS - 1)
                        norm.root(act, 10)
                        norm.root(act, 11)
                    if u == HALF + 1:
                        norm.copy(act, 10)
                        norm.copy(act, 11)
                    if u == HALF + 2:
                        moe.exp(act, 3)
                moe.weigh(act, 2 * HALF - 1)




def macaron(nc, dram, out, stages=99):
    with ExitStack() as ctx:
        core = Core(nc, dram, ctx)
        core.stored = core.sem("stored")
        core.stored_rows = lambda b: out[b].rearrange("(j p) d -> p j d", p=P)
        load_constants(core, ctx)
        core.moe = Moe(core)
        core.mamba = Mamba(core)
        core.ffn = ExitStack()
        load_ffn(core, core.ffn)
        core.early = ExitStack()
        core.attention = Attention(core, "attn")
        setup = Setup(core)
        todo = [lambda: ffn(core, "ffn_a", setup), lambda: attention(core), lambda: ffn(core, "ffn_b"), lambda: moe_mamba_moe(core)]
        for n, stage in enumerate(todo[:stages]):
            stage()
            core.end_stage()
            if n == 1:
                core.early.close()
            if n == 2:
                core.ffn.close()
        core.early.close()
        core.ffn.close()
        if stages < 4:
            with nc.Block() as block:
                @block.sync
                def _(sp):
                    for b in range(B):
                        sp.dma_start(core.stored_rows(b), core.x[:, b * TPB:(b + 1) * TPB, :]).then_inc(core.stored, 16)
                    sp.wait_ge(core.stored, 32)


def kernel(**inputs):
    import concourse.bacc as bacc
    from concourse.bass_utils import run_bass_kernel_spmd as run

    nc = bacc.Bacc("TRN2", target_bir_lowering=False, num_devices=1)
    arrays = layout(inputs)
    dram = {k: nc.dram_tensor(f"in_{k}", v.shape, mybir.dt.from_np(v.dtype), kind="ExternalInput").ap() for k, v in arrays.items()}
    out = nc.dram_tensor("out", (B, T, D), F32, kind="ExternalOutput").ap()
    macaron(nc, dram, out)
    r = run(nc, [{f"in_{k}": v for k, v in arrays.items()}], core_ids=[0])
    return r.results[0]["out"]
```

```python
from contextlib import ExitStack

import numpy as np

import concourse.bass as bass
from concourse import mybir

F32 = mybir.dt.float32
BF16 = mybir.dt.bfloat16
I32 = mybir.dt.int32
U32 = mybir.dt.uint32
ALU = mybir.AluOpType
ACT = mybir.ActivationFunctionType
AX_X = mybir.AxisListType.X

P = 128
B, T, D = 2, 1024, 128
TILES = B * T // P
TPB = T // P
GROUP = 4
GROUPS = TILES // GROUP
GT = GROUP * P
BANK = 512
LN_EPS = 1e-5

M, INNER = 64, 16
ON_PE = 8
HEADS, HD = 16, 8
PARTS = 3
HG = 4
HGROUPS = HEADS // HG
QK_ROWS = PARTS * PARTS * HD
QK_PAD = 96
NO_SHIFT_BOUND = 40.0
E_, CAP, FF = 8, 320, 448
TOPK = 2
FC = 112
FCH = FF // FC
SLOTS = E_ * CAP
DIN, NST, NH, HP = 256, 128, 4, 64
TAPS = 4


def host_constants():
    c = {}
    c["identity"] = np.eye(P, dtype=np.float32)
    freqs = (1.0 / np.float32(10000.0) ** (np.arange(0, HD, 2, dtype=np.float32) / np.float32(HD))).astype(np.float32)
    ang = np.arange(T, dtype=np.float32)[None, :] * freqs[:, None]
    cos, sin = np.cos(ang).astype(np.float32), np.sin(ang).astype(np.float32)
    sign = np.where(np.arange(HD) % 2 == 0, -1.0, 1.0).astype(np.float32)
    c["rope_cos"] = np.tile(np.repeat(cos, 2, axis=0), (HEADS, 1))
    c["rope_sin"] = np.tile(np.repeat(sin, 2, axis=0) * sign[:, None], (HEADS, 1))
    c["head_of_row"] = np.kron(np.eye(HEADS, dtype=np.float32), np.ones((HD, 1), np.float32))
    c["expert_iota"] = np.arange(E_, dtype=np.float32)[None, :]
    c["token"] = np.arange(T, dtype=np.float32).reshape(TPB, P).T
    return {k: np.ascontiguousarray(v) for k, v in c.items()}


def layout(inputs):
    a = {}
    f = lambda k: np.asarray(inputs[k])
    twice = lambda v: np.concatenate([v, v], axis=0)
    a["x"] = f("L0_attn_x")
    a["win"] = f("L0_ffn_Win")
    a["ffn_w1"] = twice(f("L0_ffn_W1"))
    a["ffn_b1"] = twice(f("L0_ffn_b1"))
    a["ffn_w2"] = twice(f("L0_ffn_W2"))
    a["ffn_bin"] = twice(f("L0_ffn_bin_"))[:, None]
    a["ffn_b2"] = twice(f("L0_ffn_b2"))[:, None]
    a["wout"] = f("L0_ffn_Wout")
    a["bout"] = f("L0_ffn_bout")[None, :]
    w, b = f("L0_attn_W_qkv"), f("L0_attn_b_qkv")
    swap = np.arange(D).reshape(-1, 2)[:, ::-1].ravel()
    wq, wk, wv = w[:D], w[D:2 * D], w[2 * D:]
    bq, bk, bv = b[:D], b[D:2 * D], b[2 * D:]
    a["w_qkv"] = np.stack([wq.T, wq[swap].T, wk.T, wk[swap].T, wv.T], axis=1)
    a["b_qk"] = np.stack([bq, bq[swap], bk, bk[swap]], axis=1)
    a["b_v"] = bv[None, :]
    a["gate"] = f("L1_ffn_gate_w").T
    a["w1"] = f("L1_ffn_w1").transpose(1, 0, 2)
    a["w3"] = f("L1_ffn_w3").transpose(1, 0, 2)
    a["w2"] = f("L1_ffn_w2").reshape(E_, FCH, FC, D).transpose(2, 0, 1, 3)
    both = lambda n, g: np.stack([g(f(f"L1_attn_{n}_f")), g(f(f"L1_attn_{n}_b"))], axis=1)
    columns = lambda v: v.reshape(-1, P).T
    z_end, x_end = DIN, DIN + 4 * P
    a["mb_w_xbc"] = both("Wi", lambda w: w[z_end:x_end].T.reshape(D, 4, P))
    a["mb_w_z"] = both("Wi", lambda w: w[:z_end].T.reshape(D, 2, P))
    a["mb_w_dt"] = both("Wi", lambda w: w[x_end:].T).reshape(D, 2 * NH)
    a["mb_taps"] = both("conv_w", lambda w: w[:, 0, :].reshape(4, P, TAPS).transpose(1, 0, 2))
    a["mb_conv_b"] = both("conv_b", columns)
    a["mb_skip"] = both("D", lambda v: columns(np.repeat(v, HP)))
    a["mb_norm_w"] = both("norm_w", columns)
    a["mb_wo"] = both("Wo", lambda w: w.T.reshape(2, P, D).transpose(1, 0, 2))
    a["mb_dt_bias"] = both("dt_bias", lambda v: v[None, :]).reshape(1, 2 * NH)
    a["mb_a_log"] = both("A_log", lambda v: v[None, :]).reshape(1, 2 * NH)
    a.update(host_constants())
    return {k: np.ascontiguousarray(v) for k, v in a.items()}


class Core:

    def __init__(self, nc, dram, ctx):
        self.nc, self.dram, self.ctx = nc, dram, ctx
        self.stage_sems, self.retired = [], []

    def sb(self, name, shape, dt=F32, ctx=None):
        return (ctx or self.ctx).enter_context(self.nc.sbuf_tensor(name, shape, dt))

    def sem(self, name, ctx=None):
        s = self.nc.alloc_semaphore(name)
        if ctx is not None:
            self.stage_sems.append(s)
        return s

    def end_stage(self):
        for s in self.retired:
            self.nc.release_semaphore(s)
        numbers = sorted(s.num for s in self.stage_sems)
        while numbers:
            n = 1
            while n < len(numbers) and numbers[n] == numbers[0] + n:
                n += 1
            self.nc.gpsimd.sem_clear(range(numbers[0], numbers[0] + n))
            numbers = numbers[n:]
        self.retired, self.stage_sems = self.stage_sems, []


class Chain:

    def __init__(self, eng, sem):
        self.eng, self.sem, self.n = eng, sem, 0

    def step(self, ins):
        ins.then_inc(self.sem, 1)
        self.n += 1
        return self.n

    def wait(self):
        self.eng.wait_ge(self.sem, self.n)


class LayerNorm:

    def __init__(self, core, name, ctx, xT, psum, order=range(GROUPS), xn=None):
        self.core, self.order, self.xT = core, list(order), xT
        self.psum = psum
        self.stats = core.sb(f"{name}_stats", [P, TILES, 6], ctx=ctx)
        self.mv = core.sb(f"{name}_mv", [P, TILES, 2], ctx=ctx)
        self.std = core.sb(f"{name}_std", [P, TILES], ctx=ctx)
        self.rstd = core.sb(f"{name}_rstd", [P, TILES], ctx=ctx)
        self.xn = xn if xn is not None else core.sb(f"{name}_xn", [P, TILES, D], ctx=ctx)
        self.aggregated = core.sem(f"{name}_aggregated", ctx)
        self.rooted = core.sem(f"{name}_rooted", ctx)
        self.normed = core.sem(f"{name}_normed", ctx)
        self.turned = core.sem(f"{name}_turned", ctx)
        self.ready = core.sem(f"{name}_ready", ctx)

    def group_tiles(self, i):
        return range(self.order[i] * GROUP, self.order[i] * GROUP + GROUP)

    def vector_stats(self, dve, ch, i):
        nc, x = self.core.nc, self.core.x
        for n in self.group_tiles(i):
            ch.step(nc.vector.bn_stats(self.stats[:, n, :], x[:, n, :]))
        ch.wait()
        for n in self.group_tiles(i):
            ins = nc.vector.bn_aggr(self.mv[:, n, :], self.stats[:, n, :])
        ins.then_inc(self.aggregated, 1)

    def scalar_root(self, act, i):
        tiles = self.group_tiles(i)
        act.wait_ge(self.aggregated, i + 1)
        self.core.nc.scalar.activation(self.std[:, tiles[0]:tiles[-1] + 1], self.mv[:, tiles[0]:tiles[-1] + 1, 1], ACT.Sqrt,
                                       bias=self.core.eps[:]).then_inc(self.rooted, 1)

    def vector_group(self, dve, ch, i):
        nc, x, tiles = self.core.nc, self.core.x, self.group_tiles(i)
        dve.wait_ge(self.aggregated, i + 1)
        dve.wait_ge(self.rooted, i + 1)
        ch.step(nc.vector.reciprocal(self.rstd[:, tiles[0]:tiles[-1] + 1], self.std[:, tiles[0]:tiles[-1] + 1]))
        ch.wait()
        for n in tiles:
            ins = nc.vector.tensor_scalar(self.xn[:, n, :], x[:, n, :], self.mv[:, n, 0:1], self.rstd[:, n:n + 1],
                                          ALU.subtract, ALU.mult)
        ins.then_inc(self.normed, 1)

    def tensor_group(self, pe, i):
        nc = self.core.nc
        pe.wait_ge(self.normed, i + 1)
        if i >= 2:
            pe.wait_ge(self.ready, i - 1)
        for j in range(GROUP):
            ins = nc.tensor.transpose(self.psum[:, i % 2, j * P:(j + 1) * P], self.xn[:, self.order[i] * GROUP + j, :],
                                      self.core.ident[:])
        ins.then_inc(self.turned, 1)

    def scalar_group(self, act, i):
        act.wait_ge(self.turned, i + 1)
        g = self.order[i]
        self.core.nc.scalar.copy(self.xT[:, g * GT:(g + 1) * GT], self.psum[:, i % 2, :]).then_inc(self.ready, 1)


def load_constants(core, ctx):
    nc, d = core.nc, core.dram
    core.x = core.sb("x_sb", [P, TILES, D])
    core.ident = core.sb("ident", [P, P])
    core.eps = core.sb("eps", [P, 1])
    core.loaded = {}

    def wait(eng, *names):
        for n in names:
            eng.wait_ge(core.loaded[n], 16)
    core.landed = wait


def load_ffn(core, ctx):
    sb = lambda n, shape: core.sb(n, shape, ctx=ctx)
    core.minus_b = sb("minus_b", [P, INNER])
    core.w2_b = sb("w2_b", [P, INNER])
    core.b2_all = sb("b2_all", [P, B])
    core.win = sb("win_sb", [D, M])
    core.w1 = sb("w1_sb", [P, INNER])
    core.b1 = sb("b1_sb", [P, INNER])
    core.w2 = sb("w2_sb", [P, INNER])
    core.bin = sb("bin_sb", [P, 1])
    core.b2 = sb("b2_sb", [P, 1])
    core.wout = sb("wout_sb", [P, B, D])
    core.bout = sb("bout_sb", [P, D])
    core.b_pre = sb("b_pre", [P, INNER])
    core.bout_half = sb("bout_half", [P, D])


class Setup:

    def __init__(self, core):
        d, self.core = core.dram, core
        tokens = d["x"].rearrange("b (j p) d -> p (b j) d", p=P)
        groups = [slice(g * GROUP, (g + 1) * GROUP) for g in range(GROUPS)]
        self.x_loads = [(f"x{g}", core.x[:, s, :], tokens[:, s, :]) for g, s in enumerate(groups)]
        self.ffn_loads = [("ident", core.ident[:], d["identity"]), ("win", core.win[:], d["win"]),
                          ("ffn_w1", core.w1[:], d["ffn_w1"]), ("ffn_b1", core.b1[:], d["ffn_b1"]), ("ffn_bin", core.bin[:], d["ffn_bin"]),
                          ("ffn_w2", core.w2[:], d["ffn_w2"]), ("ffn_b2", core.b2[:], d["ffn_b2"]),
                          ("bout", core.bout[:], d["bout"].to_broadcast([P, D])),
                          ("wout_0", core.wout[0:M, 0, :], d["wout"]), ("wout_1", core.wout[M:P, 1, :], d["wout"])]
        for name, _, _ in (*self.x_loads, *self.ffn_loads):
            core.loaded[name] = core.sem(f"ld_{name}")
        self.zeros = core.sb("zeros", [P, SLOTS // P, core.moe.ROW], ctx=core.early)
        self.zeroed, self.ones_set, self.tri_set, self.set = (core.sem(n) for n in ("zeroed", "ones_set", "tri_set", "constants_set"))

    def start(self, eng, loads):
        for name, dst, src in loads:
            eng.dma_start(dst, src).then_inc(self.core.loaded[name], 16)

    def sync(self, sp):
        core, moe = self.core, self.core.moe
        self.start(sp, self.x_loads)
        self.start(sp, (*core.attention.loads, *moe.loads, *core.mamba.loads))
        sp.wait_ge(self.zeroed, 2)
        for r in range(2 * B):
            sp.dma_start(moe.slots[r].rearrange("(p n) d -> p n d", p=P), self.zeros[:]).then_inc(moe.cleared, 16)
            sp.dma_start(moe.rows[r].rearrange("(p n) d -> p n d", p=P), self.zeros[:, 0:TOPK * T // P, 0:D]).then_inc(moe.cleared, 16)

    def scalar(self, act):
        self.start(act, self.ffn_loads)

    def vector(self, dve):
        nc, core = self.core.nc, self.core
        nc.vector.memset(core.eps[:], LN_EPS).then_inc(self.set, 1)
        nc.vector.memset(core.wout[0:M, 1, :], 0.0).then_inc(self.set, 1)
        nc.vector.memset(core.wout[M:P, 0, :], 0.0).then_inc(self.set, 1)

    def gpsimd(self, pool):
        nc, moe, zeros = self.core.nc, self.core.moe, self.zeros
        nc.gpsimd.memset(zeros[:], 0.0).then_inc(self.zeroed, 1)
        nc.gpsimd.memset(moe.tri[:], 1.0).then_inc(self.ones_set, 1)
        pool.wait_ge(self.zeroed, 1)
        nc.gpsimd.memset(zeros[:, :, moe.TOKEN], moe.NOWHERE).then_inc(self.zeroed, 1)
        pool.wait_ge(self.ones_set, 1)
        nc.gpsimd.affine_select(out=moe.tri[:, 0, :], in_=moe.tri[:, 0, :], compare_op=ALU.is_ge, fill=0.0, base=0,
                                pattern=[[1, P]], channel_multiplier=-1).then_inc(self.tri_set, 1)


def ffn(core, name, setup=None):
    nc, ctx = core.nc, ExitStack()
    RING = 4
    xT = core.sb(f"{name}_xT", [D, B * T], ctx=ctx)
    relu = core.sb(f"{name}_relu", [P, RING, T], ctx=ctx)
    acc = core.sb(f"{name}_acc", [P, T], ctx=ctx)
    mix = core.sb(f"{name}_mix", [P, T], ctx=ctx)
    xb = core.sb(f"{name}_xb", [P, TILES, D], ctx=ctx)
    psum = lambda n, shape: ctx.enter_context(nc.psum_tensor(f"{name}_{n}", shape, F32))
    ps_t, ps_s, ps_g, ps_o = psum("ps_t", [P, 2, BANK]), psum("ps_s", [P, T]), psum("ps_g", [P, T]), psum("ps_o", [P, 2, BANK])
    sem = lambda n: core.sem(f"{name}_{n}", ctx)
    s_done, relu_done, pe_used, dve_used = sem("s_done"), sem("relu_done"), sem("pe_used"), sem("dve_used")
    mixed, out_done, out_read, xb_done, steps = sem("mixed"), sem("out_done"), sem("out_read"), sem("xb_done"), sem("steps")
    core.diag = core.sb("diag", [P, ON_PE, P], ctx=ctx)
    made = sem("made")
    ln = LayerNorm(core, f"{name}_ln", ctx, xT, ps_t)
    on_pe = [h for h in range(INNER) if h % 2 == 1]
    on_dve = [h for h in range(INNER) if h % 2 == 0]
    slot = {h: i for i, h in enumerate(on_pe)}

    def freed(eng, h):
        if h >= RING:
            old = h - RING
            if old in on_pe:
                eng.wait_ge(pe_used, on_pe.index(old) + 1)
            else:
                eng.wait_ge(dve_used, on_dve.index(old) + 1)

    with nc.Block() as block:
        @block.sync
        def _(sp):
            if setup:
                setup.sync(sp)

        @block.vector
        def _(dve):
            ch = Chain(dve, steps)
            if setup:
                setup.vector(dve)
            for i in range(GROUPS):
                core.landed(dve, f"x{i}")
                ln.vector_stats(dve, ch, i)
            if setup:
                core.landed(dve, "ffn_w1", "ffn_b1", "ffn_bin")
                nc.vector.scalar_tensor_tensor(core.b_pre[:], core.w1[:], core.bin[:], core.b1[:], ALU.mult, ALU.add).then_inc(made, 1)
                core.landed(dve, "ffn_w2", "ffn_b2")
                dve.wait_ge(made, 1)
                ch.step(nc.vector.memset(core.b2_all[:], 0.0))
                nc.vector.tensor_scalar(core.minus_b[:], core.b_pre[:], -1.0, None, ALU.mult)
                ch.step(nc.vector.tensor_tensor(core.w2_b[:], core.w2[:], core.b_pre[:], ALU.mult))
                ch.wait()
                for b in range(B):
                    if FfnOfBatch.ON_ACT[b] < INNER:
                        ch.step(nc.vector.reduce_sum(core.b2_all[:, b:b + 1], core.w2_b[:, FfnOfBatch.ON_ACT[b]:INNER], AX_X))
                ch.wait()
                ch.step(nc.vector.tensor_tensor(core.b2_all[:], core.b2_all[:], core.b2[:].to_broadcast([P, B]), ALU.add))
                core.landed(dve, "bout")
                nc.vector.tensor_scalar(core.bout_half[:], core.bout[:], 0.5, None, ALU.mult).then_inc(made, 1)
            for i in range(GROUPS):
                ln.vector_group(dve, ch, i)
            core.landed(dve, "ffn_w2", "ident", "ffn_b2")
            if setup:
                for n in range(ON_PE):
                    ins = nc.vector.tensor_scalar(core.diag[:, n, :], core.ident[:], core.w2[:, 2 * n + 1:2 * n + 2], None, ALU.mult)
                ins.then_inc(made, 1)
            for n, h in enumerate(on_dve):
                dve.wait_ge(relu_done, h + 1)
                if n == 0:
                    ins = nc.vector.tensor_scalar(acc[:], relu[:, h % RING, :], core.w2[:, h:h + 1], None, ALU.mult)
                else:
                    dve.wait_ge(dve_used, n)
                    ins = nc.vector.scalar_tensor_tensor(acc[:], relu[:, h % RING, :], core.w2[:, h:h + 1], acc[:],
                                                         ALU.mult, ALU.add)
                ins.then_inc(dve_used, 1)
            dve.wait_ge(dve_used, len(on_dve))
            dve.wait_ge(pe_used, len(on_pe))
            for i in range(2):
                nc.vector.scalar_tensor_tensor(mix[:, i * BANK:(i + 1) * BANK], ps_g[:, i * BANK:(i + 1) * BANK], core.b2[:],
                                               acc[:, i * BANK:(i + 1) * BANK], ALU.add, ALU.add).then_inc(mixed, 1)
            dve.wait_ge(xb_done, 1)
            for g in range(GROUPS):
                dve.wait_ge(out_done, g + 1)
                nc.vector.scalar_tensor_tensor(core.x[:, g * GROUP:(g + 1) * GROUP, :].rearrange("p a d -> p (a d)"),
                                               ps_o[:, g % 2, :], 0.5,
                                               xb[:, g * GROUP:(g + 1) * GROUP, :].rearrange("p a d -> p (a d)"),
                                               ALU.mult, ALU.add).then_inc(out_read, 1)

        @block.gpsimd
        def _(pool):
            if setup:
                setup.gpsimd(pool)
                core.landed(pool, "x0", "x1", "x2", "x3")
                pool.wait_ge(made, 2)
            nc.gpsimd.tensor_tensor(xb[:], core.x[:], core.bout_half[:].unsqueeze(1).to_broadcast([P, TILES, D]),
                                    ALU.add).then_inc(xb_done, 1)

        @block.scalar
        def _(act):
            if setup:
                setup.scalar(act)
                act.wait_ge(setup.set, 3)
            for i in range(GROUPS):
                ln.scalar_root(act, i)
            for i in range(GROUPS):
                ln.scalar_group(act, i)
            act.wait_ge(s_done, GROUPS)
            if setup:
                act.wait_ge(made, 1)
            for h in range(INNER):
                freed(act, h)
                nc.scalar.activation(relu[:, h % RING, :], ps_s[:], ACT.Relu, bias=core.b_pre[:, h:h + 1],
                                     scale=core.w1[:, h:h + 1]).then_inc(relu_done, 1)

        @block.tensor
        def _(pe):
            core.landed(pe, "ident", "win", "wout_0", "wout_1")
            for i in range(GROUPS):
                ln.tensor_group(pe, i)
                pe.wait_ge(ln.ready, i + 1)
                b, half = i // 2, i % 2
                nc.tensor.matmul(ps_s[M * b:M * b + M, half * GT:(half + 1) * GT], core.win[:], xT[:, i * GT:(i + 1) * GT],
                                 start=True, stop=True).then_inc(s_done, 1)
            if setup:
                pe.wait_ge(made, 3)
            for n, h in enumerate(on_pe):
                pe.wait_ge(relu_done, h + 1)
                for i in range(2):
                    ins = nc.tensor.matmul(ps_g[:, i * BANK:(i + 1) * BANK], core.diag[:, n, :],
                                           relu[:, h % RING, i * BANK:(i + 1) * BANK], start=(n == 0), stop=(n == len(on_pe) - 1))
                ins.then_inc(pe_used, 1)
            if setup:
                pe.wait_ge(setup.set, 3)
            for g in range(GROUPS):
                pe.wait_ge(mixed, 2 if g % 2 else 1)
                if g >= 2:
                    pe.wait_ge(out_read, g - 1)
                for j in range(GROUP):
                    t = (g % 2) * GROUP + j
                    ins = nc.tensor.matmul(ps_o[:, g % 2, j * D:(j + 1) * D], mix[:, t * P:(t + 1) * P],
                                           core.wout[:, g // 2, :], start=True, stop=True)
                ins.then_inc(out_done, 1)
    ctx.close()


class Attention:

    def __init__(self, core, name):
        nc = core.nc
        self.core, self.name, self.ctx = core, name, core.early
        dram = lambda n, shape, dt: nc.dram_tensor(f"{name}_{n}", shape, dt).ap()
        self.q_parts = dram("q_parts", (B, HEADS, PARTS, HD, T), BF16)
        self.k_parts = dram("k_parts", (B, HEADS, 2 * PARTS - 1, HD, T), BF16)
        self.shift = dram("shift", (B, HEADS, PARTS, T), BF16)
        self.v = core.sb(f"{name}_v", [P, TILES, HEADS, 32], ctx=self.ctx)
        self.flag = core.sb(f"{name}_flag", [1, 1], I32, ctx=self.ctx)
        sb, d = (lambda n, shape: core.sb(f"{name}_{n}", shape, ctx=self.ctx)), core.dram
        self.w, self.b_qk, self.b_v = sb("w", [D, 5, D]), sb("b_qk", [D, 4]), sb("b_v", [P, D])
        self.cos, self.sin, self.head_of_row = sb("cos", [D, T]), sb("sin", [D, T]), sb("head_of_row", [P, HEADS])
        self.loads = [("w_qkv", self.w[:], d["w_qkv"]), ("b_qk", self.b_qk[:], d["b_qk"]), ("rope_cos", self.cos[:], d["rope_cos"]),
                      ("rope_sin", self.sin[:], d["rope_sin"]), ("b_v", self.b_v[:], d["b_v"].to_broadcast([P, D])),
                      ("head_of_row", self.head_of_row[:], d["head_of_row"])]
        for n, _, _ in self.loads:
            core.loaded[n] = core.sem(f"ld_{n}")

    def sem(self, n, ctx):
        return self.core.sem(f"{self.name}_{n}", ctx)

    def prepare(self):
        core, nc, name = self.core, self.core.nc, self.name
        with ExitStack() as ctx:
            sb = lambda n, shape, dt=F32: core.sb(f"{name}_{n}", shape, dt, ctx)
            sem = lambda n: self.sem(n, ctx)
            psum = lambda n, shape: ctx.enter_context(nc.psum_tensor(f"{name}_{n}", shape, F32))
            xT = sb("xT", [D, B * T])
            w, b_qk, b_v, cos, sin, head_of_row = self.w, self.b_qk, self.b_v, self.cos, self.sin, self.head_of_row
            t_cos, t_sin, rot, rest = sb("t_cos", [D, 2, GT]), sb("t_sin", [D, 2, GT]), sb("rot", [D, 2, GT]), sb("rest", [D, 2, GT])
            parts = sb("parts", [D, 2, PARTS, B * T], BF16)
            zero = sb("zero", [P, PARTS * B * HEADS * T // P], BF16)
            peaks = sb("peaks", [D, 2, GROUPS])
            peak = sb("peak", [D, 2, B])
            bound_rows = sb("bound_rows", [D, B])
            bound = sb("bound", [1, 1])
            ps_t, ps_qk, ps_v = psum("ps_t", [P, 2, BANK]), psum("ps_qk", [P, 4, BANK]), psum("ps_v", [P, 2, BANK])
            ln = LayerNorm(core, f"{name}_ln", ctx, xT, ps_t)
            steps, qk_done, v_done, v_read, v_filled = sem("steps"), sem("qk_done"), sem("v_done"), sem("v_read"), sem("v_filled")
            qk_read, rot_done, part0, rest_done, part1, part2 = (sem(n) for n in ("qk_read", "rot_done", "part0", "rest_done",
                                                                                   "part1", "part2"))
            scratch, zeroed, shift_clear = sem("scratch"), sem("zeroed"), sem("shift_clear")
            rows_done, bound_done = sem("rows_done"), sem("bound_done")

            with nc.Block() as block:
                @block.sync
                def _(sp):
                    sp.wait_ge(zeroed, 1)
                    sp.dma_start(self.shift.rearrange("b h i t -> (b h i t)").rearrange("(p n) -> p n", p=P), zero[:])\
                      .then_inc(shift_clear, 16)
                    for b in range(B):
                        sp.wait_ge(part0, 4 * (b + 1))
                        sp.wait_ge(part1, 4 * (b + 1))
                        sp.wait_ge(part2, 4 * (b + 1))
                        for which, dst, n in ((0, self.q_parts, PARTS), (1, self.k_parts, 2 * PARTS - 1)):
                            for j in range(n):
                                sp.dma_start(dst[b, :, j, :, :], parts[:, which, j % PARTS, b * T:(b + 1) * T]).then_inc(scratch, 16)
                    sp.wait_ge(scratch, 16 * B * (3 * PARTS - 1))
                    sp.wait_ge(shift_clear, 16)

                @block.gpsimd
                def _(pool):
                    nc.gpsimd.memset(zero[:], 0.0).then_inc(zeroed, 1)
                    nc.gpsimd.memset(self.v[:], 0.0).then_inc(v_filled, 1)
                    pool.wait_ge(v_filled, 1)
                    nc.gpsimd.memset(self.v[:, :, :, HD:HD + 1], 1.0).then_inc(v_filled, 1)

                @block.vector
                def _(dve):
                    ch = Chain(dve, steps)
                    for i in range(GROUPS):
                        ln.vector_stats(dve, ch, i)
                    for i in range(GROUPS):
                        ln.vector_group(dve, ch, i)
                    core.landed(dve, "b_qk", "rope_cos", "rope_sin", "b_v")
                    dve.wait_ge(v_filled, 2)
                    for i in range(GROUPS):
                        at = slice((i % 2) * GT, (i % 2) * GT + GT)
                        to = slice(i * GT, (i + 1) * GT)
                        for k in range(2):
                            dve.wait_ge(qk_done, 2 * i + k + 1)
                            nc.vector.scalar_tensor_tensor(t_cos[:, k, :], ps_qk[:, 2 * k, :], b_qk[:, 2 * k:2 * k + 1], cos[:, at],
                                                           ALU.add, ALU.mult)
                            ins = nc.vector.scalar_tensor_tensor(t_sin[:, k, :], ps_qk[:, 2 * k + 1, :], b_qk[:, 2 * k + 1:2 * k + 2],
                                                                 sin[:, at], ALU.add, ALU.mult)
                            ins.then_inc(qk_read, 1)
                        dve.wait_ge(qk_read, 2 * i + 2)
                        for k in range(2):
                            nc.vector.tensor_tensor(rot[:, k, :], t_cos[:, k, :], t_sin[:, k, :], ALU.add).then_inc(rot_done, 1)
                        dve.wait_ge(v_done, i + 1)
                        nc.vector.tensor_tensor(self.v[:, i * GROUP:(i + 1) * GROUP, :, 0:HD],
                                                ps_v[:, i % 2, :].rearrange("p (j h d) -> p j h d", j=GROUP, h=HEADS),
                                                b_v[:].rearrange("p (h d) -> p h d", h=HEADS).unsqueeze(1)
                                                .to_broadcast([P, GROUP, HEADS, HD]), ALU.add).then_inc(v_read, 1)
                        dve.wait_ge(rot_done, 2 * i + 2)
                        nc.vector.tensor_reduce(peaks[:, :, i:i + 1], rot[:], AX_X, ALU.max, apply_absolute_value=True)
                        for k in range(2):
                            dve.wait_ge(part0, 2 * i + k + 1)
                            nc.vector.tensor_tensor(rest[:, k, :], rot[:, k, :], parts[:, k, 0, to], ALU.subtract).then_inc(rest_done, 1)
                        dve.wait_ge(rest_done, 2 * i + 2)
                        for k in range(2):
                            dve.wait_ge(part1, 2 * i + k + 1)
                            nc.vector.tensor_tensor(parts[:, k, 2, to], rest[:, k, :], parts[:, k, 1, to], ALU.subtract).then_inc(part2, 1)
                    dve.wait_ge(part2, 2 * GROUPS)
                    ch.step(nc.vector.tensor_reduce(peak[:].rearrange("p k b -> p (k b)").unsqueeze(2),
                                                    peaks[:].rearrange("p k (b g) -> p (k b) g", b=B), AX_X, ALU.max))
                    ch.wait()
                    nc.vector.tensor_tensor(bound_rows[:], peak[:, 0, :], peak[:, 1, :], ALU.mult).then_inc(rows_done, 1)
                    dve.wait_ge(bound_done, 1)
                    ch.step(nc.vector.reduce_max(bound[:], ps_v[0:1, 0, 0:B * HEADS], AX_X))
                    ch.wait()
                    nc.vector.tensor_scalar(self.flag[:], bound[:], NO_SHIFT_BOUND * HD ** 0.5, None, ALU.is_gt)

                @block.scalar
                def _(act):
                    for i in range(GROUPS):
                        ln.scalar_root(act, i)
                    for i in range(GROUPS):
                        ln.scalar_group(act, i)
                    for i in range(GROUPS):
                        to = slice(i * GT, (i + 1) * GT)
                        for k in range(2):
                            act.wait_ge(rot_done, 2 * i + k + 1)
                            nc.scalar.copy(parts[:, k, 0, to], rot[:, k, :]).then_inc(part0, 1)
                        for k in range(2):
                            act.wait_ge(rest_done, 2 * i + k + 1)
                            nc.scalar.copy(parts[:, k, 1, to], rest[:, k, :]).then_inc(part1, 1)

                @block.tensor
                def _(pe):
                    core.landed(pe, "ident")
                    for i in range(GROUPS):
                        ln.tensor_group(pe, i)
                    core.landed(pe, "w_qkv")
                    for i in range(GROUPS):
                        pe.wait_ge(ln.ready, i + 1)
                        for k in range(2):
                            if i >= 1:
                                pe.wait_ge(qk_read, 2 * (i - 1) + k + 1)
                            for s in range(2):
                                ins = nc.tensor.matmul(ps_qk[:, 2 * k + s, :], w[:, 2 * k + s, :], xT[:, i * GT:(i + 1) * GT],
                                                       start=True, stop=True)
                            ins.then_inc(qk_done, 1)
                        if i >= 2:
                            pe.wait_ge(v_read, i - 1)
                        for j in range(GROUP):
                            n = i * GROUP + j
                            ins = nc.tensor.matmul(ps_v[:, i % 2, j * D:(j + 1) * D], xT[:, n * P:(n + 1) * P], w[:, 4, :],
                                                   start=True, stop=True)
                        ins.then_inc(v_done, 1)
                    core.landed(pe, "head_of_row")
                    pe.wait_ge(rows_done, 1)
                    pe.wait_ge(v_read, GROUPS)
                    for b in range(B):
                        ins = nc.tensor.matmul(ps_v[0:1, 0, b * HEADS:(b + 1) * HEADS], bound_rows[:, b:b + 1], head_of_row[:],
                                               start=True, stop=True)
                    ins.then_inc(bound_done, 1)

    def load_heads(self, eng, q, k, b, hg, landed):
        heads = slice(hg * HG, (hg + 1) * HG)
        for r in range(PARTS):
            rows = slice(r * PARTS * HD, (r + 1) * PARTS * HD)
            eng.dma_start(q[rows, :, :], self.q_parts[b, heads].rearrange("h i d t -> (i d) h t")).then_inc(landed, 16)
            eng.dma_start(k[rows, :, :], self.k_parts[b, heads, r:r + PARTS].rearrange("h i d t -> (i d) h t")).then_inc(landed, 16)

    def find_shift(self):
        core, nc, name = self.core, self.core.nc, self.name
        STEPS = HG * TPB
        NG = B * HGROUPS
        LOADS = 2 * PARTS
        with ExitStack() as ctx:
            sb = lambda n, shape, dt=F32: core.sb(f"{name}_{n}", shape, dt, ctx)
            sem = lambda n: self.sem(n, ctx)
            q, k = sb("shift_q", [QK_ROWS, HG, T], BF16), sb("shift_k", [QK_ROWS, HG, T], BF16)
            peak, rest = sb("shift_peak", [P, HG, TPB]), sb("shift_rest", [P, HG, TPB])
            parts = sb("shift_parts", [P, PARTS, HG, TPB], BF16)
            ps = ctx.enter_context(nc.psum_tensor(f"{name}_shift_ps", [P, 2, T], F32))
            free, landed, scored, maxed, own, split, stored = (
                sem(f"shift_{n}") for n in ("free", "landed", "scored", "maxed", "own", "split", "stored"))
            groups = lambda ap: ap.rearrange("b (g h) i d t -> (b g) h i d t", h=HG)

            def needed(eng):
                flag = eng.alloc_register(f"{name}_needs_shift")
                eng.reg_load(flag, self.flag[0:1, 0:1])
                return eng.If_ne(flag, 0)

            with nc.Block() as block:
                @block.sync
                def _(sp):
                    with needed(sp):
                        sp.sem_inc(free, 1)
                        with sp.Fori(0, NG) as g:
                            sp.wait_ge(free, g + 1)
                            for r in range(PARTS):
                                rows = slice(r * PARTS * HD, (r + 1) * PARTS * HD)
                                sp.dma_start(q[rows, :, :], groups(self.q_parts)[bass.ds(g, 1)].rearrange("g h i d t -> (g i d) h t"))\
                                  .then_inc(landed, 16)
                                sp.dma_start(k[rows, :, :], groups(self.k_parts)[bass.ds(g, 1), :, r:r + PARTS]
                                             .rearrange("g h i d t -> (g i d) h t")).then_inc(landed, 16)
                            sp.wait_ge(split, g + 1)
                            dst = self.shift.rearrange("b (g h) i t -> (b g) h i t", h=HG)[bass.ds(g, 1)]
                            for i in range(PARTS):
                                for h in range(HG):
                                    with nc.allow_non_contiguous_dma("one value of a query to a row"):
                                        sp.dma_start(dst[:, h, i, :].rearrange("g (j p) -> (g p) j", p=P), parts[:, i, h, :]).then_inc(stored, 16)
                            sp.wait_ge(stored, 16 * PARTS * HG * (g + 1))
                            sp.sem_inc(free, 1)

                @block.tensor
                def _(pe):
                    with needed(pe):
                        with pe.Fori(0, NG) as g:
                            pe.wait_ge(landed, 16 * LOADS * (g + 1))
                            for n in range(STEPS):
                                pe.wait_ge(maxed, STEPS * g + n + 1)
                                for half in range(2):
                                    ins = nc.tensor.matmul(ps[:, n % 2, half * BANK:(half + 1) * BANK], q[:, n // TPB, n % TPB * P:n % TPB * P + P],
                                                           k[:, n // TPB, half * BANK:(half + 1) * BANK], start=True, stop=True)
                                ins.then_inc(scored, 1)

                @block.vector
                def _(dve):
                    with needed(dve):
                        dve.sem_inc(maxed, 2)
                        with dve.Fori(0, NG) as g:
                            for n in range(STEPS):
                                dve.wait_ge(scored, STEPS * g + n + 1)
                                nc.vector.reduce_max(peak[:, n // TPB, n % TPB:n % TPB + 1], ps[:, n % 2, :], AX_X).then_inc(maxed, 1)
                            dve.wait_ge(maxed, STEPS * (g + 1) + 2)
                            dve.wait_ge(free, g + 1)
                            nc.vector.tensor_scalar(parts[:, 0, :, :], peak[:], -1.0, None, ALU.mult).then_inc(own, 1)
                            dve.wait_ge(own, 3 * g + 1)
                            nc.vector.scalar_tensor_tensor(rest[:], peak[:], -1.0, parts[:, 0, :, :], ALU.mult, ALU.subtract).then_inc(own, 1)
                            dve.wait_ge(own, 3 * g + 2)
                            nc.vector.tensor_copy(parts[:, 1, :, :], rest[:]).then_inc(own, 1)
                            dve.wait_ge(own, 3 * g + 3)
                            nc.vector.tensor_tensor(parts[:, 2, :, :], rest[:], parts[:, 1, :, :], ALU.subtract).then_inc(split, 1)

    def attend(self):
        core, nc, name = self.core, self.core.nc, self.name
        UNITS = 2 * TPB
        SB_, PB = 3, 4
        blocks = [(b, hg, half) for b in range(B) for hg in range(HGROUPS) for half in range(2)]
        LOADS = 2 * PARTS + 1
        LAST = len(blocks) // B - 1
        moe, norm = core.moe, core.norm
        with ExitStack() as ctx:
            sb = lambda n, shape, dt=F32: core.sb(f"{name}_{n}", shape, dt, ctx)
            sem = lambda n: self.sem(n, ctx)
            psum = lambda n, shape: ctx.enter_context(nc.psum_tensor(f"{name}_{n}", shape, F32))
            q = [sb(f"q{i}", [QK_PAD, HG, T], BF16) for i in range(2)]
            k = [sb(f"k{i}", [QK_PAD, HG, T], BF16) for i in range(2)]
            p = sb("p", [P, PB, 2, BANK])
            mixed = sb("mixed", [P, 2, BANK])
            rden = sb("rden", [P, GROUP, HG])
            scaled = sb("scaled", [P, GROUP, HG, HD])
            ps_s, ps_av = psum("ps_s", [P, SB_, 2, BANK]), psum("ps_av", [P, BANK])
            norm.side = SideBanks(psum("ps_side", [P, 1, BANK]), 1)
            ffn = FfnOfBatch(core, "ffn_b0", ctx, 0, norm, 0, sb("ffn_work", [P, 6, GT]))
            chain, numbered = sem("dve_chain"), sem("numbered")
            padded = sem("padded")
            landed = [sem(f"heads{i}") for i in range(2)]
            scored, exped, summed, av_read, turned, den_done, out_done, o_read = (
                sem(n) for n in ("scored", "exped", "summed", "av_read", "turned", "den_done", "out_done", "o_read"))

            with nc.Block() as block:
                @block.sync
                def _(sp):
                    sp.wait_ge(padded, 4)
                    for n, (b, hg) in enumerate((b, hg) for b in range(B) for hg in range(HGROUPS)):
                        if n >= 2:
                            sp.wait_ge(scored, 2 * UNITS * (n - 1))
                        self.load_heads(sp, q[n % 2], k[n % 2], b, hg, landed[n % 2])
                        sp.dma_start(q[n % 2][QK_ROWS:QK_ROWS + PARTS, :, :],
                                     self.shift[b, hg * HG:(hg + 1) * HG].rearrange("h i t -> i h t")).then_inc(landed[n % 2], 16)
                    sp.wait_ge(moe.cleared, 16 * 2 * 2 * B)
                    sp.wait_ge(moe.scattered[0], 16 * TOPK * TPB)

                @block.gpsimd
                def _(pool):
                    for i in range(2):
                        nc.gpsimd.memset(q[i][64:QK_PAD, :, :], 0.0).then_inc(padded, 1)
                        nc.gpsimd.memset(k[i][64:QK_PAD, :, :], 1.0).then_inc(padded, 1)
                    core.landed(pool, "moe_token")
                    pool.wait_ge(padded, 4)
                    for b in range(B):
                        nc.gpsimd.tensor_copy(core.rows[:, b * TPB:(b + 1) * TPB, moe.TOKEN], moe.token[:]).then_inc(numbered, 1)
                    ffn.base(pool)
                    pool.wait_ge(moe.cleared, 16 * 2 * 2 * B)
                    pool.wait_ge(numbered, B)
                    moe.scatter(pool, 0)

                @block.tensor
                def _(pe):
                    def scores(n, u):
                        b, hg, half = blocks[n]
                        w, i = n * UNITS + u, n // 2
                        kt, pair = u // 2, u % 2
                        if u == 0:
                            pe.wait_ge(landed[i % 2], 16 * LOADS * (i // 2 + 1))
                        if w >= SB_:
                            pe.wait_ge(exped, w - SB_ + 1)
                        for j in range(2):
                            h = 2 * pair + j
                            ins = nc.tensor.matmul(ps_s[:, w % SB_, j, :], k[i % 2][:, h, kt * P:(kt + 1) * P],
                                                   q[i % 2][:, h, half * BANK:(half + 1) * BANK], start=True, stop=True)
                        ins.then_inc(scored, 1)

                    def weigh(n, u):
                        b, hg, half = blocks[n]
                        w = n * UNITS + u
                        kt, pair = u // 2, u % 2
                        if u == 0 and n >= 1:
                            pe.wait_ge(av_read, n)
                        pe.wait_ge(exped, w + 1)
                        for j in range(2):
                            h = 2 * pair + j
                            ins = nc.tensor.matmul(ps_av[32 * h:32 * h + 32, :], self.v[:, b * TPB + kt, hg * HG + h, :],
                                                   p[:, w % PB, j, :], start=(kt == 0), stop=(kt == TPB - 1))
                        ins.then_inc(summed, 1)

                    def turn(n):
                        pe.wait_ge(av_read, n + 1)
                        ps_o = norm.side.take(pe, ("out", n), o_read, n + 1)
                        for j in range(GROUP):
                            ins = nc.tensor.transpose(ps_o[:, j * P:(j + 1) * P], mixed[:, n % 2, j * P:(j + 1) * P], core.ident[:])
                        ins.then_inc(turned, 1)

                    AHEAD = 3
                    total = len(blocks) * UNITS
                    for w in range(total + AHEAD):
                        if w >= AHEAD:
                            weigh((w - AHEAD) // UNITS, (w - AHEAD) % UNITS)
                        if w < total:
                            scores(w // UNITS, w % UNITS)
                        if w >= UNITS + 5 and (w - 5) % UNITS == 0:
                            turn((w - 5) // UNITS - 1)
                        n, u = w // UNITS - LAST, w % UNITS
                        if (n, u) in ((2, 8), (2, 10)):
                            norm.turn(pe, (u - 8) // 2)
                        if (n, u) == (2, 13):
                            ffn.project(pe)
                        if (n, u) in ((5, 8), (5, 9)):
                            ffn.output(pe, u - 8)
                        if (n, u) in ((5, 15), (6, 1)):
                            norm.turn(pe, n - 3)
                        if (n, u) == (6, 8):
                            moe.logits(pe, 0)
                        if (n, u) == (7, 1):
                            moe.counts(pe, 0)
                    turn(len(blocks) - 1)

                @block.scalar
                def _(act):
                    for w in range(len(blocks) * UNITS):
                        act.wait_ge(scored, w + 1)
                        if w >= PB:
                            act.wait_ge(summed, w - PB + 1)
                        nc.scalar.activation(p[:, w % PB, :, :].rearrange("p a n -> p (a n)"),
                                             ps_s[:, w % SB_, :, :].rearrange("p a n -> p (a n)"), ACT.Exp,
                                             scale=float(HD) ** -0.5).then_inc(exped, 1)
                        n, u = w // UNITS - LAST, w % UNITS
                        if (n, u) == (1, 6):
                            norm.root(act, 0)
                            norm.root(act, 1)
                        if (n, u) == (5, 12):
                            norm.root(act, 2)
                            norm.root(act, 3)
                        if (n, u) == (6, 10):
                            moe.exp(act, 0)

                @block.vector
                def _(dve):
                    ch = Chain(dve, chain)
                    core.landed(dve, "moe_iota")
                    for n, (b, hg, half) in enumerate(blocks):
                        dve.wait_ge(summed, UNITS * (n + 1))
                        if n >= 2:
                            dve.wait_ge(turned, n - 1)
                        nc.vector.tensor_copy(mixed[:, n % 2, :], ps_av[:]).then_inc(av_read, 1)
                        dve.wait_ge(turned, n + 1)
                        o = norm.side.of(("out", n)).rearrange("p (j h c) -> p j h c", j=GROUP, h=HG)
                        nc.vector.reciprocal(rden[:], o[:, :, :, HD]).then_inc(den_done, 1)
                        dve.wait_ge(den_done, n + 1)
                        nc.vector.tensor_tensor(scaled[:], o[:, :, :, 0:HD], rden[:].unsqueeze(3).to_broadcast([P, GROUP, HG, HD]),
                                                ALU.mult).then_inc(o_read, 1)
                        dve.wait_ge(o_read, n + 1)
                        n0 = b * TPB + half * GROUP
                        xs = core.x[:, n0:n0 + GROUP, hg * HG * HD:(hg + 1) * HG * HD]
                        nc.vector.tensor_tensor(xs, xs, scaled[:].rearrange("p j h d -> p j (h d)"), ALU.add).then_inc(out_done, 1)
                        if n == LAST:
                            dve.wait_ge(out_done, n + 1)
                            for i in (0, 1):
                                norm.stats_of(dve, ch, i)
                        if n == LAST + 1:
                            for i in (0, 1):
                                norm.normalise(dve, ch, i)
                            for i in (0, 1):
                                norm.copy(dve, nc.vector.tensor_copy, i)
                            ffn.take(dve)
                            for h in range(0, 2):
                                ffn.add(dve, h)
                        if n == LAST + 2:
                            for h in range(2, 9):
                                ffn.add(dve, h)
                        if n == LAST + 3:
                            for h in range(9, INNER):
                                ffn.add(dve, h)
                        if n == LAST + 4:
                            for i in (0, 1):
                                ffn.finish(dve, i)
                                norm.stats_of(dve, ch, 2 + i)
                            for i in (2, 3):
                                norm.normalise(dve, ch, i)
                            for i in (2, 3):
                                norm.copy(dve, nc.vector.tensor_copy, i)
                        if n == LAST + 5:
                            moe.shift(dve, ch, 0)
                            moe.pick(dve, ch, 0)
                            moe.put(dve, ch, 0)


def attention(core):
    a = core.attention
    a.prepare()
    core.end_stage()
    a.find_shift()
    core.end_stage()
    a.attend()


class SideBanks:

    def __init__(self, psum, banks):
        self.psum, self.banks, self.bank, self.reader, self.uses = psum, banks, {}, [None] * banks, 0

    def take(self, pe, use, read, count):
        n = self.uses % self.banks
        if self.reader[n] is not None:
            pe.wait_ge(*self.reader[n])
        self.bank[use], self.reader[n], self.uses = n, (read, count), self.uses + 1
        return self.psum[:, n, :]

    def of(self, use):
        return self.psum[:, self.bank[use], :]


class Norm:

    def __init__(self, core, name, ctx, xn, xT, side, groups):
        self.core, self.xn, self.xT, self.side, self.groups = core, xn, xT, side, groups
        small = lambda n, shape: core.sb(f"{name}_{n}", shape, ctx=ctx)
        self.stats, self.mv = small("stats", [P, TILES, 6]), small("mv", [P, TILES, 2])
        self.std, self.rstd = small("std", [P, TILES]), small("rstd", [P, TILES])
        sem = lambda n: core.sem(f"{name}_{n}")
        self.aggregated, self.rooted = sem("aggregated"), sem("rooted")
        self.normed, self.turned, self.ready = sem("normed"), sem("turned"), sem("ready")

    def tiles(self, i):
        return slice(self.groups[i] * GROUP, (self.groups[i] + 1) * GROUP)

    def stats_of(self, dve, ch, i):
        nc, tiles = self.core.nc, range(TILES)[self.tiles(i)]
        for n in tiles:
            ch.step(nc.vector.bn_stats(self.stats[:, n, :], self.core.x[:, n, :]))
        ch.wait()
        for n in tiles:
            ins = nc.vector.bn_aggr(self.mv[:, n, :], self.stats[:, n, :])
        ins.then_inc(self.aggregated, 1)

    def root(self, act, i):
        act.wait_ge(self.aggregated, i + 1)
        self.core.nc.scalar.activation(self.std[:, self.tiles(i)], self.mv[:, self.tiles(i), 1], ACT.Sqrt,
                                       bias=self.core.eps[:]).then_inc(self.rooted, 1)

    def normalise(self, dve, ch, i):
        nc = self.core.nc
        dve.wait_ge(self.aggregated, i + 1)
        dve.wait_ge(self.rooted, i + 1)
        ch.step(nc.vector.reciprocal(self.rstd[:, self.tiles(i)], self.std[:, self.tiles(i)]))
        ch.wait()
        if i in self.groups and self.groups.index(self.groups[i]) != i:
            dve.wait_ge(self.turned, i)
        for n in range(TILES)[self.tiles(i)]:
            ins = nc.vector.tensor_scalar(self.xn(n), self.core.x[:, n, :], self.mv[:, n, 0:1], self.rstd[:, n:n + 1],
                                          ALU.subtract, ALU.mult)
        ins.then_inc(self.normed, 1)

    def turn(self, pe, i):
        pe.wait_ge(self.normed, i + 1)
        bank = self.side.take(pe, ("turn", i), self.ready, i + 1)
        for j, n in enumerate(range(TILES)[self.tiles(i)]):
            ins = self.core.nc.tensor.transpose(bank[:, j * P:(j + 1) * P], self.xn(n), self.core.ident[:])
        ins.then_inc(self.turned, 1)

    def copy(self, eng, copy, i):
        eng.wait_ge(self.turned, i + 1)
        g = self.groups[i]
        copy(self.xT[:, g * GT:(g + 1) * GT], self.side.of(("turn", i))).then_inc(self.ready, 1)


class FfnOfBatch:

    ON_ACT = (0, INNER)

    def __init__(self, core, name, ctx, b, norm, first, work):
        self.core, self.b, self.norm, self.first, self.on_act = core, b, norm, first, self.ON_ACT[b]
        self.s, self.acc, self.unit = work[:, 0, :], work[:, 1, :], work[:, 2:6, :]
        sem = lambda n: core.sem(f"{name}_{n}", ctx)
        (self.based, self.s_done, self.s_read, self.relu_done, self.clipped, self.added, self.out_done, self.out_read) = (
            sem(n) for n in ("based", "s_done", "s_read", "relu_done", "clipped", "added", "out_done", "out_read"))

    def base(self, pool):
        core, tiles = self.core, slice(self.b * TPB, (self.b + 1) * TPB)
        pool.wait_ge(self.norm.normed, self.first + 2)
        core.nc.gpsimd.tensor_tensor(core.x[:, tiles, :], core.x[:, tiles, :], core.bout_half[:].unsqueeze(1).to_broadcast([P, TPB, D]), ALU.add)\
            .then_inc(self.based, 1)

    def project(self, pe):
        bank = self.norm.side.take(pe, ("s", self.b), self.s_read, 1)
        pe.wait_ge(self.norm.ready, self.first + 2)
        for half in range(2):
            g = 2 * self.b + half
            ins = self.core.nc.tensor.matmul(bank[M * half:M * half + M, :], self.core.win[:], self.norm.xT[:, g * GT:(g + 1) * GT], start=True, stop=True)
        ins.then_inc(self.s_done, 1)

    def take(self, dve):
        dve.wait_ge(self.s_done, 1)
        self.core.nc.vector.tensor_copy(self.s, self.norm.side.of(("s", self.b))).then_inc(self.s_read, 1)

    def relu(self, act, h):
        core = self.core
        act.wait_ge(self.s_read, 1)
        if h >= 2:
            act.wait_ge(self.added, h - 1)
        core.nc.scalar.activation(self.unit[:, h % 2, :], self.s, ACT.Relu, bias=core.b_pre[:, h:h + 1], scale=core.w1[:, h:h + 1]).then_inc(self.relu_done, 1)

    def add(self, dve, h):
        core, nc = self.core, self.core.nc
        if h < self.on_act:
            unit = self.unit[:, h % 2, :]
            dve.wait_ge(self.relu_done, h + 1)
        else:
            unit = self.unit[:, 2 + h % 2, :]
            dve.wait_ge(self.s_read, 1)
            if h - self.on_act >= 2:
                dve.wait_ge(self.added, h - 1)
            nc.vector.tensor_scalar(unit, self.s, core.w1[:, h:h + 1], core.minus_b[:, h:h + 1], ALU.mult, ALU.max).then_inc(self.clipped, 1)
            dve.wait_ge(self.clipped, h - self.on_act + 1)
        if h == 0:
            ins = nc.vector.tensor_scalar(self.acc, unit, core.w2[:, 0:1], core.b2_all[:, self.b:self.b + 1], ALU.mult, ALU.add)
        else:
            dve.wait_ge(self.added, h)
            ins = nc.vector.scalar_tensor_tensor(self.acc, unit, core.w2[:, h:h + 1], self.acc, ALU.mult, ALU.add)
        ins.then_inc(self.added, 1)

    def output(self, pe, half):
        core = self.core
        bank = self.norm.side.take(pe, ("ffn_out", self.b, half), self.out_read, half + 1)
        pe.wait_ge(self.added, INNER)
        for j in range(GROUP):
            ins = core.nc.tensor.matmul(bank[:, j * D:(j + 1) * D], self.acc[:, j * P:(j + 1) * P], core.wout[:, half, :], start=True, stop=True)
        ins.then_inc(self.out_done, 1)

    def finish(self, dve, half):
        core, n0 = self.core, self.b * TPB + half * GROUP
        dve.wait_ge(self.out_done, half + 1)
        dve.wait_ge(self.based, 1)
        x = core.x[:, n0:n0 + GROUP, :].rearrange("p a d -> p (a d)")
        core.nc.vector.scalar_tensor_tensor(x, self.norm.side.of(("ffn_out", self.b, half)), 0.5, x, ALU.mult, ALU.add).then_inc(self.out_read, 1)
        dve.wait_ge(self.out_read, half + 1)


class Moe:

    PROB, TOKEN, FIRST, ROW = D, D + E_, D + E_ + 1, D + E_ + 2
    NOWHERE = float(16 * T)
    RING = 3

    def __init__(self, core):
        nc, d = core.nc, core.dram
        self.core = core
        self.w1 = core.sb("moe_w1", [D, E_, FF])
        self.w3 = core.sb("moe_w3", [D, E_, FF])
        self.w2 = core.sb("moe_w2", [FC, E_, FCH, D])
        self.gate = core.sb("moe_gate", [D, E_])
        self.iota = core.sb("moe_iota", [P, E_])
        self.token = core.sb("moe_token", [P, TPB])
        self.tri = core.sb("moe_tri", [P, 2, P], BF16)
        per_batch = lambda n, rows, cols: [nc.dram_tensor(f"moe_{n}{i}", (rows, cols), F32).ap() for i in range(2 * B)]
        self.slots, self.rows = per_batch("slots", SLOTS, self.ROW), per_batch("rows", TOPK * T, D)
        self.loads = [("moe_gate", self.gate[:], d["gate"]), ("moe_iota", self.iota[:], d["expert_iota"].to_broadcast([P, E_])),
                      ("moe_token", self.token[:], d["token"]),
                      ("moe_w1", self.w1[:], d["w1"]), ("moe_w3", self.w3[:], d["w3"]), ("moe_w2", self.w2[:], d["w2"])]
        for n, _, _ in self.loads:
            core.loaded[n] = core.sem(f"ld_{n}")
        self.cleared = core.sem("moe_cleared")

    def open_routing(self, ctx, name, rows, xT, norm):
        core = self.core
        self.row_of, self.xT, self.norm = rows, xT, norm
        sb = lambda n, shape, dt=F32: core.sb(f"{name}_{n}", shape, dt, ctx)
        sem = lambda n: core.sem(f"{name}_{n}")
        NT = TPB
        self.e0, self.e1, self.pr = sb("e0", [P, NT, E_]), sb("e1", [P, NT, E_]), sb("pr", [P, NT, E_])
        self.mx, self.den, self.rden = sb("mx", [P, NT]), sb("den", [P, NT]), sb("rden", [P, NT])
        self.top, self.at, self.atf = sb("top", [P, NT, 8]), sb("at", [P, NT, 8], U32), sb("atf", [P, TOPK, NT])
        self.hot, self.tmp = sb("hot", [P, TOPK, NT, E_]), sb("tmp", [P, TOPK, NT, E_])
        self.picked = sb("picked", [P, NT, E_], BF16)
        self.mine, self.place, self.over = (sb(n, [P, TOPK, NT]) for n in ("mine", "place", "over"))
        self.scatter_at = sb("scatter_at", [P, B, TOPK, NT], U32)
        (self.logits_done, self.shifted, self.exped, self.picked_done, self.counted, self.placed, self.routed) = (
            sem(n) for n in ("logits_done", "shifted", "exped", "picked_done", "counted", "placed", "routed"))
        self.scattered = [sem(f"scattered{b}") for b in range(B)]

    def open(self, ctx, name, main):
        core = self.core
        sb = lambda n, shape, dt=F32: core.sb(f"{name}_{n}", shape, dt, ctx)
        sem = lambda n: core.sem(f"{name}_{n}", ctx)
        self.xs, self.xsT = sb("xs", [P, self.RING, 3, self.ROW]), sb("xsT", [D, 2, CAP])
        self.act_h, self.hid = sb("act_h", [FC, 2, CAP]), sb("hid", [FC, 2, FCH, CAP])
        self.y = sb("y", [P, 2, 3, D])
        self.second, self.dest, self.weight = sb("second", [P, 2, 3]), sb("dest", [P, 2, 3], U32), sb("weight", [P, 2, 3])
        self.back = sb("back", [P, TOPK, TPB, D])
        self.ps_t, self.ps_h1, self.ps_h3, self.ps_y = main[:, 0, :], main[:, 1:3, :], main[:, 3:5, :], main[:, 5, :]
        self.tail_clear, self.chain = sem("tail_clear"), sem("chain")
        self.slots_in = [sem(f"slots_in{i}") for i in range(self.RING)]
        self.y_out = [sem(f"y_out{i}") for i in range(2)]
        self.back_in = [sem(f"back_in{i}") for i in range(2)]
        (self.turned, self.t_read, self.h_done, self.silu_done, self.gated, self.y_done, self.y_read, self.sent, self.combined) = (
            sem(n) for n in ("turned", "t_read", "h_done", "silu_done", "gated", "y_done", "y_read", "sent", "combined"))

    UNITS = 2 * B * E_
    FULL = CAP // P
    REST = CAP - FULL * P
    CHUNKS = [(s * P, min(P, CAP - s * P)) for s in range(FULL + 1)]


    def logits(self, pe, r):
        nc, b = self.core.nc, r % B
        bank = self.norm.side.take(pe, ("logits", r), self.shifted, r + 1)
        for j in range(TPB):
            n = b * TPB + j
            ins = nc.tensor.matmul(bank[:, j * E_:(j + 1) * E_], self.xT[:, n * P:(n + 1) * P], self.gate[:], start=True, stop=True)
        ins.then_inc(self.logits_done, 1)

    def counts(self, pe, r):
        pe.wait_ge(self.picked_done, r + 1)
        bank = self.norm.side.take(pe, ("counts", r), self.placed, r + 1)
        for step in range(TPB):
            ins = self.core.nc.tensor.matmul(bank[:, step * E_:TPB * E_], self.tri[:, min(step, 1), :],
                                             self.picked[:, 0:TPB - step, :].rearrange("p j e -> p (j e)"),
                                             start=(step == 0), stop=(step == TPB - 1))
        ins.then_inc(self.counted, 1)

    def shift(self, dve, ch, r):
        nc = self.core.nc
        dve.wait_ge(self.logits_done, r + 1)
        logits = self.norm.side.of(("logits", r))[:, 0:TPB * E_].rearrange("p (j e) -> p j e", e=E_)
        ch.step(nc.vector.reduce_max(self.mx[:], logits, AX_X))
        ch.wait()
        nc.vector.tensor_tensor(self.e0[:], logits, self.mx[:].unsqueeze(2).to_broadcast([P, TPB, E_]), ALU.subtract).then_inc(self.shifted, 1)

    def exp(self, act, r):
        act.wait_ge(self.shifted, r + 1)
        self.core.nc.scalar.activation(self.e1[:], self.e0[:], ACT.Exp).then_inc(self.exped, 1)

    def pick(self, dve, ch, r):
        nc, b = self.core.nc, r % B
        over_e = lambda v: v.unsqueeze(2).to_broadcast([P, TPB, E_])
        tiles = slice(b * TPB, (b + 1) * TPB)

        def then(ins):
            ch.step(ins)
            ch.wait()

        dve.wait_ge(self.exped, r + 1)
        then(nc.vector.reduce_sum(self.den[:], self.e1[:], AX_X))
        then(nc.vector.reciprocal(self.rden[:], self.den[:]))
        then(nc.vector.tensor_tensor(self.pr[:], self.e1[:], over_e(self.rden[:]), ALU.mult))
        for j in range(TPB):
            ch.step(nc.vector.max(self.top[:, j, :], self.pr[:, j, :]))
        ch.wait()
        for j in range(TPB):
            ch.step(nc.vector.max_index(self.at[:, j, :], self.top[:, j, :], self.pr[:, j, :]))
        ch.wait()
        then(nc.vector.tensor_copy(self.atf[:].rearrange("p k j -> p j k"), self.at[:, :, 0:TOPK]))
        for k in range(TOPK):
            ch.step(nc.vector.tensor_tensor(self.hot[:, k, :, :], self.iota[:].unsqueeze(1).to_broadcast([P, TPB, E_]),
                                            over_e(self.atf[:, k, :]), ALU.is_equal))
        ch.wait()
        nc.vector.tensor_tensor(self.picked[:], self.hot[:, 0, :, :], self.hot[:, 1, :, :], ALU.add).then_inc(self.picked_done, 1)
        ch.step(nc.vector.tensor_scalar(self.row_of[:, tiles, self.PROB:self.PROB + E_], self.pr[:], 0.5, None, ALU.mult))
        ch.step(nc.vector.tensor_copy(self.row_of[:, tiles, self.FIRST], self.atf[:, 0, :]))

    def put(self, dve, ch, r):
        nc, b = self.core.nc, r % B

        def then(ins):
            ch.step(ins)
            ch.wait()

        dve.wait_ge(self.counted, r + 1)
        seen = self.norm.side.of(("counts", r))[:, 0:TPB * E_].rearrange("p (j e) -> p j e", e=E_)
        ch.step(nc.vector.tensor_tensor(self.tmp[:, 0, :, :], self.hot[:, 0, :, :], seen, ALU.mult))
        nc.vector.tensor_tensor(self.tmp[:, 1, :, :], self.hot[:, 1, :, :], seen, ALU.mult).then_inc(self.placed, 1)
        ch.wait()
        dve.wait_ge(self.placed, r + 1)
        then(nc.vector.reduce_sum(self.mine[:], self.tmp[:], AX_X))
        ch.step(nc.vector.scalar_tensor_tensor(self.place[:], self.atf[:], float(CAP), self.mine[:], ALU.mult, ALU.add))
        then(nc.vector.tensor_scalar(self.over[:], self.mine[:], float(CAP), float(4 * SLOTS), ALU.is_gt, ALU.mult))
        nc.vector.scalar_tensor_tensor(self.scatter_at[:, b, :, :], self.place[:], -1.0, self.over[:], ALU.add, ALU.add)\
          .then_inc(self.routed, 1)

    def scatter(self, pool, r, first=0, last=TOPK * TPB):
        nc, b = self.core.nc, r % B
        if first == 0:
            pool.wait_ge(self.routed, r + 1)
        for n in range(first, last):
            k, j = n // TPB, n % TPB
            nc.gpsimd.indirect_dma_start(self.slots[r], bass.IndirectOffsetOnAxis(self.scatter_at[:, b, k, j:j + 1], 0),
                                         self.row_of[:, b * TPB + j, :], None, bounds_check=SLOTS - 1, oob_is_err=False)\
              .then_inc(self.scattered[b], 16)


    def load(self, sp, u):
        r, e = u // E_, u % E_
        if e == 0:
            sp.wait_ge(self.scattered[r % B], 16 * TOPK * TPB * (r // B + 1))
        if u == 0:
            sp.wait_ge(self.tail_clear, 1)
        if u >= self.RING:
            sp.wait_ge(self.turned, u - self.RING + 1)
            sp.wait_ge(self.sent, u - self.RING + 1)
        src, r0 = self.slots[r], e * CAP
        sp.dma_start(self.xs[:, u % self.RING, 0:self.FULL, :], src[r0:r0 + self.FULL * P, :].rearrange("(s p) d -> p s d", p=P))\
          .then_inc(self.slots_in[u % self.RING], 16)
        sp.dma_start(self.xs[0:self.REST, u % self.RING, self.FULL, :], src[r0 + self.FULL * P:r0 + CAP, :])\
          .then_inc(self.slots_in[u % self.RING], 16)

    def loaded(self, eng, u):
        eng.wait_ge(self.slots_in[u % self.RING], 32 * (u // self.RING + 1))

    def turn(self, pe, u):
        self.loaded(pe, u)
        if u >= 1:
            pe.wait_ge(self.t_read, u)
        for s, (c0, n) in enumerate(self.CHUNKS):
            ins = self.core.nc.tensor.transpose(self.ps_t[:, c0:c0 + n], self.xs[0:n, u % self.RING, s, 0:D], self.core.ident[0:n, 0:n])
        ins.then_inc(self.turned, 1)

    def take(self, dve, u):
        nc = self.core.nc
        dve.wait_ge(self.turned, u + 1)
        if u >= 2:
            dve.wait_ge(self.h_done, 2 * FCH * (u - 1))
        nc.vector.tensor_copy(self.xsT[:, u % 2, :], self.ps_t[:, 0:CAP]).then_inc(self.t_read, 1)

    def address(self, dve, u):
        nc, e = self.core.nc, u % E_
        self.loaded(dve, u)
        if u >= 2:
            dve.wait_ge(self.y_out[u % 2], 48 * (u // 2))
        row = self.xs[:, u % self.RING, :, :]
        nc.vector.tensor_scalar(self.second[:, u % 2, :], row[:, :, self.FIRST], float(e), float(T), ALU.not_equal, ALU.mult).then_inc(self.chain, 1)
        nc.vector.tensor_copy(self.weight[:, u % 2, :], row[:, :, self.PROB + e]).then_inc(self.chain, 1)
        dve.wait_ge(self.chain, 2 * u + 2)
        nc.vector.tensor_tensor(self.dest[:, u % 2, :], self.second[:, u % 2, :], row[:, :, self.TOKEN], ALU.add).then_inc(self.sent, 1)

    def hidden(self, pe, u):
        e = u % E_
        pe.wait_ge(self.t_read, u + 1)
        for c in range(FCH):
            w = u * FCH + c
            for ps, wt in ((self.ps_h1, self.w1), (self.ps_h3, self.w3)):
                if w >= 2:
                    pe.wait_ge(self.gated, w - 1)
                self.core.nc.tensor.matmul(ps[0:FC, w % 2, 0:CAP], wt[:, e, c * FC:(c + 1) * FC], self.xsT[:, u % 2, :],
                                           start=True, stop=True).then_inc(self.h_done, 1)

    def silu(self, act, u, chunks=range(FCH)):
        for c in chunks:
            w = u * FCH + c
            act.wait_ge(self.h_done, 2 * w + 1)
            if w >= 2:
                act.wait_ge(self.gated, w - 1)
            self.core.nc.scalar.activation(self.act_h[:, w % 2, :], self.ps_h1[0:FC, w % 2, 0:CAP], ACT.Silu).then_inc(self.silu_done, 1)

    def gating(self, dve, u, chunks=range(FCH)):
        for c in chunks:
            w = u * FCH + c
            dve.wait_ge(self.silu_done, w + 1)
            dve.wait_ge(self.h_done, 2 * (w + 1))
            if u >= 2 and c == 0:
                dve.wait_ge(self.y_done, u - 1)
            self.core.nc.vector.tensor_tensor(self.hid[:, u % 2, c, :], self.act_h[:, w % 2, :], self.ps_h3[0:FC, w % 2, 0:CAP], ALU.mult)\
                .then_inc(self.gated, 1)

    def results(self, pe, u):
        pe.wait_ge(self.gated, FCH * (u + 1))
        if u >= 1:
            pe.wait_ge(self.y_read, 3 * u)
        for s, (c0, n) in enumerate(self.CHUNKS):
            for c in range(FCH):
                ins = self.core.nc.tensor.matmul(self.ps_y[0:n, s * D:(s + 1) * D], self.hid[:, u % 2, c, c0:c0 + n], self.w2[:, u % E_, c, :],
                                                 start=(c == 0), stop=(c == FCH - 1))
        ins.then_inc(self.y_done, 1)

    def weigh(self, act, u):
        act.wait_ge(self.y_done, u + 1)
        act.wait_ge(self.sent, u + 1)
        for s, (c0, n) in enumerate(self.CHUNKS):
            self.core.nc.scalar.activation(self.y[0:n, u % 2, s, :], self.ps_y[0:n, s * D:(s + 1) * D], ACT.Copy,
                                           scale=self.weight[0:n, u % 2, s:s + 1]).then_inc(self.y_read, 1)

    def send(self, pool, u):
        pool.wait_ge(self.y_read, 3 * (u + 1))
        pool.wait_ge(self.sent, u + 1)
        for s, (c0, n) in enumerate(self.CHUNKS):
            self.core.nc.gpsimd.indirect_dma_start(self.rows[u // E_], bass.IndirectOffsetOnAxis(self.dest[0:n, u % 2, s:s + 1], 0),
                                                   self.y[0:n, u % 2, s, :], None, bounds_check=TOPK * T - 1, oob_is_err=False)\
                .then_inc(self.y_out[u % 2], 16)

    def fetch(self, sp, r):
        for i in range(2):
            sp.wait_ge(self.y_out[i], 48 * E_ // 2 * (r + 1))
        if r >= 1:
            sp.wait_ge(self.combined, 2 * r)
        src = self.rows[r].rearrange("(k j p) d -> p k j d", k=TOPK, p=P)
        for half in range(2):
            tiles = slice(half * GROUP, (half + 1) * GROUP)
            for k in range(TOPK):
                sp.dma_start(self.back[:, k, tiles, :], src[:, k, tiles, :]).then_inc(self.back_in[half], 16)

    def combine(self, dve, ch, r, half):
        nc, n0 = self.core.nc, r % B * TPB + half * GROUP
        dve.wait_ge(self.back_in[half], 16 * TOPK * (r + 1))
        x, back = self.core.x[:, n0:n0 + GROUP, :], self.back[:, :, half * GROUP:(half + 1) * GROUP, :]
        ch.step(nc.vector.tensor_tensor(x, x, back[:, 0, :, :], ALU.add))
        ch.wait()
        nc.vector.tensor_tensor(x, x, back[:, 1, :, :], ALU.add).then_inc(self.combined, 1)
        dve.wait_ge(self.combined, 2 * r + half + 1)


class Mamba:

    UNITS = [(di, b) for b in range(B) for di in range(2)]
    NC = TPB
    N = len(UNITS) * NC
    PIECES = 6
    LOG_TERMS = 8
    PARTS_OUT = [range(0, 3), range(3, 6), range(6, 8)]
    PIECES_AT = [(0,), (1,), (), (2,), (3,), (), (4,), (5,)]
    TAPS_AT = [(), ((0, 1), (0, 2)), ((0, 3), (1, 1), (1, 2)), ((1, 3),), ((2, 1), (2, 2), (2, 3)), ((3, 1), (3, 2), (3, 3)), (), ()]

    def __init__(self, core):
        d = core.dram
        self.core = core
        sb = core.sb
        self.w_xbc, self.w_z, self.w_dt = sb("mb_w_xbc", [D, 2, 4, P]), sb("mb_w_z", [D, 2, 2, P]), sb("mb_w_dt", [D, 2 * NH])
        self.taps, self.conv_b = sb("mb_taps", [P, 2, 4, TAPS]), sb("mb_conv_b", [P, 2, 4])
        self.skip, self.norm_w, self.wo = sb("mb_skip", [P, 2, 2]), sb("mb_norm_w", [P, 2, 2]), sb("mb_wo", [P, 2, 2, D])
        self.dt_bias, self.a_log = sb("mb_dt_bias", [P, 2 * NH]), sb("mb_a_log", [P, 2 * NH])
        self.loads = [("mb_w_xbc", self.w_xbc[:], d["mb_w_xbc"]), ("mb_w_z", self.w_z[:], d["mb_w_z"]), ("mb_w_dt", self.w_dt[:], d["mb_w_dt"]),
                      ("mb_taps", self.taps[:], d["mb_taps"]), ("mb_conv_b", self.conv_b[:], d["mb_conv_b"]),
                      ("mb_skip", self.skip[:], d["mb_skip"]), ("mb_norm_w", self.norm_w[:], d["mb_norm_w"]), ("mb_wo", self.wo[:], d["mb_wo"]),
                      ("mb_dt_bias", self.dt_bias[:], d["mb_dt_bias"].to_broadcast([P, 2 * NH])),
                      ("mb_a_log", self.a_log[:], d["mb_a_log"].to_broadcast([P, 2 * NH]))]
        for n, _, _ in self.loads:
            core.loaded[n] = core.sem(f"ld_{n}")

    def open(self, ctx, name, xT, side, main):
        core = self.core
        self.xT, self.side = xT, side
        sb = lambda n, shape, dt=F32: core.sb(f"{name}_{n}", shape, dt, ctx)
        sem = lambda n: core.sem(f"{name}_{n}", ctx)
        XP = T + 2 * (TAPS - 1)
        self.padded = sb("padded", [P, 2, XP])
        self.act_t = sb("act", [P, 2, 4, T])
        self.z = sb("z", [P, 2, 2, T])
        self.strict, self.incl, self.ones = sb("strict", [P, 2, P]), sb("incl", [P, 2, P]), sb("ones", [P, P])
        small = lambda n: sb(n, [P, TILES, 2 * NH])
        self.dt, self.a, self.whole = small("dt"), small("a"), small("whole")
        self.v, self.ab, self.ex, self.sq, self.poly = (sb(n, [P, TPB, 2 * NH]) for n in ("v", "ab", "ex", "sq", "poly"))
        self.a_exp, self.to_end = sb("a_exp", [P, 2 * NH]), sb("to_end", [P, 2, TILES, NH])
        self.cut, self.e_seg, self.mt = (sb(n, [P, 2, NH, P]) for n in ("cut", "e_seg", "mt"))
        self.e_cum, self.gm, self.bs = sb("e_cum", [P, 2, 2, P]), sb("gm", [P, 2, P]), sb("bs", [P, 2, 2 * P])
        self.xdt, self.xw, self.h, self.h_dec = sb("xdt", [P, 2, DIN]), sb("xw", [P, 2, DIN]), sb("h", [P, 2, DIN]), sb("h_dec", [P, DIN])
        self.y_in, self.y_old, self.y2 = sb("y_in", [P, 2, 2, P]), sb("y_old", [P, 2, 2, P]), sb("y2", [P, 2, 2, P])
        self.var, self.std, self.rstd = (sb(n, [P, self.NC]) for n in ("var", "std", "rstd"))
        self.ps_seg, self.ps_cb, self.ps_x, self.ps_y, self.ps_st, self.ps_o = (main[:, i, :] for i in range(6))
        (self.masks, self.pads, self.dt_done, self.dt_in, self.dt_exp, self.a_exped, self.a_done, self.sums_done, self.decays, self.norm_done) = (
            sem(n) for n in ("masks", "pads", "dt_done", "dt_in", "dt_exp", "a_exped", "a_done", "sums_done", "decays", "norm_done"))
        self.proj_done, self.proj_read, self.tapped, self.conv_done, self.act_ready, self.z_ready = (
            sem(n) for n in ("proj_done", "proj_read", "tapped", "conv_done", "act_ready", "z_ready"))
        (self.cut_done, self.seg_done, self.cb_done, self.x_done, self.y_done, self.st_done, self.seg_exp, self.cb_read, self.x_read) = (
            sem(n) for n in ("cut_done", "seg_done", "cb_done", "x_done", "y_done", "st_done", "seg_exp", "cb_read", "x_read"))
        (self.gm_done, self.mt_done, self.xw_done, self.h_decayed, self.h_ready, self.y_read, self.y_sum, self.gate_done) = (
            sem(n) for n in ("gm_done", "mt_done", "xw_done", "h_decayed", "h_ready", "y_read", "y_sum", "gate_done"))
        (self.squared, self.ss_done, self.ss_read, self.std_done, self.rms_done, self.out_done, self.out_read) = (
            sem(n) for n in ("squared", "ss_done", "ss_read", "std_done", "rms_done", "out_done", "out_read"))

    def at(self, g):
        u, i = g // self.NC, g % self.NC
        di, b = self.UNITS[u]
        j = i if di == 0 else self.NC - 1 - i
        return u, di, b, i, b * TPB + j, slice(j * P, (j + 1) * P)

    def carried(self, g):
        return (g // self.NC) * (self.NC - 1) + g % self.NC

    def passed(self, g):
        return (g // self.NC) * (self.NC - 1) + min(g % self.NC + 1, self.NC - 1)

    def passes_on(self, g):
        return g % self.NC < self.NC - 1


    def make_masks(self, pool):
        nc = self.core.nc
        for m in (self.ones, self.strict, self.incl):
            nc.gpsimd.memset(m[:], 1.0).then_inc(self.masks, 1)
        nc.gpsimd.memset(self.padded[:], 0.0).then_inc(self.pads, 1)
        pool.wait_ge(self.masks, 3)
        for m, di, op, sign in ((self.strict, 0, ALU.is_gt, 1), (self.strict, 1, ALU.is_gt, -1), (self.incl, 0, ALU.is_ge, -1), (self.incl, 1, ALU.is_ge, 1)):
            nc.gpsimd.affine_select(out=m[:, di, :], in_=m[:, di, :], compare_op=op, fill=0.0, base=0,
                                    pattern=[[-sign, P]], channel_multiplier=sign).then_inc(self.masks, 1)
        pool.wait_ge(self.masks, 7)

    def steps(self, pe, b):
        bank = self.side.take(pe, ("dt", b), self.dt_in, b + 1)
        for j in range(TPB):
            n = b * TPB + j
            ins = self.core.nc.tensor.matmul(bank[:, j * 2 * NH:(j + 1) * 2 * NH], self.xT[:, n * P:(n + 1) * P], self.w_dt[:], start=True, stop=True)
        ins.then_inc(self.dt_done, 1)

    def sums(self, pe, b):
        nc, tiles = self.core.nc, slice(b * TPB, (b + 1) * TPB)
        pe.wait_ge(self.a_done, b + 1)
        pe.wait_ge(self.masks, 7)
        bank = self.side.take(pe, ("sums", b), self.decays, 3 * (b + 1))
        n = TPB * NH
        for di in range(2):
            nc.tensor.matmul(bank[:, di * n:(di + 1) * n], self.strict[:, di, :], self.a[:, tiles, di * NH:(di + 1) * NH], start=True, stop=True)
        nc.tensor.matmul(bank[:, 2 * n:4 * n], self.ones[:], self.a[:, tiles, :], start=True, stop=True).then_inc(self.sums_done, 1)

    def exp_a(self, act):
        self.core.landed(act, "mb_a_log", "mb_conv_b")
        self.core.nc.scalar.activation(self.a_exp[:], self.a_log[:], ACT.Exp).then_inc(self.a_exped, 1)

    def exp_dt(self, act, b):
        act.wait_ge(self.dt_in, b + 1)
        self.core.nc.scalar.activation(self.ex[:], self.ab[:], ACT.Exp, scale=-1.0).then_inc(self.dt_exp, 1)

    def exp_sums(self, act, b):
        nc, tiles, n = self.core.nc, slice(b * TPB, (b + 1) * TPB), TPB * NH
        act.wait_ge(self.sums_done, b + 1)
        bank = self.side.of(("sums", b))
        for di in range(2):
            nc.scalar.activation(self.to_end[:, di, tiles, :], bank[:, di * n:(di + 1) * n].rearrange("p (j h) -> p j h", h=NH), ACT.Exp)\
              .then_inc(self.decays, 1)
        nc.scalar.activation(self.whole[:, tiles, :], bank[:, 2 * n:4 * n].rearrange("p (j h) -> p j h", h=2 * NH), ACT.Exp).then_inc(self.decays, 1)

    def weigh_out(self, dve):
        self.core.landed(dve, "mb_norm_w", "mb_wo", "mb_dt_bias", "mb_taps", "mb_skip")
        for di in range(2):
            for c in range(2):
                ins = self.core.nc.vector.tensor_scalar(self.wo[:, di, c, :], self.wo[:, di, c, :], self.norm_w[:, di, c:c + 1], None, ALU.mult)
        ins.then_inc(self.norm_done, 1)

    def step_sizes(self, dve, ch, b):
        nc, tiles, every = self.core.nc, slice(b * TPB, (b + 1) * TPB), [P, TPB, 2 * NH]
        v, ab, ex, sq, poly = self.v, self.ab, self.ex, self.sq, self.poly

        def then(ins):
            ch.step(ins)
            ch.wait()

        dve.wait_ge(self.dt_done, b + 1)
        then(nc.vector.tensor_tensor(v[:], self.side.of(("dt", b))[:, 0:TPB * 2 * NH].rearrange("p (j h) -> p j h", h=2 * NH),
                                     self.dt_bias[:].unsqueeze(1).to_broadcast(every), ALU.add))
        nc.vector.scalar_tensor_tensor(ab[:], v[:], -1.0, v[:], ALU.mult, ALU.max).then_inc(self.dt_in, 1)
        dve.wait_ge(self.dt_exp, b + 1)
        then(nc.vector.tensor_scalar(poly[:], ex[:], 2.0, None, ALU.add))
        then(nc.vector.reciprocal(poly[:], poly[:]))
        then(nc.vector.tensor_tensor(ex[:], ex[:], poly[:], ALU.mult))
        then(nc.vector.tensor_tensor(sq[:], ex[:], ex[:], ALU.mult))
        then(nc.vector.tensor_scalar(poly[:], sq[:], 1.0 / (2 * self.LOG_TERMS + 1), None, ALU.mult))
        for k in range(self.LOG_TERMS - 1, 0, -1):
            then(nc.vector.scalar_tensor_tensor(poly[:], poly[:], 1.0 / (2 * k + 1), sq[:], ALU.add, ALU.mult))
        then(nc.vector.scalar_tensor_tensor(poly[:], poly[:], 1.0, ex[:], ALU.add, ALU.mult))
        then(nc.vector.tensor_scalar(v[:], v[:], 0.0, None, ALU.max))
        then(nc.vector.scalar_tensor_tensor(self.dt[:, tiles, :], poly[:], 2.0, v[:], ALU.mult, ALU.add))
        dve.wait_ge(self.a_exped, 1)
        nc.vector.scalar_tensor_tensor(self.a[:, tiles, :], self.dt[:, tiles, :], -1.0, self.a_exp[:].unsqueeze(1).to_broadcast(every), ALU.mult, ALU.mult)\
          .then_inc(self.a_done, 1)


    def project(self, pe, u, c):
        di, b = self.UNITS[u]
        weight = self.w_xbc[:, di, c, :] if c < 4 else self.w_z[:, di, c - 4, :]
        for half in range(2):
            w = (u * self.PIECES + c) * 2 + half
            bank = self.side.take(pe, ("proj", w), self.proj_read, w + 1)
            t0 = b * T + half * BANK
            self.core.nc.tensor.matmul(bank[:], weight, self.xT[:, t0:t0 + BANK], start=True, stop=True).then_inc(self.proj_done, 1)

    def take(self, act, u, c):
        if c < 4:
            if u >= 1 or c >= 2:
                act.wait_ge(self.conv_done, 4 * u + c - 1)
        elif u >= 2:
            act.wait_ge(self.out_done, len(self.PARTS_OUT) * (u - 1))
        for half in range(2):
            w = (u * self.PIECES + c) * 2 + half
            act.wait_ge(self.proj_done, w + 1)
            t0 = half * BANK
            dst = self.padded[:, c % 2, TAPS - 1 + t0:TAPS - 1 + t0 + BANK] if c < 4 else self.z[:, u % 2, c - 4, t0:t0 + BANK]
            self.core.nc.scalar.copy(dst, self.side.of(("proj", w))).then_inc(self.proj_read, 1)

    def window(self, u, c, k):
        di, b = self.UNITS[u]
        t0 = k if di == 0 else 2 * (TAPS - 1) - k
        return self.padded[:, c % 2, t0:t0 + T], self.taps[:, di, c, k:k + 1]

    def first_tap(self, act, u, c):
        src, tap = self.window(u, c, 0)
        act.wait_ge(self.proj_read, (u * self.PIECES + c) * 2 + 2)
        if u >= 2:
            act.wait_ge(self.y_read, self.NC * (u - 1))
        self.core.nc.scalar.activation(self.act_t[:, u % 2, c, :], src, ACT.Copy, scale=tap).then_inc(self.tapped, 1)

    def convolve(self, dve, ch, u, c, k):
        (src, tap), out = self.window(u, c, k), self.act_t[:, u % 2, c, :]
        if k == 1:
            dve.wait_ge(self.tapped, 4 * u + c + 1)
        else:
            ch.wait()
        ins = self.core.nc.vector.scalar_tensor_tensor(out, src, tap, out, ALU.mult, ALU.add)
        ch.step(ins) if k < TAPS - 1 else ins.then_inc(self.conv_done, 1)

    def silu_rows(self, act, u):
        di, b = self.UNITS[u]
        for c in range(4):
            act.wait_ge(self.conv_done, 4 * u + c + 1)
            self.core.nc.scalar.activation(self.act_t[:, u % 2, c, :], self.act_t[:, u % 2, c, :], ACT.Silu, bias=self.conv_b[:, di, c:c + 1])\
                .then_inc(self.act_ready, 1)

    def silu_z(self, act, u):
        act.wait_ge(self.proj_read, (u + 1) * self.PIECES * 2)
        for c in range(2):
            self.core.nc.scalar.activation(self.z[:, u % 2, c, :], self.z[:, u % 2, c, :], ACT.Silu).then_inc(self.z_ready, 1)


    def cut_a(self, pool, g):
        u, di, b, i, n, cols = self.at(g)
        pool.wait_ge(self.a_done, b + 1)
        if g >= 2:
            pool.wait_ge(self.seg_done, g - 1)
        self.core.nc.gpsimd.tensor_tensor(self.cut[:, g % 2, :, :], self.strict[:, di, :].unsqueeze(1).to_broadcast([P, NH, P]),
                                          self.a[:, n, di * NH:(di + 1) * NH].unsqueeze(2).to_broadcast([P, NH, P]), ALU.mult)\
            .then_inc(self.cut_done, 1)

    def before(self, pe, g):
        nc = self.core.nc
        u, di, b, i, n, cols = self.at(g)
        act = self.act_t[:, u % 2, :, :]
        pe.wait_ge(self.act_ready, 4 * (u + 1))
        pe.wait_ge(self.cut_done, g + 1)
        if g >= 1:
            pe.wait_ge(self.seg_exp, g)
        for hh in range(NH):
            ins = nc.tensor.matmul(self.ps_seg[:, hh * P:(hh + 1) * P], self.cut[:, g % 2, hh, :], self.incl[:, di, :], start=True, stop=True)
        ins.then_inc(self.seg_done, 1)
        if g >= 1:
            pe.wait_ge(self.x_read, g)
        for c in range(2):
            ins = nc.tensor.transpose(self.ps_x[:, c * P:(c + 1) * P], act[:, c, cols], self.core.ident[:])
        ins.then_inc(self.x_done, 1)
        if g >= 1:
            pe.wait_ge(self.cb_read, g)
        if i:
            for hh in range(NH):
                nc.tensor.matmul(self.ps_cb[HP * (hh % 2):HP * (hh % 2) + HP, hh // 2 * P:hh // 2 * P + P],
                                 self.a[:, n, di * NH + hh:di * NH + hh + 1].to_broadcast([P, HP]), self.incl[:, di, :], start=True, stop=True)
        nc.tensor.transpose(self.ps_cb[:, 2 * P:3 * P], act[:, 2, cols], self.core.ident[:])
        nc.tensor.matmul(self.ps_cb[:, 3 * P:4 * P], act[:, 2, cols], act[:, 3, cols], start=True, stop=True).then_inc(self.cb_done, 1)

    def exps(self, act, g):
        nc = self.core.nc
        u, di, b, i, n, cols = self.at(g)
        act.wait_ge(self.seg_done, g + 1)
        if g >= 2:
            act.wait_ge(self.mt_done, g - 1)
        nc.scalar.activation(self.e_seg[:, g % 2, :, :], self.ps_seg.rearrange("p (h t) -> p h t", h=NH), ACT.Exp).then_inc(self.seg_exp, 1)
        act.wait_ge(self.cb_done, g + 1)
        if g >= 2:
            act.wait_ge(self.y_read, g - 1)
            act.wait_ge(self.st_done, self.passed(g - 2))
            act.wait_ge(self.gm_done, g - 1)
        if i:
            nc.scalar.activation(self.e_cum[:, g % 2, :, :], self.ps_cb[:, 0:2 * P].rearrange("p (c t) -> p c t", c=2), ACT.Exp)
        nc.scalar.copy(self.bs[:, g % 2, :], self.ps_cb[:, 2 * P:4 * P]).then_inc(self.cb_read, 1)

    def by_head(self, ap):
        return ap.rearrange("p (h c) -> p h c", h=NH)

    def heads(self, ap):
        return ap.unsqueeze(2).to_broadcast([P, NH, HP])

    def front(self, dve, g):
        nc = self.core.nc
        u, di, b, i, n, cols = self.at(g)
        dve.wait_ge(self.x_done, g + 1)
        if g >= 2:
            dve.wait_ge(self.y_done, g - 1)
            if self.passes_on(g - 2):
                dve.wait_ge(self.xw_done, self.passed(g - 2))
        nc.vector.tensor_tensor(self.by_head(self.xdt[:, g % 2, :]), self.by_head(self.ps_x[:, 0:DIN]), self.heads(self.dt[:, n, di * NH:(di + 1) * NH]), ALU.mult)\
          .then_inc(self.x_read, 1)
        dve.wait_ge(self.cb_read, g + 1)
        if g >= 2:
            dve.wait_ge(self.mt_done, g - 1)
        nc.vector.tensor_tensor(self.gm[:, g % 2, :], self.bs[:, g % 2, P:2 * P], self.incl[:, di, :], ALU.mult).then_inc(self.gm_done, 1)
        dve.wait_ge(self.seg_exp, g + 1)
        dve.wait_ge(self.gm_done, g + 1)
        nc.vector.tensor_tensor(self.mt[:, g % 2, :, :], self.e_seg[:, g % 2, :, :], self.gm[:, g % 2, :].unsqueeze(1).to_broadcast([P, NH, P]),
                                ALU.mult).then_inc(self.mt_done, 1)

    def to_state(self, pool, g):
        u, di, b, i, n, cols = self.at(g)
        if not self.passes_on(g):
            return
        pool.wait_ge(self.x_read, g + 1)
        pool.wait_ge(self.decays, 3 * (b + 1))
        if self.carried(g) >= 2:
            pool.wait_ge(self.st_done, self.carried(g) - 1)
        self.core.nc.gpsimd.tensor_tensor(self.by_head(self.xw[:, g % 2, :]), self.by_head(self.xdt[:, g % 2, :]), self.heads(self.to_end[:, di, n, :]), ALU.mult)\
            .then_inc(self.xw_done, 1)

    def state(self, pe, g):
        if not self.passes_on(g):
            return
        n = self.carried(g)
        pe.wait_ge(self.cb_read, g + 1)
        pe.wait_ge(self.xw_done, n + 1)
        if n >= 1:
            pe.wait_ge(self.h_ready, n)
        self.core.nc.tensor.matmul(self.ps_st[:, 0:DIN], self.bs[:, g % 2, 0:P], self.xw[:, g % 2, :], start=True, stop=True).then_inc(self.st_done, 1)

    def decay(self, pool, g):
        u, di, b, i, n, cols = self.at(g)
        if i == 0 or not self.passes_on(g):
            return
        pool.wait_ge(self.h_ready, self.carried(g))
        self.core.nc.gpsimd.tensor_tensor(self.by_head(self.h_dec[:]), self.by_head(self.h[:, (g - 1) % 2, :]),
                                          self.heads(self.whole[:, n, di * NH:(di + 1) * NH]), ALU.mult).then_inc(self.h_decayed, 1)

    def pass_state(self, dve, g):
        u, di, b, i, n, cols = self.at(g)
        if not self.passes_on(g):
            return
        if g >= 1:
            dve.wait_ge(self.y_done, g)
        dve.wait_ge(self.st_done, self.carried(g) + 1)
        if i == 0:
            self.core.nc.vector.tensor_copy(self.h[:, g % 2, :], self.ps_st[:, 0:DIN]).then_inc(self.h_ready, 1)
            return
        dve.wait_ge(self.h_decayed, u * (self.NC - 2) + i)
        self.core.nc.vector.tensor_tensor(self.h[:, g % 2, :], self.h_dec[:], self.ps_st[:, 0:DIN], ALU.add).then_inc(self.h_ready, 1)

    def outputs(self, pe, g):
        nc = self.core.nc
        u, di, b, i, n, cols = self.at(g)
        if g >= 1:
            pe.wait_ge(self.y_read, g)
        if i:
            pe.wait_ge(self.h_ready, self.carried(g))
            for c in range(2):
                nc.tensor.matmul(self.ps_y[:, (2 + c) * P:(3 + c) * P], self.h[:, (g - 1) % 2, c * P:(c + 1) * P], self.act_t[:, u % 2, 3, cols],
                                 start=True, stop=True)
        pe.wait_ge(self.mt_done, g + 1)
        pe.wait_ge(self.x_read, g + 1)
        for hh in range(NH):
            out = self.ps_y[HP * (hh % 2):HP * (hh % 2) + HP, hh // 2 * P:hh // 2 * P + P]
            ins = nc.tensor.matmul(out, self.xdt[:, g % 2, hh * HP:(hh + 1) * HP], self.mt[:, g % 2, hh, :], start=True, stop=True)
        ins.then_inc(self.y_done, 1)

    def back(self, dve, g):
        nc = self.core.nc
        u, di, b, i, n, cols = self.at(g)
        dve.wait_ge(self.y_done, g + 1)
        if g >= 2:
            dve.wait_ge(self.gate_done, g - 1)
        if i:
            dve.wait_ge(self.cb_read, g + 1)
            nc.vector.tensor_tensor(self.y_old[:, g % 2, :, :], self.e_cum[:, g % 2, :, :], self.ps_y[:, 2 * P:4 * P].rearrange("p (c t) -> p c t", c=2), ALU.mult)
        for c in range(2):
            ins = nc.vector.scalar_tensor_tensor(self.y_in[:, g % 2, c, :], self.act_t[:, u % 2, c, cols], self.skip[:, di, c:c + 1], self.ps_y[:, c * P:(c + 1) * P],
                                                 ALU.mult, ALU.add)
        ins.then_inc(self.y_read, 1)

    def gate(self, eng, ops, g):
        u, di, b, i, n, cols = self.at(g)
        eng.wait_ge(self.y_read, g + 1)
        eng.wait_ge(self.z_ready, 2 * (u + 1))
        if i:
            ops.tensor_tensor(self.y_in[:, g % 2, :, :], self.y_in[:, g % 2, :, :], self.y_old[:, g % 2, :, :], ALU.add).then_inc(self.y_sum, 1)
            eng.wait_ge(self.y_sum, self.carried(g))
        ops.tensor_tensor(self.z[:, u % 2, :, cols], self.y_in[:, g % 2, :, :], self.z[:, u % 2, :, cols], ALU.mult).then_inc(self.gate_done, 1)


    def square(self, act, g):
        u, di, b, i, n, cols = self.at(g)
        act.wait_ge(self.gate_done, g + 1)
        if g >= 2:
            act.wait_ge(self.ss_done, g - 1)
        self.core.nc.scalar.activation(self.y2[:, g % 2, :, :], self.z[:, u % 2, :, cols], ACT.Square).then_inc(self.squared, 1)

    def squares(self, pe, g, parts):
        u, di, b, i, n, cols = self.at(g)
        pe.wait_ge(self.squared, g + 1)
        if parts:
            pe.wait_ge(self.out_read, parts)
        if i == 0 and u >= 1:
            pe.wait_ge(self.ss_read, u)
        col = 3 * D + n % TPB
        for c in range(2):
            ins = self.core.nc.tensor.matmul(self.ps_o[:, col:col + 1], self.y2[:, g % 2, c, :], self.ones[:, 0:1], start=(c == 0), stop=(c == 1))
        ins.then_inc(self.ss_done, 1)

    def variance(self, dve, u):
        dve.wait_ge(self.ss_done, self.NC * (u + 1))
        if u >= 1:
            dve.wait_ge(self.std_done, u)
        self.core.nc.vector.tensor_scalar(self.var[:], self.ps_o[:, 3 * D:3 * D + self.NC], 1.0 / DIN, None, ALU.mult).then_inc(self.ss_read, 1)

    def deviation(self, act, u):
        act.wait_ge(self.ss_read, u + 1)
        if u >= 1:
            act.wait_ge(self.rms_done, u)
        self.core.nc.scalar.activation(self.std[:], self.var[:], ACT.Sqrt, bias=self.core.eps[:]).then_inc(self.std_done, 1)

    def output(self, pe, u, part):
        parts = len(self.PARTS_OUT)
        pe.wait_ge(self.gate_done, self.NC * (u + 1))
        pe.wait_ge(self.ss_read, u + 1)
        if u or part:
            pe.wait_ge(self.out_read, parts * u + part)
        for q, j in enumerate(self.PARTS_OUT[part]):
            for c in range(2):
                ins = self.core.nc.tensor.matmul(self.ps_o[:, q * D:(q + 1) * D], self.z[:, u % 2, c, j * P:(j + 1) * P],
                                                 self.wo[:, self.UNITS[u][0], c, :], start=(c == 0), stop=(c == 1))
        ins.then_inc(self.out_done, 1)

    def add(self, dve, ch, u, part):
        nc, core, (di, b) = self.core.nc, self.core, self.UNITS[u]
        if part == 0:
            dve.wait_ge(self.std_done, u + 1)
            nc.vector.reciprocal(self.rstd[:], self.std[:]).then_inc(self.rms_done, 1)
            dve.wait_ge(self.rms_done, u + 1)
            ch.step(nc.vector.tensor_scalar(self.rstd[:], self.rstd[:], 0.5, None, ALU.mult))
            ch.wait()
        dve.wait_ge(self.out_done, len(self.PARTS_OUT) * u + part + 1)
        for q, j in enumerate(self.PARTS_OUT[part]):
            n = b * TPB + j
            ins = nc.vector.scalar_tensor_tensor(core.x[:, n, :], self.ps_o[:, q * D:(q + 1) * D], self.rstd[:, j:j + 1], core.x[:, n, :], ALU.mult, ALU.add)
        ins.then_inc(self.out_read, 1)
        if part == len(self.PARTS_OUT) - 1:
            dve.wait_ge(self.out_read, len(self.PARTS_OUT) * (u + 1))


def moe_mamba_moe(core):
    nc, moe, mamba = core.nc, core.moe, core.mamba
    NC, N, UNITS = mamba.NC, mamba.N, len(mamba.UNITS)
    HALF = B * E_
    with ExitStack() as ctx:
        norm = core.norm
        norm.side = SideBanks(ctx.enter_context(nc.psum_tensor("ps_side", [P, 2, BANK], F32)), 2)
        main = ctx.enter_context(nc.psum_tensor("ps_main", [P, 6, BANK], F32))
        moe.open(ctx, "moe", main)
        mamba.open(ctx, "mb", norm.xT, norm.side, main)
        ffn = FfnOfBatch(core, "ffn_b1", ctx, 1, norm, 4, mamba.act_t[:, 1, :, :].rearrange("p c (h t) -> p (c h) t", h=2)[:, 0:6, :])
        chain = core.sem("dve_chain", ctx)
        PARTS_OUT = len(mamba.PARTS_OUT)
        share = lambda units, c: units[len(units) * c // FCH:len(units) * (c + 1) // FCH]
        UNITS_AT = [range(0, 4), range(4, 10), range(10, INNER)]

        with nc.Block() as block:
            @block.tensor
            def _(pe):
                def experts(u):
                    if u == E_:
                        moe.results(pe, u - 1)
                        moe.turn(pe, u)
                    if u + 1 < HALF and u + 1 != E_:
                        moe.turn(pe, u + 1)
                    moe.hidden(pe, u)
                    if u and u != E_:
                        moe.results(pe, u - 1)

                core.landed(pe, "moe_gate", "ident", "moe_w1", "moe_w3", "moe_w2", "mb_w_dt", "mb_w_xbc", "mb_w_z")
                moe.turn(pe, 0)
                for i in (4, 5):
                    norm.turn(pe, i)
                ffn.project(pe)
                for u in range(HALF):
                    if u == 4:
                        for i in (6, 7):
                            norm.turn(pe, i)
                    if u == 6:
                        moe.counts(pe, 1)
                    experts(u)
                    if u == 2:
                        for half in range(2):
                            ffn.output(pe, half)
                    if u == 4:
                        pe.wait_ge(norm.ready, 8)
                        moe.logits(pe, 1)
                    if u == 12:
                        norm.turn(pe, 8)
                        norm.turn(pe, 9)
                    if u == 13:
                        pe.wait_ge(norm.ready, 10)
                        mamba.steps(pe, 0)
                        mamba.project(pe, 0, 0)
                    if u == 15:
                        mamba.sums(pe, 0)
                    if u >= 13:
                        mamba.project(pe, 0, u - 12)
                moe.results(pe, HALF - 1)
                for c in (4, 5):
                    mamba.project(pe, 0, c)
                pe.wait_ge(moe.y_read, 3 * HALF)
                pe.wait_ge(mamba.norm_done, 1)
                mamba.before(pe, 0)
                for g in range(N):
                    u, i = g // NC, g % NC
                    if g + 1 < N and i < NC - 1:
                        mamba.before(pe, g + 1)
                    mamba.state(pe, g)
                    if u == 1 and i == 0:
                        pe.wait_ge(norm.ready, 12)
                    if u + 1 < UNITS:
                        for c in mamba.PIECES_AT[i]:
                            mamba.project(pe, u + 1, c)
                    mamba.outputs(pe, g)
                    if g >= 2:
                        mamba.squares(pe, g - 2, 0 if u == 0 else PARTS_OUT * (u - 1) + min(max(i - 3, 0), PARTS_OUT))
                    if u >= 1 and i in (3, 4, 5):
                        mamba.output(pe, u - 1, i - 3)
                    if u == 0 and i == 7:
                        norm.turn(pe, 10)
                        norm.turn(pe, 11)
                    if u == 1 and i == 1:
                        mamba.steps(pe, 1)
                    if u == 1 and i == 4:
                        mamba.sums(pe, 1)
                    if u == 2 and i == 7:
                        norm.turn(pe, 12)
                        norm.turn(pe, 13)
                    if u == 3 and i == 0:
                        pe.wait_ge(norm.ready, 14)
                        moe.logits(pe, 2)
                    if u == 3 and i == 1:
                        moe.counts(pe, 2)
                    if g + 1 < N and i == NC - 1:
                        mamba.before(pe, g + 1)
                pe.wait_ge(mamba.seg_exp, N)
                pe.wait_ge(mamba.cb_read, N)
                pe.wait_ge(mamba.x_read, N)
                pe.wait_ge(mamba.y_read, N)
                pe.wait_ge(mamba.h_ready, UNITS * (NC - 1))
                for g in (N - 2, N - 1):
                    mamba.squares(pe, g, PARTS_OUT * (UNITS - 1))
                mamba.output(pe, UNITS - 1, 0)
                moe.turn(pe, HALF)
                for u in range(HALF, 2 * HALF):
                    if u + 1 < 2 * HALF:
                        moe.turn(pe, u + 1)
                    if u == HALF + 2:
                        norm.turn(pe, 14)
                        norm.turn(pe, 15)
                    if u == HALF + 3:
                        moe.counts(pe, 3)
                    moe.hidden(pe, u)
                    if u in (HALF, HALF + 1):
                        mamba.output(pe, UNITS - 1, u - HALF + 1)
                    if u == HALF + 1:
                        pe.wait_ge(mamba.out_read, PARTS_OUT * UNITS)
                    if u == HALF + 2:
                        pe.wait_ge(norm.ready, 16)
                        moe.logits(pe, 3)
                    if u > HALF:
                        moe.results(pe, u - 1)
                moe.results(pe, 2 * HALF - 1)

            @block.sync
            def _(sp):
                for u in range(2 * HALF):
                    moe.load(sp, u)
                    if u in (E_ + 4, HALF + E_ + 4):
                        moe.fetch(sp, u // E_ - 1)
                    if u == HALF - 1:
                        moe.fetch(sp, 1)
                for half in range(2):
                    sp.wait_ge(moe.combined, 2 * 2 + half + 1)
                    sp.dma_start(core.stored_rows(0, half), core.x[:, half * GROUP:(half + 1) * GROUP, :]).then_inc(core.stored, 16)
                moe.fetch(sp, 3)
                for half in range(2):
                    sp.wait_ge(moe.combined, 2 * 3 + half + 1)
                    sp.dma_start(core.stored_rows(1, half), core.x[:, TPB + half * GROUP:TPB + (half + 1) * GROUP, :]).then_inc(core.stored, 16)
                sp.wait_ge(core.stored, 16 * 2 * B)

            @block.gpsimd
            def _(pool):
                ffn.base(pool)
                mamba.make_masks(pool)
                for u in range(HALF):
                    moe.send(pool, u)
                    if u in (4, 5, 6):
                        moe.scatter(pool, 1, 6 * (u - 4), min(6 * (u - 3), TOPK * TPB))
                for g in range(2):
                    mamba.cut_a(pool, g)
                mamba.to_state(pool, 0)
                for g in range(N):
                    u, i = g // NC, g % NC
                    if g + 2 < N:
                        mamba.cut_a(pool, g + 2)
                    if i < NC - 1:
                        mamba.to_state(pool, g + 1)
                    if u < 3:
                        mamba.gate(pool, nc.gpsimd, g)
                    if i < NC - 1:
                        mamba.decay(pool, g + 1)
                    elif g + 1 < N:
                        mamba.to_state(pool, g + 1)
                    if u == 3 and i >= 2:
                        moe.scatter(pool, 2, 3 * (i - 2), min(3 * (i - 1), TOPK * TPB))
                for u in range(HALF, 2 * HALF):
                    moe.send(pool, u)
                    if u in (HALF + 1, HALF + 2, HALF + 3):
                        n = 5 * (u - HALF - 1)
                        moe.scatter(pool, 3, n, n + 5 if u < HALF + 3 else TOPK * TPB)

            @block.vector
            def _(dve):
                ch = Chain(dve, chain)

                def experts(u, last):
                    if u == E_:
                        moe.take(dve, u)
                    if u + 1 < last and u + 1 != E_:
                        moe.take(dve, u + 1)
                    moe.gating(dve, u)
                    moe.address(dve, u)

                nc.vector.memset(moe.xs[64:P, :, moe.FULL, :], 0.0).then_inc(moe.tail_clear, 1)
                for i in (4, 5):
                    norm.stats_of(dve, ch, i)
                for i in (4, 5):
                    norm.normalise(dve, ch, i)
                moe.take(dve, 0)
                for u in range(HALF):
                    if u == 0:
                        ffn.take(dve)
                    if u == 6:
                        moe.put(dve, ch, 1)
                    if u < 3:
                        moe.take(dve, u + 1)
                        for c in range(FCH):
                            moe.gating(dve, u, [c])
                            for h in share(UNITS_AT[u], c):
                                ffn.add(dve, h)
                        moe.address(dve, u)
                    else:
                        experts(u, HALF)
                    if u == 3:
                        for half in range(2):
                            ffn.finish(dve, half)
                            norm.stats_of(dve, ch, 6 + half)
                        for i in (6, 7):
                            norm.normalise(dve, ch, i)
                    if u == 5:
                        moe.shift(dve, ch, 1)
                        moe.pick(dve, ch, 1)
                    if u == 8:
                        mamba.weigh_out(dve)
                    if u == 11:
                        for half in range(2):
                            moe.combine(dve, ch, 0, half)
                            norm.stats_of(dve, ch, 8 + half)
                        norm.normalise(dve, ch, 8)
                        norm.normalise(dve, ch, 9)
                    if u == 13:
                        mamba.step_sizes(dve, ch, 0)
                    if u >= 13:
                        for k in range(1, TAPS):
                            mamba.convolve(dve, ch, 0, u - 13, k)
                for k in range(1, TAPS):
                    mamba.convolve(dve, ch, 0, 3, k)
                dve.wait_ge(mamba.decays, 3)
                mamba.front(dve, 0)
                for g in range(N):
                    u, i = g // NC, g % NC
                    if u >= 1 and i == 2:
                        mamba.variance(dve, u - 1)
                    if g + 1 < N and i < NC - 1:
                        mamba.front(dve, g + 1)
                    mamba.pass_state(dve, g)
                    mamba.back(dve, g)
                    if u == 3:
                        mamba.gate(dve, nc.vector, g)
                    if u >= 1 and i in (3, 4, 5):
                        mamba.add(dve, ch, u - 1, i - 3)
                    if u + 1 < UNITS:
                        for c, k in mamba.TAPS_AT[i]:
                            mamba.convolve(dve, ch, u + 1, c, k)
                    if u == 0 and i in (3, 4):
                        moe.combine(dve, ch, 1, i - 3)
                        norm.stats_of(dve, ch, i + 7)
                    if u == 0 and i in (5, 6):
                        norm.normalise(dve, ch, i + 5)
                    if u == 1 and i == 2:
                        mamba.step_sizes(dve, ch, 1)
                    if u == 2 and i == 5:
                        norm.stats_of(dve, ch, 12)
                        norm.stats_of(dve, ch, 13)
                    if u == 2 and i == 6:
                        norm.normalise(dve, ch, 12)
                        norm.normalise(dve, ch, 13)
                    if u == 3 and i == 0:
                        moe.shift(dve, ch, 2)
                        moe.pick(dve, ch, 2)
                    if u == 3 and i == 1:
                        moe.put(dve, ch, 2)
                    if g + 1 < N and i == NC - 1:
                        mamba.front(dve, g + 1)
                mamba.variance(dve, UNITS - 1)
                moe.take(dve, HALF)
                for u in range(HALF, 2 * HALF):
                    if u == HALF + 3:
                        moe.put(dve, ch, 3)
                    experts(u, 2 * HALF)
                    if u == HALF:
                        mamba.add(dve, ch, UNITS - 1, 0)
                    if u == HALF + 1:
                        mamba.add(dve, ch, UNITS - 1, 1)
                        mamba.add(dve, ch, UNITS - 1, 2)
                        for n in (14, 15):
                            norm.stats_of(dve, ch, n)
                        for n in (14, 15):
                            norm.normalise(dve, ch, n)
                    if u == HALF + 2:
                        moe.shift(dve, ch, 3)
                        moe.pick(dve, ch, 3)
                    if u == HALF + 13:
                        for half in range(2):
                            moe.combine(dve, ch, 2, half)
                for half in range(2):
                    moe.combine(dve, ch, 3, half)

            @block.scalar
            def _(act):
                def experts(u, last):
                    moe.silu(act, u)
                    if u > last - HALF:
                        moe.weigh(act, u - 1)

                for i in (4, 5):
                    norm.root(act, i)
                mamba.exp_a(act)
                for i in (4, 5):
                    norm.copy(act, nc.scalar.copy, i)
                act.wait_ge(mamba.pads, 1)
                for u in range(HALF):
                    if u == 4:
                        for i in (6, 7):
                            norm.copy(act, nc.scalar.copy, i)
                    if u < 3:
                        for c in range(FCH):
                            moe.silu(act, u, [c])
                            for h in share(UNITS_AT[u], c):
                                ffn.relu(act, h)
                        if u:
                            moe.weigh(act, u - 1)
                    else:
                        experts(u, HALF)
                    if u == 3:
                        for i in (6, 7):
                            norm.root(act, i)
                    if u == 5:
                        moe.exp(act, 1)
                    if u == 11:
                        norm.root(act, 8)
                        norm.root(act, 9)
                    if u == 12:
                        norm.copy(act, nc.scalar.copy, 8)
                        norm.copy(act, nc.scalar.copy, 9)
                    if u == 13:
                        mamba.exp_dt(act, 0)
                        mamba.take(act, 0, 0)
                        mamba.first_tap(act, 0, 0)
                    if u == 15:
                        mamba.exp_sums(act, 0)
                    if u >= 13:
                        mamba.take(act, 0, u - 12)
                        mamba.first_tap(act, 0, u - 12)
                moe.weigh(act, HALF - 1)
                mamba.take(act, 0, 4)
                mamba.take(act, 0, 5)
                mamba.silu_rows(act, 0)
                mamba.silu_z(act, 0)
                mamba.exps(act, 0)
                for g in range(N):
                    u, i = g // NC, g % NC
                    if g + 1 < N and i < NC - 1:
                        mamba.exps(act, g + 1)
                    if u >= 1 and i == 2:
                        mamba.deviation(act, u - 1)
                    if u + 1 < UNITS:
                        for c in mamba.PIECES_AT[i]:
                            mamba.take(act, u + 1, c)
                            if c < 4:
                                mamba.first_tap(act, u + 1, c)
                    if g >= 1:
                        mamba.square(act, g - 1)
                    if u + 1 < UNITS and i == 6:
                        mamba.silu_rows(act, u + 1)
                    if u + 1 < UNITS and i == 7:
                        mamba.silu_z(act, u + 1)
                    if u == 0 and i == 5:
                        norm.root(act, 10)
                        norm.root(act, 11)
                    if u == 0 and i == 7:
                        norm.copy(act, nc.scalar.copy, 10)
                        norm.copy(act, nc.scalar.copy, 11)
                    if u == 1 and i == 2:
                        mamba.exp_dt(act, 1)
                    if u == 1 and i == 4:
                        mamba.exp_sums(act, 1)
                    if u == 2 and i == 6:
                        norm.root(act, 12)
                        norm.root(act, 13)
                    if u == 2 and i == 7:
                        norm.copy(act, nc.scalar.copy, 12)
                        norm.copy(act, nc.scalar.copy, 13)
                    if u == 3 and i == 0:
                        moe.exp(act, 2)
                    if g + 1 < N and i == NC - 1:
                        mamba.exps(act, g + 1)
                mamba.square(act, N - 1)
                mamba.deviation(act, UNITS - 1)
                for u in range(HALF, 2 * HALF):
                    if u == HALF + 2:
                        norm.copy(act, nc.scalar.copy, 14)
                        norm.copy(act, nc.scalar.copy, 15)
                    experts(u, 2 * HALF)
                    if u == HALF + 1:
                        norm.root(act, 14)
                        norm.root(act, 15)
                    if u == HALF + 2:
                        moe.exp(act, 3)
                moe.weigh(act, 2 * HALF - 1)




def macaron(nc, dram, out, stages=99):
    with ExitStack() as ctx:
        core = Core(nc, dram, ctx)
        core.stored = core.sem("stored")
        core.stored_rows = lambda b, half: out[b].rearrange("(g j p) d -> p g j d", g=2, p=P)[:, half, :, :]
        load_constants(core, ctx)
        core.moe = Moe(core)
        core.mamba = Mamba(core)
        load_ffn(core, ctx)
        core.rows = core.sb("rows", [P, TILES, core.moe.ROW])
        core.norm = Norm(core, "norm", ctx, lambda n: core.rows[:, n, 0:D], core.sb("norm_xT", [D, B * T]), None,
                         [0, 1] * 2 + [2, 3] * 2 + [0, 1, 2, 3] * 2)
        core.moe.open_routing(ctx, "moe", core.rows, core.norm.xT, core.norm)
        core.early = ExitStack()
        core.attention = Attention(core, "attn")
        setup = Setup(core)
        todo = [lambda: ffn(core, "ffn_a", setup), lambda: attention(core), lambda: moe_mamba_moe(core)]
        for n, stage in enumerate(todo[:stages]):
            stage()
            core.end_stage()
            if n == 1:
                core.early.close()
        core.early.close()
        if stages < 3:
            with nc.Block() as block:
                @block.sync
                def _(sp):
                    for g in range(GROUPS):
                        sp.dma_start(core.stored_rows(g // 2, g % 2), core.x[:, g * GROUP:(g + 1) * GROUP, :]).then_inc(core.stored, 16)
                    sp.wait_ge(core.stored, 64)


def kernel(**inputs):
    import concourse.bacc as bacc
    from concourse.bass_utils import run_bass_kernel_spmd as run

    nc = bacc.Bacc("TRN2", target_bir_lowering=False, num_devices=1)
    arrays = layout(inputs)
    dram = {k: nc.dram_tensor(f"in_{k}", v.shape, mybir.dt.from_np(v.dtype), kind="ExternalInput").ap() for k, v in arrays.items()}
    out = nc.dram_tensor("out", (B, T, D), F32, kind="ExternalOutput").ap()
    macaron(nc, dram, out)
    r = run(nc, [{f"in_{k}": v for k, v in arrays.items()}], core_ids=[0])
    return r.results[0]["out"]
```

```python
from contextlib import ExitStack

import numpy as np

import concourse.bass as bass
from concourse import mybir

F32 = mybir.dt.float32
BF16 = mybir.dt.bfloat16
I32 = mybir.dt.int32
U32 = mybir.dt.uint32
ALU = mybir.AluOpType
ACT = mybir.ActivationFunctionType
AX_X = mybir.AxisListType.X

P = 128
B, T, D = 2, 1024, 128
TILES = B * T // P
TPB = T // P
GROUP = 4
GROUPS = TILES // GROUP
GT = GROUP * P
BANK = 512
LN_EPS = 1e-5

M, INNER = 64, 16
HEADS, HD = 16, 8
PARTS = 3
HG = 4
HGROUPS = HEADS // HG
QK_ROWS = PARTS * PARTS * HD
QK_PAD = 96
ROOT_GUESS = 0x5f3759df
ROOT_STEPS = 3
NO_SHIFT_BOUND = 40.0
E_, CAP, FF = 8, 320, 448
TOPK = 2
FCF = FF // P
FCR = FF - FCF * P
FCH = FCF + 1
SLOTS = E_ * CAP
DIN, NST, NH, HP = 256, 128, 4, 64
TAPS = 4


def host_constants():
    c = {}
    c["identity"] = np.eye(P, dtype=np.float32)
    freqs = (1.0 / np.float32(10000.0) ** (np.arange(0, HD, 2, dtype=np.float32) / np.float32(HD))).astype(np.float32)
    ang = np.arange(T, dtype=np.float32)[None, :] * freqs[:, None]
    cos, sin = np.cos(ang).astype(np.float32), np.sin(ang).astype(np.float32)
    sign = np.where(np.arange(HD) % 2 == 0, -1.0, 1.0).astype(np.float32)
    c["rope_cos"] = np.tile(np.repeat(cos, 2, axis=0), (HEADS, 1))
    c["rope_sin"] = np.tile(np.repeat(sin, 2, axis=0) * sign[:, None], (HEADS, 1))
    c["head_of_row"] = np.kron(np.eye(HEADS, dtype=np.float32), np.ones((HD, 1), np.float32))
    c["expert_iota"] = np.arange(E_, dtype=np.float32)[None, :]
    c["token"] = np.arange(T, dtype=np.float32).reshape(TPB, P).T
    return {k: np.ascontiguousarray(v) for k, v in c.items()}


def layout(inputs):
    a = {}
    f = lambda k: np.asarray(inputs[k])
    twice = lambda v: np.concatenate([v, v], axis=0)
    a["x"] = f("L0_attn_x")
    a["win"] = f("L0_ffn_Win")
    a["ffn_w1"] = twice(f("L0_ffn_W1"))
    a["ffn_b1"] = twice(f("L0_ffn_b1"))
    a["ffn_w2"] = twice(f("L0_ffn_W2"))
    a["ffn_bin"] = twice(f("L0_ffn_bin_"))[:, None]
    a["ffn_b2"] = twice(f("L0_ffn_b2"))[:, None]
    a["wout"] = f("L0_ffn_Wout")
    a["bout"] = f("L0_ffn_bout")[None, :]
    w, b = f("L0_attn_W_qkv"), f("L0_attn_b_qkv")
    swap = np.arange(D).reshape(-1, 2)[:, ::-1].ravel()
    wq, wk, wv = w[:D], w[D:2 * D], w[2 * D:]
    bq, bk, bv = b[:D], b[D:2 * D], b[2 * D:]
    a["w_qkv"] = np.stack([wq.T, wq[swap].T, wk.T, wk[swap].T, wv.T], axis=1)
    a["b_qk"] = np.stack([bq, bq[swap], bk, bk[swap]], axis=1)
    a["b_v"] = bv[None, :]
    a["gate"] = f("L1_ffn_gate_w").T
    for n in ("w1", "w3"):
        w = f(f"L1_ffn_{n}").transpose(1, 0, 2)
        a[n], a[f"{n}_rest"] = w[:, :, 0:FCF * P], w[:, :, FCF * P:]
    w = f("L1_ffn_w2")
    a["w2"] = w[:, 0:FCF * P].reshape(E_, FCF, P, D).transpose(2, 0, 1, 3)
    a["w2_rest"] = w[:, FCF * P:].transpose(1, 0, 2)
    both = lambda n, g: np.stack([g(f(f"L1_attn_{n}_f")), g(f(f"L1_attn_{n}_b"))], axis=1)
    columns = lambda v: v.reshape(-1, P).T
    z_end, x_end = DIN, DIN + 4 * P
    a["mb_w_xbc"] = both("Wi", lambda w: w[z_end:x_end].T.reshape(D, 4, P))
    a["mb_w_z"] = both("Wi", lambda w: w[:z_end].T.reshape(D, 2, P))
    a["mb_w_dt"] = both("Wi", lambda w: w[x_end:].T).reshape(D, 2 * NH)
    a["mb_taps"] = both("conv_w", lambda w: w[:, 0, :].reshape(4, P, TAPS).transpose(1, 0, 2))
    a["mb_conv_b"] = both("conv_b", columns)
    a["mb_skip"] = both("D", lambda v: columns(np.repeat(v, HP)))
    a["mb_norm_w"] = both("norm_w", columns)
    a["mb_wo"] = both("Wo", lambda w: w.T.reshape(2, P, D).transpose(1, 0, 2))
    a["mb_dt_bias"] = both("dt_bias", lambda v: v[None, :]).reshape(1, 2 * NH)
    a["mb_a_log"] = both("A_log", lambda v: v[None, :]).reshape(1, 2 * NH)
    a.update(host_constants())
    return {k: np.ascontiguousarray(v) for k, v in a.items()}


class Core:

    def __init__(self, nc, dram, ctx):
        self.nc, self.dram, self.ctx = nc, dram, ctx
        self.stage_sems, self.retired = [], []

    def sb(self, name, shape, dt=F32, ctx=None):
        return (ctx or self.ctx).enter_context(self.nc.sbuf_tensor(name, shape, dt))

    def sem(self, name, ctx=None):
        s = self.nc.alloc_semaphore(name)
        if ctx is not None:
            self.stage_sems.append(s)
        return s

    def end_stage(self):
        for s in self.retired:
            self.nc.release_semaphore(s)
        numbers = sorted(s.num for s in self.stage_sems)
        while numbers:
            n = 1
            while n < len(numbers) and numbers[n] == numbers[0] + n:
                n += 1
            self.nc.gpsimd.sem_clear(range(numbers[0], numbers[0] + n))
            numbers = numbers[n:]
        self.retired, self.stage_sems = self.stage_sems, []


class Chain:

    def __init__(self, eng, sem):
        self.eng, self.sem, self.n = eng, sem, 0

    def step(self, ins):
        ins.then_inc(self.sem, 1)
        self.n += 1
        return self.n

    def wait(self):
        self.eng.wait_ge(self.sem, self.n)


def load_constants(core, ctx):
    nc, d = core.nc, core.dram
    core.x = core.sb("x_sb", [P, TILES, D])
    core.ident = core.sb("ident", [P, P])
    core.eps = core.sb("eps", [P, 1])
    core.loaded = {}

    def wait(eng, *names):
        for n in names:
            eng.wait_ge(*core.loaded[n])

    def await_together(name, loads):
        landed = core.sem(f"ld_{name}")
        for n, _, _ in loads:
            core.loaded[n] = (landed, 16 * len(loads))
    core.landed, core.await_together = wait, await_together


def load_ffn(core, ctx):
    sb = lambda n, shape: core.sb(n, shape, ctx=ctx)
    core.minus_b = sb("minus_b", [P, INNER])
    core.w2_b = sb("w2_b", [P, INNER])
    core.b2_clip = sb("b2_clip", [P, 1])
    core.win = sb("win_sb", [D, M])
    core.w1 = sb("w1_sb", [P, INNER])
    core.b1 = sb("b1_sb", [P, INNER])
    core.w2 = sb("w2_sb", [P, INNER])
    core.bin = sb("bin_sb", [P, 1])
    core.b2 = sb("b2_sb", [P, 1])
    core.wout = sb("wout_sb", [P, B, D])
    core.bout = sb("bout_sb", [P, D])
    core.b_pre = sb("b_pre", [P, INNER])
    core.bout_half = sb("bout_half", [P, D])
    core.biases_made = core.sem("biases_made")
    core.ffn_semaphores = FfnOfBatch.semaphores(core)


class Setup:

    def __init__(self, core):
        d, self.core = core.dram, core
        tokens = d["x"].rearrange("b (j p) d -> p (b j) d", p=P)
        groups = [slice(g * GROUP, (g + 1) * GROUP) for g in range(GROUPS)]
        self.x_loads = [(f"x{g}", core.x[:, s, :], tokens[:, s, :]) for g, s in enumerate(groups)]
        self.ffn_loads = [("ident", core.ident[:], d["identity"]), ("win", core.win[:], d["win"]),
                          ("ffn_w1", core.w1[:], d["ffn_w1"]), ("ffn_b1", core.b1[:], d["ffn_b1"]), ("ffn_bin", core.bin[:], d["ffn_bin"]),
                          ("ffn_w2", core.w2[:], d["ffn_w2"]), ("ffn_b2", core.b2[:], d["ffn_b2"]),
                          ("bout", core.bout[:], d["bout"].to_broadcast([P, D])),
                          ("wout_0", core.wout[0:M, 0, :], d["wout"]), ("wout_1", core.wout[M:P, 1, :], d["wout"])]
        for load in (*self.x_loads, *self.ffn_loads[:2]):
            core.await_together(load[0], [load])
        core.await_together("ffn_units", self.ffn_loads[2:7])
        core.await_together("ffn_out", self.ffn_loads[7:])
        self.zeros = core.sb("zeros", [P, 1, core.moe.ROW], ctx=core.early)
        self.zeroed, self.ones_set, self.tri_set, self.set = (core.sem(n) for n in ("zeroed", "ones_set", "tri_set", "constants_set"))

    def start(self, eng, loads):
        for name, dst, src in loads:
            eng.dma_start(dst, src).then_inc(self.core.loaded[name][0], 16)

    def sync(self, sp):
        core, moe = self.core, self.core.moe
        self.start(sp, (*self.x_loads[:2], *self.ffn_loads[2:], *self.x_loads[2:]))
        self.start(sp, (*core.attention.loads, *moe.loads, *core.mamba.loads))

    def clear(self, sp):
        moe = self.core.moe
        sp.wait_ge(self.zeroed, 2)
        for r in range(2 * B):
            sp.dma_start(moe.slots[r].rearrange("(p n) d -> p n d", p=P), self.zeros[:].to_broadcast([P, SLOTS // P, moe.ROW])).then_inc(moe.cleared, 16)
            sp.dma_start(moe.rows[r].rearrange("(p n) d -> p n d", p=P), self.zeros[:, :, 0:D].to_broadcast([P, TOPK * T // P, D])).then_inc(moe.cleared, 16)

    def scalar(self, act):
        self.start(act, self.ffn_loads[:2])

    def vector(self, dve):
        nc, core = self.core.nc, self.core
        nc.vector.memset(core.eps[:], LN_EPS).then_inc(self.set, 1)
        nc.vector.memset(core.wout[0:M, 1, :], 0.0).then_inc(self.set, 1)
        nc.vector.memset(core.wout[M:P, 0, :], 0.0).then_inc(self.set, 1)

    def biases(self, dve, ch):
        nc, core = self.core.nc, self.core
        core.landed(dve, "ffn_w1", "ffn_w2")
        nc.vector.scalar_tensor_tensor(core.b_pre[:], core.w1[:], core.bin[:], core.b1[:], ALU.mult, ALU.add).then_inc(core.biases_made, 1)
        dve.wait_ge(core.biases_made, 1)
        nc.vector.tensor_scalar(core.minus_b[:], core.b_pre[:], -1.0, None, ALU.mult)
        ch.step(nc.vector.tensor_tensor(core.w2_b[:], core.w2[:], core.b_pre[:], ALU.mult))
        ch.wait()
        ch.step(nc.vector.reduce_sum(core.b2_clip[:], core.w2_b[:], AX_X))
        ch.wait()
        nc.vector.tensor_tensor(core.b2_clip[:], core.b2_clip[:], core.b2[:], ALU.add).then_inc(core.biases_made, 1)
        core.landed(dve, "bout")
        nc.vector.tensor_scalar(core.bout_half[:], core.bout[:], 0.5, None, ALU.mult).then_inc(core.biases_made, 1)
        dve.wait_ge(core.biases_made, 3)

    def gpsimd(self, pool):
        nc, moe, zeros = self.core.nc, self.core.moe, self.zeros
        nc.gpsimd.memset(zeros[:], 0.0).then_inc(self.zeroed, 1)
        nc.gpsimd.memset(moe.tri[:], 1.0).then_inc(self.ones_set, 1)
        pool.wait_ge(self.zeroed, 1)
        nc.gpsimd.memset(zeros[:, :, moe.TOKEN], moe.NOWHERE).then_inc(self.zeroed, 1)
        pool.wait_ge(self.ones_set, 1)
        nc.gpsimd.affine_select(out=moe.tri[:, 0, :], in_=moe.tri[:, 0, :], compare_op=ALU.is_ge, fill=0.0, base=0,
                                pattern=[[1, P]], channel_multiplier=-1).then_inc(self.tri_set, 1)


class Attention:

    def __init__(self, core, name):
        nc = core.nc
        self.core, self.name, self.ctx = core, name, core.early
        dram = lambda n, shape, dt: nc.dram_tensor(f"{name}_{n}", shape, dt).ap()
        self.q_parts = dram("q_parts", (B, HEADS, PARTS, HD, T), BF16)
        self.k_parts = dram("k_parts", (B, HEADS, 2 * PARTS - 1, HD, T), BF16)
        self.shift = dram("shift", (B, HEADS, PARTS, T), BF16)
        sb, d = (lambda n, shape: core.sb(f"{name}_{n}", shape, ctx=self.ctx)), core.dram
        self.w, self.b_qk, self.b_v = sb("w", [D, 5, D]), sb("b_qk", [D, 4]), sb("b_v", [P, D])
        self.cos, self.sin, self.head_of_row = sb("cos", [D, T]), sb("sin", [D, T]), sb("head_of_row", [P, HEADS])
        self.loads = [("w_qkv", self.w[:], d["w_qkv"]), ("b_qk", self.b_qk[:], d["b_qk"]), ("rope_cos", self.cos[:], d["rope_cos"]),
                      ("rope_sin", self.sin[:], d["rope_sin"]), ("b_v", self.b_v[:], d["b_v"].to_broadcast([P, D])),
                      ("head_of_row", self.head_of_row[:], d["head_of_row"])]
        core.await_together("w_qkv", self.loads[:1])
        core.await_together("attention", self.loads[1:])

    def open(self, ctx):
        core, nc, name = self.core, self.core.nc, self.name
        sb = lambda n, shape, dt=F32: core.sb(f"{name}_{n}", shape, dt, ctx)
        sem = lambda n: core.sem(f"{name}_{n}", ctx)
        psum = lambda n, shape: ctx.enter_context(nc.psum_tensor(f"{name}_{n}", shape, F32))
        self.v = sb("v", [P, TILES, HEADS, 32])
        self.q = [sb(f"q{i}", [QK_PAD, HG, T], BF16) for i in range(2)]
        self.k = [sb(f"k{i}", [QK_PAD, HG, T], BF16) for i in range(2)]
        self.p = sb("p", [P, self.PB, 2, BANK])
        self.mixed = sb("mixed", [P, BANK])
        self.rden, self.scaled = sb("rden", [P, GROUP, HG]), sb("scaled", [P, GROUP, HG, HD])
        self.work = sb("work", [P, 8, GT])
        self.t_cos, self.t_sin, self.rot, self.rest = (self.work[:, 2 * i:2 * i + 2, :] for i in range(4))
        self.parts = sb("parts", [D, 2, PARTS, T], BF16)
        self.zero = sb("zero", [P, 1, T // 4], BF16)
        self.peaks, self.peak, self.bound_rows = sb("peaks", [D, 2, GROUPS]), sb("peak", [D, 2, B]), sb("bound_rows", [D, B])
        self.bound, self.flag = sb("bound", [1, B]), sb("flag", [1, B], I32)
        self.top, self.top_rest = sb("top", [P, HG, TPB]), sb("top_rest", [P, HG, TPB])
        self.top_parts = sb("top_parts", [P, PARTS, HG, TPB], BF16)
        self.ps_s, self.ps_av = psum("ps_s", [P, self.SB, 2, BANK]), psum("ps_av", [P, BANK])
        self.ps_side = psum("ps_side", [P, 1, BANK])
        self.v_filled, self.zeroed, self.shift_clear, self.padded = (sem(n) for n in ("v_filled", "zeroed", "shift_clear", "padded"))
        self.qk_done, self.v_done, self.v_read, self.qk_read, self.rot_done = (sem(n) for n in ("qk_done", "v_done", "v_read", "qk_read", "rot_done"))
        self.part0, self.rest_done, self.part1, self.part2 = (sem(n) for n in ("part0", "rest_done", "part1", "part2"))
        self.peaked, self.rows_done, self.bound_done, self.flagged, self.scratch = (
            sem(n) for n in ("peaked", "rows_done", "bound_done", "flagged", "scratch"))
        self.landed = [sem(f"heads{i}") for i in range(2)]
        self.scored, self.exped, self.summed, self.av_read, self.turned, self.den_done, self.out_done, self.o_read = (
            sem(n) for n in ("scored", "exped", "summed", "av_read", "turned", "den_done", "out_done", "o_read"))
        self.shifting = [{n: sem(f"shift{b}_{n}") for n in ("free", "landed", "scored", "maxed", "own", "split", "stored")} for b in range(B)]


    def project(self, pe, side, i):
        nc, xT = self.core.nc, self.core.norm.xT

        def qk(s):
            bank = side.take(pe, ("qk", i, s), self.qk_read, 4 * i + s + 1)
            nc.tensor.matmul(bank, self.w[:, s, :], xT[:, i * GT:(i + 1) * GT], start=True, stop=True).then_inc(self.qk_done, 1)

        def v():
            bank = side.take(pe, ("v", i), self.v_read, i + 1)
            for j in range(GROUP):
                n = i * GROUP + j
                ins = nc.tensor.matmul(bank[:, j * D:(j + 1) * D], xT[:, n * P:(n + 1) * P], self.w[:, 4, :], start=True, stop=True)
            ins.then_inc(self.v_done, 1)

        return qk, v

    def rope(self, dve, side, i):
        nc = self.core.nc
        at = slice((i % 2) * GT, (i % 2) * GT + GT)
        for s in range(4):
            k, (tile, table) = s // 2, ((self.t_cos, self.cos), (self.t_sin, self.sin))[s % 2]
            dve.wait_ge(self.qk_done, 4 * i + s + 1)
            nc.vector.scalar_tensor_tensor(tile[:, k, :], side.of(("qk", i, s)), self.b_qk[:, s:s + 1], table[:, at], ALU.add, ALU.mult)\
              .then_inc(self.qk_read, 1)
        dve.wait_ge(self.qk_read, 4 * i + 4)
        if i:
            dve.wait_ge(self.rest_done, 2 * i)
        for k in range(2):
            nc.vector.tensor_tensor(self.rot[:, k, :], self.t_cos[:, k, :], self.t_sin[:, k, :], ALU.add).then_inc(self.rot_done, 1)

    def take_v(self, dve, side, i):
        nc = self.core.nc
        dve.wait_ge(self.v_done, i + 1)
        dve.wait_ge(self.v_filled, 2)
        nc.vector.tensor_tensor(self.v[:, i * GROUP:(i + 1) * GROUP, :, 0:HD], side.of(("v", i)).rearrange("p (j h d) -> p j h d", j=GROUP, h=HEADS),
                                self.b_v[:].rearrange("p (h d) -> p h d", h=HEADS).unsqueeze(1).to_broadcast([P, GROUP, HEADS, HD]),
                                ALU.add).then_inc(self.v_read, 1)

    def peak_of(self, dve, i):
        nc = self.core.nc
        dve.wait_ge(self.rot_done, 2 * i + 2)
        nc.vector.tensor_reduce(self.peaks[:, :, i:i + 1], self.rot, AX_X, ALU.max, apply_absolute_value=True).then_inc(self.peaked, 1)

    def columns(self, i):
        return slice((i % 2) * GT, (i % 2) * GT + GT)

    def leading(self, eng, copy, i):
        if i >= 2:
            eng.wait_ge(self.scratch, 16 * (3 * PARTS - 1))
        for k in range(2):
            eng.wait_ge(self.rot_done, 2 * i + k + 1)
            copy(self.parts[:, k, 0, self.columns(i)], self.rot[:, k, :]).then_inc(self.part0, 1)

    def middle(self, eng, copy, i):
        for k in range(2):
            eng.wait_ge(self.rest_done, 2 * i + k + 1)
            copy(self.parts[:, k, 1, self.columns(i)], self.rest[:, k, :]).then_inc(self.part1, 1)

    def rests(self, dve, i):
        if i:
            dve.wait_ge(self.part2, 2 * i)
        for k in range(2):
            dve.wait_ge(self.part0, 2 * i + k + 1)
            self.core.nc.vector.tensor_tensor(self.rest[:, k, :], self.rot[:, k, :], self.parts[:, k, 0, self.columns(i)], ALU.subtract).then_inc(self.rest_done, 1)

    def last(self, dve, i):
        for k in range(2):
            dve.wait_ge(self.part1, 2 * i + k + 1)
            self.core.nc.vector.tensor_tensor(self.parts[:, k, 2, self.columns(i)], self.rest[:, k, :], self.parts[:, k, 1, self.columns(i)], ALU.subtract)\
                .then_inc(self.part2, 1)

    def store(self, sp, b):
        for j, done in enumerate((self.part0, self.part1, self.part2)):
            sp.wait_ge(done, 4 * (b + 1))
            sp.dma_start(self.q_parts[b, :, j, :, :], self.parts[:, 0, j, :]).then_inc(self.scratch, 16)
            for at in range(j, 2 * PARTS - 1, PARTS):
                sp.dma_start(self.k_parts[b, :, at, :, :], self.parts[:, 1, j, :]).then_inc(self.scratch, 16)
        sp.wait_ge(self.scratch, 16 * (b + 1) * (3 * PARTS - 1))


    def bound_factors(self, dve, ch, b):
        nc = self.core.nc
        dve.wait_ge(self.peaked, 2 * (b + 1))
        ch.step(nc.vector.tensor_reduce(self.peak[:, :, b:b + 1], self.peaks[:, :, 2 * b:2 * b + 2], AX_X, ALU.max))
        ch.wait()
        nc.vector.tensor_tensor(self.bound_rows[:, b:b + 1], self.peak[:, 0, b:b + 1], self.peak[:, 1, b:b + 1], ALU.mult).then_inc(self.rows_done, 1)

    def bound_sums(self, pe, side, b):
        pe.wait_ge(self.rows_done, b + 1)
        bank = side.take(pe, ("bound", b), self.flagged, b + 1)
        self.core.nc.tensor.matmul(bank[0:1, 0:HEADS], self.bound_rows[:, b:b + 1], self.head_of_row[:], start=True, stop=True).then_inc(self.bound_done, 1)

    def bound_flag(self, dve, ch, side, b):
        nc = self.core.nc
        dve.wait_ge(self.bound_done, b + 1)
        ch.step(nc.vector.reduce_max(self.bound[:, b:b + 1], side.of(("bound", b))[0:1, 0:HEADS], AX_X))
        ch.wait()
        nc.vector.tensor_scalar(self.flag[:, b:b + 1], self.bound[:, b:b + 1], NO_SHIFT_BOUND * HD ** 0.5, None, ALU.is_gt).then_inc(self.flagged, 1)


    def needed(self, eng, b):
        eng.wait_ge(self.flagged, b + 1)
        flag = eng.alloc_register(f"{self.name}_needs_shift{b}")
        eng.reg_load(flag, self.flag[0:1, b:b + 1])
        return eng.If_ne(flag, 0)

    def shift_sync(self, sp, b):
        nc, sems = self.core.nc, self.shifting[b]
        q, k = self.q[1], self.k[1]
        groups = lambda ap: ap[b].rearrange("(g h) i d t -> g h i d t", h=HG)
        with self.needed(sp, b):
            sp.wait_ge(self.padded, 4)
            sp.wait_ge(self.shift_clear, 16)
            if b:
                sp.wait_ge(self.scored, 2 * HGROUPS * self.UNITS)
            sp.sem_inc(sems["free"], 1)
            with sp.Fori(0, HGROUPS) as g:
                sp.wait_ge(sems["free"], g + 1)
                for r in range(PARTS):
                    rows = slice(r * PARTS * HD, (r + 1) * PARTS * HD)
                    sp.dma_start(q[rows, :, :], groups(self.q_parts)[bass.ds(g, 1)].rearrange("g h i d t -> (g i d) h t")).then_inc(sems["landed"], 16)
                    sp.dma_start(k[rows, :, :], groups(self.k_parts)[bass.ds(g, 1), :, r:r + PARTS].rearrange("g h i d t -> (g i d) h t"))\
                      .then_inc(sems["landed"], 16)
                sp.wait_ge(sems["split"], g + 1)
                dst = self.shift[b].rearrange("(g h) i t -> g h i t", h=HG)[bass.ds(g, 1)]
                for i in range(PARTS):
                    for h in range(HG):
                        with nc.allow_non_contiguous_dma("one value of a query to a row"):
                            sp.dma_start(dst[:, h, i, :].rearrange("g (j p) -> (g p) j", p=P), self.top_parts[:, i, h, :]).then_inc(sems["stored"], 16)
                sp.wait_ge(sems["stored"], 16 * PARTS * HG * (g + 1))
                sp.sem_inc(sems["free"], 1)

    def shift_tensor(self, pe, b):
        sems, STEPS = self.shifting[b], HG * TPB
        ps = self.ps_s.rearrange("p s a n -> p s (a n)")
        with self.needed(pe, b):
            if b:
                pe.wait_ge(self.exped, self.UNITS * 2 * HGROUPS)
            with pe.Fori(0, HGROUPS) as g:
                pe.wait_ge(sems["landed"], 16 * 2 * PARTS * (g + 1))
                for n in range(STEPS):
                    pe.wait_ge(sems["maxed"], STEPS * g + n + 1)
                    for half in range(2):
                        ins = self.core.nc.tensor.matmul(ps[:, n % 2, half * BANK:(half + 1) * BANK], self.q[1][0:QK_ROWS, n // TPB, n % TPB * P:n % TPB * P + P],
                                                         self.k[1][0:QK_ROWS, n // TPB, half * BANK:(half + 1) * BANK], start=True, stop=True)
                    ins.then_inc(sems["scored"], 1)
            pe.wait_ge(sems["maxed"], STEPS * HGROUPS + 2)

    def shift_vector(self, dve, b):
        nc, sems, STEPS = self.core.nc, self.shifting[b], HG * TPB
        ps, parts, peak, rest = self.ps_s.rearrange("p s a n -> p s (a n)"), self.top_parts, self.top, self.top_rest
        with self.needed(dve, b):
            dve.sem_inc(sems["maxed"], 2)
            with dve.Fori(0, HGROUPS) as g:
                for n in range(STEPS):
                    dve.wait_ge(sems["scored"], STEPS * g + n + 1)
                    nc.vector.reduce_max(peak[:, n // TPB, n % TPB:n % TPB + 1], ps[:, n % 2, :], AX_X).then_inc(sems["maxed"], 1)
                dve.wait_ge(sems["maxed"], STEPS * (g + 1) + 2)
                dve.wait_ge(sems["free"], g + 1)
                nc.vector.tensor_scalar(parts[:, 0, :, :], peak[:], -1.0, None, ALU.mult).then_inc(sems["own"], 1)
                dve.wait_ge(sems["own"], 3 * g + 1)
                nc.vector.scalar_tensor_tensor(rest[:], peak[:], -1.0, parts[:, 0, :, :], ALU.mult, ALU.subtract).then_inc(sems["own"], 1)
                dve.wait_ge(sems["own"], 3 * g + 2)
                nc.vector.tensor_copy(parts[:, 1, :, :], rest[:]).then_inc(sems["own"], 1)
                dve.wait_ge(sems["own"], 3 * g + 3)
                nc.vector.tensor_tensor(parts[:, 2, :, :], rest[:], parts[:, 1, :, :], ALU.subtract).then_inc(sems["split"], 1)


    UNITS = 2 * TPB
    SB, PB = 3, 4
    BLOCKS = [(b, hg, half) for b in range(B) for hg in range(HGROUPS) for half in range(2)]
    LAST = len(BLOCKS) // B - 1
    LOADS = 2 * PARTS + 1

    def load_heads(self, sp, n):
        b, hg = n // HGROUPS, n % HGROUPS
        heads = slice(hg * HG, (hg + 1) * HG)
        q, k, landed = self.q[n % 2], self.k[n % 2], self.landed[n % 2]
        if n >= 2:
            sp.wait_ge(self.scored, 2 * self.UNITS * (n - 1))
        for r in range(PARTS):
            rows = slice(r * PARTS * HD, (r + 1) * PARTS * HD)
            if n:
                sp.dma_start(q[rows, :, :], self.q_parts[b, heads].rearrange("h i d t -> (i d) h t")).then_inc(landed, 16)
            sp.dma_start(k[rows, :, :], self.k_parts[b, heads, r:r + PARTS].rearrange("h i d t -> (i d) h t")).then_inc(landed, 16)

    def load_first_q(self, act):
        act.wait_ge(self.scratch, 16 * (3 * PARTS - 1))
        act.wait_ge(self.padded, 4)
        for r in range(PARTS):
            act.dma_start(self.q[0][r * PARTS * HD:(r + 1) * PARTS * HD, :, :], self.q_parts[0, 0:HG].rearrange("h i d t -> (i d) h t"))\
               .then_inc(self.landed[0], 16)

    def load_shift(self, sp, n):
        b, hg = n // HGROUPS, n % HGROUPS
        sp.dma_start(self.q[n % 2][QK_ROWS:QK_ROWS + PARTS, :, :], self.shift[b, hg * HG:(hg + 1) * HG].rearrange("h i t -> i h t"))\
          .then_inc(self.landed[n % 2], 16)

    def scores(self, pe, w):
        n, u = w // self.UNITS, w % self.UNITS
        b, hg, half = self.BLOCKS[n]
        i, kt, pair = n // 2, u // 2, u % 2
        if u == 0:
            pe.wait_ge(self.landed[i % 2], 16 * self.LOADS * (i // 2 + 1))
        if w >= self.SB:
            pe.wait_ge(self.exped, w - self.SB + 1)
        for j in range(2):
            h = 2 * pair + j
            ins = self.core.nc.tensor.matmul(self.ps_s[:, w % self.SB, j, :], self.k[i % 2][:, h, kt * P:(kt + 1) * P],
                                             self.q[i % 2][:, h, half * BANK:(half + 1) * BANK], start=True, stop=True)
        ins.then_inc(self.scored, 1)

    def exp(self, act, w):
        act.wait_ge(self.scored, w + 1)
        if w >= self.PB:
            act.wait_ge(self.summed, w - self.PB + 1)
        self.core.nc.scalar.activation(self.p[:, w % self.PB, :, :].rearrange("p a n -> p (a n)"),
                                       self.ps_s[:, w % self.SB, :, :].rearrange("p a n -> p (a n)"), ACT.Exp, scale=float(HD) ** -0.5)\
            .then_inc(self.exped, 1)

    def weigh(self, pe, w):
        n, u = w // self.UNITS, w % self.UNITS
        b, hg, half = self.BLOCKS[n]
        kt, pair = u // 2, u % 2
        if u == 0 and n >= 1:
            pe.wait_ge(self.av_read, n)
        pe.wait_ge(self.exped, w + 1)
        for j in range(2):
            h = 2 * pair + j
            ins = self.core.nc.tensor.matmul(self.ps_av[32 * h:32 * h + 32, :], self.v[:, b * TPB + kt, hg * HG + h, :],
                                             self.p[:, w % self.PB, j, :], start=(kt == 0), stop=(kt == TPB - 1))
        ins.then_inc(self.summed, 1)

    def turn(self, pe, side, n):
        pe.wait_ge(self.av_read, n + 1)
        bank = side.take(pe, ("out", n), self.o_read, n + 1)
        for j in range(GROUP):
            ins = self.core.nc.tensor.transpose(bank[:, j * P:(j + 1) * P], self.mixed[:, j * P:(j + 1) * P], self.core.ident[:])
        ins.then_inc(self.turned, 1)

    def finish(self, dve, side, n):
        nc, (b, hg, half) = self.core.nc, self.BLOCKS[n]
        dve.wait_ge(self.summed, self.UNITS * (n + 1))
        if n:
            dve.wait_ge(self.turned, n)
        nc.vector.tensor_copy(self.mixed[:], self.ps_av[:]).then_inc(self.av_read, 1)
        dve.wait_ge(self.turned, n + 1)
        o = side.of(("out", n)).rearrange("p (j h c) -> p j h c", j=GROUP, h=HG)
        nc.vector.reciprocal(self.rden[:], o[:, :, :, HD]).then_inc(self.den_done, 1)
        dve.wait_ge(self.den_done, n + 1)
        nc.vector.tensor_tensor(self.scaled[:], o[:, :, :, 0:HD], self.rden[:].unsqueeze(3).to_broadcast([P, GROUP, HG, HD]), ALU.mult)\
          .then_inc(self.o_read, 1)
        dve.wait_ge(self.o_read, n + 1)
        n0 = b * TPB + half * GROUP
        xs = self.core.x[:, n0:n0 + GROUP, hg * HG * HD:(hg + 1) * HG * HD]
        nc.vector.tensor_tensor(xs, xs, self.scaled[:].rearrange("p j h d -> p j (h d)"), ALU.add).then_inc(self.out_done, 1)

    def fill(self, pool):
        nc = self.core.nc
        nc.gpsimd.memset(self.v[:], 0.0).then_inc(self.v_filled, 1)
        nc.gpsimd.memset(self.zero[:], 0.0).then_inc(self.zeroed, 1)
        pool.wait_ge(self.v_filled, 1)
        nc.gpsimd.memset(self.v[:, :, :, HD:HD + 1], 1.0).then_inc(self.v_filled, 1)
        pool.wait_ge(self.v_filled, 2)

    def pad(self, pool):
        nc = self.core.nc
        for i in range(2):
            nc.gpsimd.memset(self.q[i][64:QK_PAD, :, :], 0.0).then_inc(self.padded, 1)
            nc.gpsimd.memset(self.k[i][64:QK_PAD, :, :], 1.0).then_inc(self.padded, 1)
        pool.wait_ge(self.padded, 4)


def ffn_and_attention(core, setup):
    a, nc, moe, norm = core.attention, core.nc, core.moe, core.norm
    UNITS, LAST = a.UNITS, a.LAST
    TOTAL = len(a.BLOCKS) * UNITS
    with ExitStack() as ctx:
        a.open(ctx)
        side = norm.side = SideBanks(a.ps_side, 1)
        early = SideBanks(a.ps_s.rearrange("p s a n -> p (s a) n"), 2 * a.SB)
        first_ffn, ffn = [FfnOfBatch(core, b, 4 * b, a.work) for b in range(B)], FfnOfBatch(core, B, 8, a.work)
        chain, numbered = core.sem("attn_dve_chain", ctx), core.sem("numbered", ctx)
        with nc.Block() as block:
            @block.tensor
            def _(pe):
                core.landed(pe, "ident", "win")
                norm.side = early
                for i in (0, 1):
                    norm.turn(pe, i)
                first_ffn[0].project(pe)
                core.landed(pe, "wout_0")
                pe.wait_ge(setup.set, 3)
                for half in range(2):
                    first_ffn[0].output(pe, half)
                for i in (2, 3):
                    norm.turn(pe, i)
                norm.side = side
                core.landed(pe, "w_qkv")
                for i in (0, 1):
                    pe.wait_ge(norm.ready, i + 3)
                    qk, v = a.project(pe, early, i)
                    for s in range(4):
                        qk(s)
                    v()
                core.landed(pe, "head_of_row")
                a.bound_sums(pe, early, 0)
                for i in (4, 5):
                    norm.turn(pe, i)
                pe.wait_ge(a.v_read, 2)
                pe.wait_ge(a.flagged, 1)
                a.shift_tensor(pe, 0)
                first_ffn[1].project(pe)
                PRODUCTS_AT = (7, 9, 11, 13, 15)
                AHEAD = 3
                for w in range(TOTAL + AHEAD):
                    n, u = w // UNITS, w % UNITS
                    if (n, u) == (LAST + 1, 0):
                        a.shift_tensor(pe, 1)
                    opens = u == AHEAD
                    if w >= AHEAD and not opens:
                        a.weigh(pe, w - AHEAD)
                    if w < TOTAL:
                        a.scores(pe, w)
                    if opens:
                        a.weigh(pe, w - AHEAD)
                    if w > UNITS and u == 5:
                        a.turn(pe, side, n - 1)
                    if n == 2 and u in (8, 10):
                        first_ffn[1].output(pe, (u - 8) // 2)
                    if (n, u) in ((3, 7), (3, 9)):
                        norm.turn(pe, 6 + (u - 7) // 2)
                    if (n, u) == (4, 7):
                        pe.wait_ge(norm.ready, 8)
                    if n in (4, 5) and u in PRODUCTS_AT:
                        qk, v = a.project(pe, side, n - 2)
                        step = PRODUCTS_AT.index(u)
                        qk(step) if step < 4 else v()
                    if (n, u) == (7, 8):
                        a.bound_sums(pe, side, 1)
                    n -= LAST
                    if (n, u) in ((2, 8), (2, 10)):
                        norm.turn(pe, 8 + (u - 8) // 2)
                    if (n, u) == (2, 13):
                        ffn.project(pe)
                    if (n, u) in ((5, 8), (5, 9)):
                        ffn.output(pe, u - 8)
                    if (n, u) in ((5, 15), (6, 1)):
                        norm.turn(pe, n + 5)
                    if (n, u) == (6, 8):
                        moe.logits(pe, 0)
                    if (n, u) == (7, 1):
                        moe.counts(pe, 0)
                a.turn(pe, side, len(a.BLOCKS) - 1)

            @block.sync
            def _(sp):
                setup.sync(sp)
                sp.wait_ge(a.zeroed, 1)
                sp.dma_start(a.shift.rearrange("b h i (c t) -> (b h i) c t", c=4), a.zero[0:B * HEADS * PARTS].to_broadcast([B * HEADS * PARTS, 4, T // 4])).then_inc(a.shift_clear, 16)
                a.store(sp, 0)
                sp.wait_ge(a.padded, 4)
                a.load_heads(sp, 0)
                a.shift_sync(sp, 0)
                sp.wait_ge(a.shift_clear, 16)
                a.load_shift(sp, 0)
                for n in range(1, B * HGROUPS):
                    if n == HGROUPS:
                        a.store(sp, 1)
                    a.load_heads(sp, n)
                    if n == HGROUPS:
                        a.shift_sync(sp, 1)
                    a.load_shift(sp, n)
                    if n == 1:
                        setup.clear(sp)
                sp.wait_ge(moe.cleared, 16 * 2 * 2 * B)
                sp.wait_ge(moe.scattered[0], 16 * TOPK * TPB)

            @block.gpsimd
            def _(pool):
                setup.gpsimd(pool)
                a.fill(pool)
                first_ffn[0].base(pool)
                a.pad(pool)
                core.landed(pool, "moe_token")
                for b in range(B):
                    nc.gpsimd.tensor_copy(core.rows[:, b * TPB:(b + 1) * TPB, moe.TOKEN], moe.token[:]).then_inc(numbered, 1)
                first_ffn[1].base(pool)
                for i in (2, 3):
                    a.leading(pool, nc.gpsimd.tensor_copy, i)
                    a.middle(pool, nc.gpsimd.tensor_copy, i)
                ffn.base(pool)
                pool.wait_ge(moe.cleared, 16 * 2 * 2 * B)
                pool.wait_ge(numbered, B)
                moe.scatter(pool, 0)

            @block.scalar
            def _(act):
                setup.scalar(act)
                act.wait_ge(setup.set, 3)
                norm.side = early
                for i in (0, 1):
                    norm.root(act, i)
                for i in (0, 1):
                    norm.copy(act, nc.scalar.copy, i)
                act.wait_ge(core.biases_made, 1)
                for h in range(INNER):
                    first_ffn[0].relu(act, h)
                for i in (2, 3):
                    norm.root(act, i)
                for i in (2, 3):
                    norm.copy(act, nc.scalar.copy, i)
                for i in (4, 5):
                    norm.root(act, i)
                norm.side = side
                for i in (0, 1):
                    a.leading(act, nc.scalar.copy, i)
                    a.middle(act, nc.scalar.copy, i)
                for i in (4, 5):
                    norm.copy(act, nc.scalar.copy, i)
                a.load_first_q(act)
                for w in range(TOTAL):
                    n, u = w // UNITS, w % UNITS
                    a.exp(act, w)
                    if (n, u) == (LAST + 6, 10):
                        moe.exp(act, 0)

            @block.vector
            def _(dve):
                ch = Chain(dve, chain)
                setup.vector(dve)
                for i in (0, 1):
                    core.landed(dve, f"x{i}")
                    norm.stats_of(dve, ch, i)
                for i in (0, 1):
                    norm.normalise(dve, ch, i)
                setup.biases(dve, ch)
                norm.side = early
                first_ffn[0].take(dve)
                for h in range(INNER):
                    first_ffn[0].add(dve, h)
                for half in range(2):
                    first_ffn[0].finish(dve, half)
                    norm.stats_of(dve, ch, 2 + half)
                norm.side = side
                for i in (2, 3):
                    norm.normalise(dve, ch, i)
                for i in (2, 3):
                    core.landed(dve, f"x{i}")
                    norm.stats_of(dve, ch, 2 + i)
                core.landed(dve, "b_qk", "moe_iota")
                for i in (0, 1):
                    a.rope(dve, early, i)
                    if i == 0:
                        a.peak_of(dve, i)
                    a.rests(dve, i)
                    a.last(dve, i)
                a.peak_of(dve, 1)
                a.bound_factors(dve, ch, 0)
                for i in (0, 1):
                    a.take_v(dve, early, i)
                for i in (4, 5):
                    norm.normalise(dve, ch, i)
                a.bound_flag(dve, ch, early, 0)
                a.shift_vector(dve, 0)
                first_ffn[1].take(dve)
                for h in range(0, 13):
                    first_ffn[1].add(dve, h)
                for n in range(len(a.BLOCKS)):
                    if n == LAST:
                        a.shift_vector(dve, 1)
                    a.finish(dve, side, n)
                    if n == 0:
                        for h in range(13, INNER):
                            first_ffn[1].add(dve, h)
                    if n == 1:
                        for half in range(2):
                            first_ffn[1].finish(dve, half)
                            norm.stats_of(dve, ch, 6 + half)
                        norm.invert(dve, ch, 6)
                        for i in (6, 7):
                            norm.normalise(dve, ch, i)
                    if n == 2:
                        for i in (6, 7):
                            norm.copy(dve, nc.vector.tensor_copy, i)
                    if n == 3:
                        a.rope(dve, side, 2)
                        a.take_v(dve, side, 2)
                        a.peak_of(dve, 2)
                    if n == 4:
                        a.rests(dve, 2)
                        a.rope(dve, side, 3)
                        a.take_v(dve, side, 3)
                        a.peak_of(dve, 3)
                    if n == 5:
                        a.last(dve, 2)
                        a.rests(dve, 3)
                        a.last(dve, 3)
                        a.bound_factors(dve, ch, 1)
                    if n == 6:
                        a.bound_flag(dve, ch, side, 1)
                    if n == LAST:
                        dve.wait_ge(a.out_done, n + 1)
                        for i in (8, 9):
                            norm.stats_of(dve, ch, i)
                        norm.invert(dve, ch, 8)
                    if n == LAST + 1:
                        for i in (8, 9):
                            norm.normalise(dve, ch, i)
                        for i in (8, 9):
                            norm.copy(dve, nc.vector.tensor_copy, i)
                        ffn.take(dve)
                        for h in range(0, 2):
                            ffn.add(dve, h)
                    if n == LAST + 2:
                        for h in range(2, 9):
                            ffn.add(dve, h)
                    if n == LAST + 3:
                        for h in range(9, INNER):
                            ffn.add(dve, h)
                    if n == LAST + 4:
                        for i in (0, 1):
                            ffn.finish(dve, i)
                            norm.stats_of(dve, ch, 10 + i)
                        norm.invert(dve, ch, 10)
                        for i in (10, 11):
                            norm.normalise(dve, ch, i)
                        for i in (10, 11):
                            norm.copy(dve, nc.vector.tensor_copy, i)
                    if n == LAST + 5:
                        moe.shift(dve, ch, 0)
                        moe.pick(dve, ch, 0)
                        moe.put(dve, ch, 0)


class SideBanks:

    def __init__(self, psum, banks):
        self.psum, self.banks, self.bank, self.reader, self.uses = psum, banks, {}, [None] * banks, 0

    def take(self, pe, use, read, count):
        n = self.uses % self.banks
        if self.reader[n] is not None:
            pe.wait_ge(*self.reader[n])
        self.bank[use], self.reader[n], self.uses = n, (read, count), self.uses + 1
        return self.psum[:, n, :]

    def of(self, use):
        return self.psum[:, self.bank[use], :]


class Norm:

    def __init__(self, core, name, ctx, xn, xT, side, groups):
        self.core, self.xn, self.xT, self.side, self.groups = core, xn, xT, side, groups
        small = lambda n, shape: core.sb(f"{name}_{n}", shape, ctx=ctx)
        self.stats, self.mv = small("stats", [P, TILES, 6]), small("mv", [P, TILES, 2])
        self.std, self.rstd, self.root_work = (small(n, [P, TILES]) for n in ("std", "rstd", "root_work"))
        self.inverted = set()
        sem = lambda n: core.sem(f"{name}_{n}")
        self.aggregated, self.rooted = sem("aggregated"), sem("rooted")
        self.normed, self.turned, self.ready = sem("normed"), sem("turned"), sem("ready")

    def tiles(self, i):
        return slice(self.groups[i] * GROUP, (self.groups[i] + 1) * GROUP)

    def stats_of(self, dve, ch, i):
        nc, tiles = self.core.nc, range(TILES)[self.tiles(i)]
        for n in tiles:
            ch.step(nc.vector.bn_stats(self.stats[:, n, :], self.core.x[:, n, :]))
        ch.wait()
        for n in tiles:
            ins = nc.vector.bn_aggr(self.mv[:, n, :], self.stats[:, n, :])
        ins.then_inc(self.aggregated, 1)

    def root(self, act, i):
        act.wait_ge(self.aggregated, i + 1)
        self.core.nc.scalar.activation(self.std[:, self.tiles(i)], self.mv[:, self.tiles(i), 1], ACT.Sqrt,
                                       bias=self.core.eps[:]).then_inc(self.rooted, 1)

    def invert(self, dve, ch, i):
        nc = self.core.nc
        tiles = slice(self.tiles(i).start, self.tiles(i + 1).stop)
        v, t, y = self.std[:, tiles], self.root_work[:, tiles], self.rstd[:, tiles]

        def then(ins):
            ch.step(ins)
            ch.wait()

        dve.wait_ge(self.aggregated, i + 2)
        then(nc.vector.tensor_scalar(v, self.mv[:, tiles, 1], LN_EPS, None, ALU.add))
        then(nc.vector.tensor_scalar(y.bitcast(I32), v.bitcast(I32), -0.5, float(ROOT_GUESS), ALU.mult, ALU.add))
        for step in range(ROOT_STEPS):
            then(nc.vector.tensor_tensor(t, v, y, ALU.mult))
            then(nc.vector.scalar_tensor_tensor(t, t, -0.5, y, ALU.mult, ALU.mult))
            last = nc.vector.scalar_tensor_tensor(y, t, 1.5, y, ALU.add, ALU.mult)
            then(last) if step < ROOT_STEPS - 1 else last.then_inc(self.rooted, 2)
        self.inverted |= {i, i + 1}

    def normalise(self, dve, ch, i):
        nc = self.core.nc
        dve.wait_ge(self.aggregated, i + 1)
        dve.wait_ge(self.rooted, i + 1)
        if i not in self.inverted:
            ch.step(nc.vector.reciprocal(self.rstd[:, self.tiles(i)], self.std[:, self.tiles(i)]))
            ch.wait()
        before = [k for k in range(i) if self.groups[k] == self.groups[i]]
        if before:
            dve.wait_ge(self.turned, before[-1] + 1)
        for n in range(TILES)[self.tiles(i)]:
            ins = nc.vector.tensor_scalar(self.xn(n), self.core.x[:, n, :], self.mv[:, n, 0:1], self.rstd[:, n:n + 1],
                                          ALU.subtract, ALU.mult)
        ins.then_inc(self.normed, 1)

    def turn(self, pe, i):
        pe.wait_ge(self.normed, i + 1)
        bank = self.side.take(pe, ("turn", i), self.ready, i + 1)
        for j, n in enumerate(range(TILES)[self.tiles(i)]):
            ins = self.core.nc.tensor.transpose(bank[:, j * P:(j + 1) * P], self.xn(n), self.core.ident[:])
        ins.then_inc(self.turned, 1)

    def copy(self, eng, copy, i):
        eng.wait_ge(self.turned, i + 1)
        g = self.groups[i]
        copy(self.xT[:, g * GT:(g + 1) * GT], self.side.of(("turn", i))).then_inc(self.ready, 1)


class FfnOfBatch:

    ON_ACT = (True, False, False, True)
    SUMS = (2, 1, 1, 1)
    RING = 4

    @staticmethod
    def semaphores(core):
        return [core.sem(f"ffn_{n}") for n in ("based", "s_done", "s_read", "relu_done", "clipped", "added", "out_done", "out_read")]

    def __init__(self, core, run, first, work):
        self.core, self.run, self.b, self.norm, self.first, self.on_act = core, run, run % B, core.norm, first, self.ON_ACT[run]
        self.s, self.unit = work[:, 0, :], work[:, 2:2 + self.RING, :]
        self.sums = [work[:, at, :] for at in (1, 2 + self.RING)[:self.SUMS[run]]]
        self.steps_before = sum(INNER + n - 1 for n in self.SUMS[:run])
        (self.based, self.s_done, self.s_read, self.relu_done, self.clipped, self.added, self.out_done, self.out_read) = core.ffn_semaphores
        self.units_before = INNER * self.ON_ACT[:run].count(self.on_act)

    def base(self, pool):
        core, tiles = self.core, slice(self.b * TPB, (self.b + 1) * TPB)
        pool.wait_ge(self.norm.normed, self.first + 2)
        pool.wait_ge(core.biases_made, 3)
        core.nc.gpsimd.tensor_tensor(core.x[:, tiles, :], core.x[:, tiles, :], core.bout_half[:].unsqueeze(1).to_broadcast([P, TPB, D]), ALU.add)\
            .then_inc(self.based, 1)
        pool.wait_ge(self.based, self.run + 1)

    def project(self, pe):
        bank = self.norm.side.take(pe, ("s", self.run), self.s_read, self.run + 1)
        pe.wait_ge(self.norm.ready, self.first + 2)
        for half in range(2):
            g = 2 * self.b + half
            ins = self.core.nc.tensor.matmul(bank[M * half:M * half + M, :], self.core.win[:], self.norm.xT[:, g * GT:(g + 1) * GT], start=True, stop=True)
        ins.then_inc(self.s_done, 1)

    def take(self, dve):
        dve.wait_ge(self.s_done, self.run + 1)
        self.core.nc.vector.tensor_copy(self.s, self.norm.side.of(("s", self.run))).then_inc(self.s_read, 1)

    def relu(self, act, h):
        core = self.core
        act.wait_ge(self.s_read, self.run + 1)
        if h >= self.RING:
            act.wait_ge(self.added, self.steps_before + h - self.RING + 1)
        core.nc.scalar.activation(self.unit[:, h % self.RING, :], self.s, ACT.Relu, bias=core.b_pre[:, h:h + 1], scale=core.w1[:, h:h + 1]).then_inc(self.relu_done, 1)

    def add(self, dve, h):
        core, nc = self.core, self.core.nc
        unit = self.unit[:, h % self.RING, :]
        if self.on_act:
            dve.wait_ge(self.relu_done, self.units_before + h + 1)
        else:
            dve.wait_ge(self.s_read, self.run + 1)
            if h >= self.RING:
                dve.wait_ge(self.added, self.steps_before + h - self.RING + 1)
            nc.vector.tensor_scalar(unit, self.s, core.w1[:, h:h + 1], core.minus_b[:, h:h + 1], ALU.mult, ALU.max).then_inc(self.clipped, 1)
            dve.wait_ge(self.clipped, self.units_before + h + 1)
        n = len(self.sums)
        acc = self.sums[h % n]
        if h == 0:
            ins = nc.vector.tensor_scalar(acc, unit, core.w2[:, 0:1], (core.b2 if self.on_act else core.b2_clip)[:], ALU.mult, ALU.add)
        elif h < n:
            ins = nc.vector.tensor_scalar(acc, unit, core.w2[:, h:h + 1], None, ALU.mult)
        else:
            dve.wait_ge(self.added, self.steps_before + h - n + 1)
            ins = nc.vector.scalar_tensor_tensor(acc, unit, core.w2[:, h:h + 1], acc, ALU.mult, ALU.add)
        ins.then_inc(self.added, 1)
        if h == INNER - 1 and n == 2:
            dve.wait_ge(self.added, self.steps_before + INNER)
            nc.vector.tensor_tensor(self.sums[0], self.sums[0], self.sums[1], ALU.add).then_inc(self.added, 1)

    def output(self, pe, half):
        core = self.core
        bank = self.norm.side.take(pe, ("ffn_out", self.run, half), self.out_read, 2 * self.run + half + 1)
        pe.wait_ge(self.added, self.steps_before + INNER + self.SUMS[self.run] - 1)
        for j in range(GROUP):
            ins = core.nc.tensor.matmul(bank[:, j * D:(j + 1) * D], self.sums[0][:, j * P:(j + 1) * P], core.wout[:, half, :], start=True, stop=True)
        ins.then_inc(self.out_done, 1)

    def finish(self, dve, half):
        core, n0 = self.core, self.b * TPB + half * GROUP
        dve.wait_ge(self.out_done, 2 * self.run + half + 1)
        dve.wait_ge(self.based, self.run + 1)
        x = core.x[:, n0:n0 + GROUP, :].rearrange("p a d -> p (a d)")
        core.nc.vector.scalar_tensor_tensor(x, self.norm.side.of(("ffn_out", self.run, half)), 0.5, x, ALU.mult, ALU.add).then_inc(self.out_read, 1)
        dve.wait_ge(self.out_read, 2 * self.run + half + 1)


class Moe:

    PROB, TOKEN, FIRST, ROW = D, D + E_, D + E_ + 1, D + E_ + 2
    NOWHERE = float(16 * T)
    RING = 3

    REST_ROWS = slice(FCR, 2 * FCR)

    def __init__(self, core):
        nc, d = core.nc, core.dram
        self.core = core
        self.w1, self.w3 = core.sb("moe_w1", [D, E_, FCF * P]), core.sb("moe_w3", [D, E_, FCF * P])
        self.w_rest = core.sb("moe_w_rest", [D, E_, 2 * FCR])
        self.w2 = core.sb("moe_w2", [P, E_, FCH, D])
        self.gate = core.sb("moe_gate", [D, E_])
        self.iota = core.sb("moe_iota", [P, E_])
        self.token = core.sb("moe_token", [P, TPB])
        self.tri = core.sb("moe_tri", [P, 2, P], BF16)
        per_batch = lambda n, rows, cols: [nc.dram_tensor(f"moe_{n}{i}", (rows, cols), F32).ap() for i in range(2 * B)]
        self.slots, self.rows = per_batch("slots", SLOTS, self.ROW), per_batch("rows", TOPK * T, D)
        self.loads = [("moe_gate", self.gate[:], d["gate"]), ("moe_iota", self.iota[:], d["expert_iota"].to_broadcast([P, E_])),
                      ("moe_token", self.token[:], d["token"]),
                      ("moe_w1", self.w1[:], d["w1"]), ("moe_w3", self.w3[:], d["w3"]),
                      ("moe_w1_rest", self.w_rest[:, :, 0:FCR], d["w1_rest"]), ("moe_w3_rest", self.w_rest[:, :, FCR:2 * FCR], d["w3_rest"]),
                      ("moe_w2", self.w2[:, :, 0:FCF, :].rearrange("p e c d -> p e (c d)"), d["w2"].rearrange("p e c d -> p e (c d)")),
                      ("moe_w2_rest", self.w2[self.REST_ROWS, :, FCF, :], d["w2_rest"])]
        core.await_together("routing", self.loads[:3])
        core.await_together("experts", self.loads[3:])
        self.cleared = core.sem("moe_cleared")

    def open_routing(self, ctx, name, rows, xT, norm):
        core = self.core
        self.row_of, self.xT, self.norm = rows, xT, norm
        sb = lambda n, shape, dt=F32: core.sb(f"{name}_{n}", shape, dt, ctx)
        sem = lambda n: core.sem(f"{name}_{n}")
        NT = TPB
        self.e0, self.e1, self.pr = sb("e0", [P, NT, E_]), sb("e1", [P, NT, E_]), sb("pr", [P, NT, E_])
        self.mx, self.den, self.rden = sb("mx", [P, NT]), sb("den", [P, NT]), sb("rden", [P, NT])
        self.top, self.at, self.atf = sb("top", [P, NT, 8]), sb("at", [P, NT, 8], U32), sb("atf", [P, TOPK, NT])
        self.hot, self.tmp = sb("hot", [P, TOPK, NT, E_]), sb("tmp", [P, TOPK, NT, E_])
        self.picked = sb("picked", [P, NT, E_], BF16)
        self.mine, self.place, self.over = (sb(n, [P, TOPK, NT]) for n in ("mine", "place", "over"))
        self.scatter_at = sb("scatter_at", [P, B, TOPK, NT], U32)
        (self.logits_done, self.shifted, self.exped, self.picked_done, self.counted, self.placed, self.routed) = (
            sem(n) for n in ("logits_done", "shifted", "exped", "picked_done", "counted", "placed", "routed"))
        self.scattered = [sem(f"scattered{b}") for b in range(B)]

    def open(self, ctx, name, main):
        core = self.core
        sb = lambda n, shape, dt=F32: core.sb(f"{name}_{n}", shape, dt, ctx)
        sem = lambda n: core.sem(f"{name}_{n}", ctx)
        self.xs, self.xsT = sb("xs", [P, self.RING, 3, self.ROW]), sb("xsT", [D, 2, CAP])
        self.act_h, self.hid = sb("act_h", [P, 2, CAP]), sb("hid", [P, 2, FCH, CAP])
        own = sb("y", [P, self.OUT // 2, 3, D])
        self.y = [own[:, i, :, :] for i in range(self.OUT // 2)]
        self.second, self.dest, self.weight = (sb(n, [P, self.OUT, 3], dt) for n, dt in (("second", F32), ("dest", U32), ("weight", F32)))
        self.back = sb("back", [P, TOPK, TPB, D])
        self.ps_t, self.ps_h1, self.ps_h3, self.ps_y = main[:, 0, :], main[:, 1:3, :], main[:, 3:5, :], main[:, 5, :]
        self.tail_clear, self.chain = sem("tail_clear"), sem("chain")
        self.slots_in = [sem(f"slots_in{i}") for i in range(self.RING)]
        self.y_out = [sem(f"y_out{i}") for i in range(self.OUT)]
        self.back_in = [sem(f"back_in{i}") for i in range(2)]
        (self.turned, self.t_read, self.h_done, self.silu_done, self.gated, self.y_done, self.y_read, self.sent, self.combined) = (
            sem(n) for n in ("turned", "t_read", "h_done", "silu_done", "gated", "y_done", "y_read", "sent", "combined"))

    OUT = 4
    UNITS = 2 * B * E_
    FULL = CAP // P
    REST = CAP - FULL * P
    CHUNKS = [(s * P, min(P, CAP - s * P)) for s in range(FULL + 1)]


    def logits(self, pe, r):
        nc, b = self.core.nc, r % B
        bank = self.norm.side.take(pe, ("logits", r), self.shifted, r + 1)
        for j in range(TPB):
            n = b * TPB + j
            ins = nc.tensor.matmul(bank[:, j * E_:(j + 1) * E_], self.xT[:, n * P:(n + 1) * P], self.gate[:], start=True, stop=True)
        ins.then_inc(self.logits_done, 1)

    def counts(self, pe, r):
        pe.wait_ge(self.picked_done, r + 1)
        bank = self.norm.side.take(pe, ("counts", r), self.placed, r + 1)
        for step in range(TPB):
            ins = self.core.nc.tensor.matmul(bank[:, step * E_:TPB * E_], self.tri[:, min(step, 1), :],
                                             self.picked[:, 0:TPB - step, :].rearrange("p j e -> p (j e)"),
                                             start=(step == 0), stop=(step == TPB - 1))
        ins.then_inc(self.counted, 1)

    def shift(self, dve, ch, r):
        nc = self.core.nc
        dve.wait_ge(self.logits_done, r + 1)
        logits = self.norm.side.of(("logits", r))[:, 0:TPB * E_].rearrange("p (j e) -> p j e", e=E_)
        ch.step(nc.vector.reduce_max(self.mx[:], logits, AX_X))
        ch.wait()
        nc.vector.tensor_tensor(self.e0[:], logits, self.mx[:].unsqueeze(2).to_broadcast([P, TPB, E_]), ALU.subtract).then_inc(self.shifted, 1)

    def exp(self, act, r):
        act.wait_ge(self.shifted, r + 1)
        self.core.nc.scalar.activation(self.e1[:], self.e0[:], ACT.Exp).then_inc(self.exped, 1)

    def pick(self, dve, ch, r):
        nc, b = self.core.nc, r % B
        over_e = lambda v: v.unsqueeze(2).to_broadcast([P, TPB, E_])
        tiles = slice(b * TPB, (b + 1) * TPB)

        def then(ins):
            ch.step(ins)
            ch.wait()

        dve.wait_ge(self.exped, r + 1)
        then(nc.vector.reduce_sum(self.den[:], self.e1[:], AX_X))
        then(nc.vector.reciprocal(self.rden[:], self.den[:]))
        then(nc.vector.tensor_tensor(self.pr[:], self.e1[:], over_e(self.rden[:]), ALU.mult))
        for j in range(TPB):
            ch.step(nc.vector.max(self.top[:, j, :], self.pr[:, j, :]))
        ch.wait()
        for j in range(TPB):
            ch.step(nc.vector.max_index(self.at[:, j, :], self.top[:, j, :], self.pr[:, j, :]))
        ch.wait()
        then(nc.vector.tensor_copy(self.atf[:].rearrange("p k j -> p j k"), self.at[:, :, 0:TOPK]))
        for k in range(TOPK):
            ch.step(nc.vector.tensor_tensor(self.hot[:, k, :, :], self.iota[:].unsqueeze(1).to_broadcast([P, TPB, E_]),
                                            over_e(self.atf[:, k, :]), ALU.is_equal))
        ch.wait()
        nc.vector.tensor_tensor(self.picked[:], self.hot[:, 0, :, :], self.hot[:, 1, :, :], ALU.add).then_inc(self.picked_done, 1)
        ch.step(nc.vector.tensor_scalar(self.row_of[:, tiles, self.PROB:self.PROB + E_], self.pr[:], 0.5, None, ALU.mult))
        ch.step(nc.vector.tensor_copy(self.row_of[:, tiles, self.FIRST], self.atf[:, 0, :]))

    def put(self, dve, ch, r):
        nc, b = self.core.nc, r % B

        def then(ins):
            ch.step(ins)
            ch.wait()

        dve.wait_ge(self.counted, r + 1)
        seen = self.norm.side.of(("counts", r))[:, 0:TPB * E_].rearrange("p (j e) -> p j e", e=E_)
        ch.step(nc.vector.tensor_tensor(self.tmp[:, 0, :, :], self.hot[:, 0, :, :], seen, ALU.mult))
        nc.vector.tensor_tensor(self.tmp[:, 1, :, :], self.hot[:, 1, :, :], seen, ALU.mult).then_inc(self.placed, 1)
        ch.wait()
        dve.wait_ge(self.placed, r + 1)
        then(nc.vector.reduce_sum(self.mine[:], self.tmp[:], AX_X))
        ch.step(nc.vector.scalar_tensor_tensor(self.place[:], self.atf[:], float(CAP), self.mine[:], ALU.mult, ALU.add))
        then(nc.vector.tensor_scalar(self.over[:], self.mine[:], float(CAP), float(4 * SLOTS), ALU.is_gt, ALU.mult))
        nc.vector.scalar_tensor_tensor(self.scatter_at[:, b, :, :], self.place[:], -1.0, self.over[:], ALU.add, ALU.add)\
          .then_inc(self.routed, 1)

    def scatter(self, pool, r, first=0, last=TOPK * TPB):
        nc, b = self.core.nc, r % B
        if first == 0:
            pool.wait_ge(self.routed, r + 1)
        for n in range(first, last):
            k, j = n // TPB, n % TPB
            nc.gpsimd.indirect_dma_start(self.slots[r], bass.IndirectOffsetOnAxis(self.scatter_at[:, b, k, j:j + 1], 0),
                                         self.row_of[:, b * TPB + j, :], None, bounds_check=SLOTS - 1, oob_is_err=False)\
              .then_inc(self.scattered[b], 16)


    def load(self, sp, u):
        r, e = u // E_, u % E_
        if e == 0:
            sp.wait_ge(self.scattered[r % B], 16 * TOPK * TPB * (r // B + 1))
        if u == 0:
            sp.wait_ge(self.tail_clear, 1)
        if u >= self.RING:
            sp.wait_ge(self.turned, u - self.RING + 1)
            sp.wait_ge(self.sent, u - self.RING + 1)
        src, r0 = self.slots[r], e * CAP
        sp.dma_start(self.xs[:, u % self.RING, 0:self.FULL, :], src[r0:r0 + self.FULL * P, :].rearrange("(s p) d -> p s d", p=P))\
          .then_inc(self.slots_in[u % self.RING], 16)
        sp.dma_start(self.xs[0:self.REST, u % self.RING, self.FULL, :], src[r0 + self.FULL * P:r0 + CAP, :])\
          .then_inc(self.slots_in[u % self.RING], 16)

    def loaded(self, eng, u):
        eng.wait_ge(self.slots_in[u % self.RING], 32 * (u // self.RING + 1))

    def turn(self, pe, u):
        self.loaded(pe, u)
        if u >= 1:
            pe.wait_ge(self.t_read, u)
        for s, (c0, n) in enumerate(self.CHUNKS):
            ins = self.core.nc.tensor.transpose(self.ps_t[:, c0:c0 + n], self.xs[0:n, u % self.RING, s, 0:D], self.core.ident[0:n, 0:n])
        ins.then_inc(self.turned, 1)

    def take(self, dve, u):
        nc = self.core.nc
        dve.wait_ge(self.turned, u + 1)
        if u >= 2:
            dve.wait_ge(self.h_done, 2 * FCH * (u - 1))
        nc.vector.tensor_copy(self.xsT[:, u % 2, :], self.ps_t[:, 0:CAP]).then_inc(self.t_read, 1)

    def address(self, dve, u):
        nc, e = self.core.nc, u % E_
        self.loaded(dve, u)
        at = u % self.OUT
        if u >= self.OUT:
            dve.wait_ge(self.y_out[at], 48 * (u // self.OUT))
        row = self.xs[:, u % self.RING, :, :]
        nc.vector.tensor_scalar(self.second[:, at, :], row[:, :, self.FIRST], float(e), float(T), ALU.not_equal, ALU.mult).then_inc(self.chain, 1)
        nc.vector.tensor_copy(self.weight[:, at, :], row[:, :, self.PROB + e]).then_inc(self.chain, 1)
        dve.wait_ge(self.chain, 2 * u + 2)
        nc.vector.tensor_tensor(self.dest[:, at, :], self.second[:, at, :], row[:, :, self.TOKEN], ALU.add).then_inc(self.sent, 1)

    def hidden(self, pe, u, chunks=range(FCH)):
        e = u % E_
        pe.wait_ge(self.t_read, u + 1)
        for c in chunks:
            w = u * FCH + c
            if w >= 2:
                pe.wait_ge(self.gated, w - 1)
            if c == FCF:
                self.core.nc.tensor.matmul(self.ps_h1[:, w % 2, 0:CAP], self.w_rest[:, e, :], self.xsT[:, u % 2, :], start=True, stop=True)\
                    .then_inc(self.h_done, 2)
                continue
            for ps, wt in ((self.ps_h1, self.w1), (self.ps_h3, self.w3)):
                self.core.nc.tensor.matmul(ps[:, w % 2, 0:CAP], wt[:, e, c * P:(c + 1) * P], self.xsT[:, u % 2, :],
                                           start=True, stop=True).then_inc(self.h_done, 1)

    def silu(self, act, u, chunks=range(FCH)):
        for c in chunks:
            w = u * FCH + c
            act.wait_ge(self.h_done, 2 * w + 1)
            if w >= 2:
                act.wait_ge(self.gated, w - 1)
            rows, into = (slice(0, P), slice(0, P)) if c < FCF else (slice(0, FCR), self.REST_ROWS)
            self.core.nc.scalar.activation(self.act_h[into, w % 2, :], self.ps_h1[rows, w % 2, 0:CAP], ACT.Silu).then_inc(self.silu_done, 1)

    def gating(self, dve, u, chunks=range(FCH)):
        for c in chunks:
            w = u * FCH + c
            dve.wait_ge(self.silu_done, w + 1)
            dve.wait_ge(self.h_done, 2 * (w + 1))
            if u >= 2 and c == 0:
                dve.wait_ge(self.y_done, u - 1)
            rows, bank = (slice(0, P), self.ps_h3) if c < FCF else (self.REST_ROWS, self.ps_h1)
            self.core.nc.vector.tensor_tensor(self.hid[rows, u % 2, c, :], self.act_h[rows, w % 2, :], bank[rows, w % 2, 0:CAP], ALU.mult)\
                .then_inc(self.gated, 1)

    def results(self, pe, u):
        pe.wait_ge(self.gated, FCH * (u + 1))
        if u >= 1:
            pe.wait_ge(self.y_read, 3 * u)
        for s, (c0, n) in enumerate(self.CHUNKS):
            for c in range(FCH):
                rows = slice(0, P) if c < FCF else self.REST_ROWS
                ins = self.core.nc.tensor.matmul(self.ps_y[0:n, s * D:(s + 1) * D], self.hid[rows, u % 2, c, c0:c0 + n], self.w2[rows, u % E_, c, :],
                                                 start=(c == 0), stop=(c == FCH - 1))
        ins.then_inc(self.y_done, 1)

    def weigh(self, act, u):
        act.wait_ge(self.y_done, u + 1)
        act.wait_ge(self.sent, u + 1)
        for s, (c0, n) in enumerate(self.CHUNKS):
            self.core.nc.scalar.activation(self.y[u % self.OUT][0:n, s, :], self.ps_y[0:n, s * D:(s + 1) * D], ACT.Copy,
                                           scale=self.weight[0:n, u % self.OUT, s:s + 1]).then_inc(self.y_read, 1)

    def send(self, pool, u):
        pool.wait_ge(self.y_read, 3 * (u + 1))
        pool.wait_ge(self.sent, u + 1)
        for s, (c0, n) in enumerate(self.CHUNKS):
            self.core.nc.gpsimd.indirect_dma_start(self.rows[u // E_], bass.IndirectOffsetOnAxis(self.dest[0:n, u % self.OUT, s:s + 1], 0),
                                                   self.y[u % self.OUT][0:n, s, :], None, bounds_check=TOPK * T - 1, oob_is_err=False)\
                .then_inc(self.y_out[u % self.OUT], 16)

    def fetch(self, sp, r):
        for i in range(self.OUT):
            sp.wait_ge(self.y_out[i], 48 * E_ // self.OUT * (r + 1))
        if r >= 1:
            sp.wait_ge(self.combined, 2 * r)
        src = self.rows[r].rearrange("(k j p) d -> p k j d", k=TOPK, p=P)
        for half in range(2):
            tiles = slice(half * GROUP, (half + 1) * GROUP)
            for k in range(TOPK):
                sp.dma_start(self.back[:, k, tiles, :], src[:, k, tiles, :]).then_inc(self.back_in[half], 16)

    def combine(self, dve, ch, r, half):
        nc, n0 = self.core.nc, r % B * TPB + half * GROUP
        dve.wait_ge(self.back_in[half], 16 * TOPK * (r + 1))
        x, back = self.core.x[:, n0:n0 + GROUP, :], self.back[:, :, half * GROUP:(half + 1) * GROUP, :]
        ch.step(nc.vector.tensor_tensor(x, x, back[:, 0, :, :], ALU.add))
        ch.wait()
        nc.vector.tensor_tensor(x, x, back[:, 1, :, :], ALU.add).then_inc(self.combined, 1)
        dve.wait_ge(self.combined, 2 * r + half + 1)


class Mamba:

    UNITS = [(di, b) for b in range(B) for di in range(2)]
    NC = TPB
    N = len(UNITS) * NC
    PIECES = 6
    LOG_TERMS = 8
    PARTS_OUT = [range(0, 3), range(3, 6), range(6, 8)]
    PIECES_AT = [(0,), (1,), (), (2,), (3,), (), (4, 5), ()]
    TAPS_AT = [((0, 1), (0, 2)), ((0, 3), (1, 1)), ((1, 2),), ((1, 3),), ((2, 1), (2, 2), (2, 3)), ((3, 1), (3, 2), (3, 3)), (), ()]

    def __init__(self, core):
        d = core.dram
        self.core = core
        sb = core.sb
        self.w_xbc, self.w_z, self.w_dt = sb("mb_w_xbc", [D, 2, 4, P]), sb("mb_w_z", [D, 2, 2, P]), sb("mb_w_dt", [D, 2 * NH])
        self.taps, self.conv_b = sb("mb_taps", [P, 2, 4, TAPS]), sb("mb_conv_b", [P, 2, 4])
        self.skip, self.norm_w, self.wo = sb("mb_skip", [P, 2, 2]), sb("mb_norm_w", [P, 2, 2]), sb("mb_wo", [P, 2, 2, D])
        self.dt_bias, self.a_log = sb("mb_dt_bias", [P, 2 * NH]), sb("mb_a_log", [P, 2 * NH])
        self.loads = [("mb_w_xbc", self.w_xbc[:], d["mb_w_xbc"]), ("mb_w_z", self.w_z[:], d["mb_w_z"]), ("mb_w_dt", self.w_dt[:], d["mb_w_dt"]),
                      ("mb_taps", self.taps[:], d["mb_taps"]), ("mb_conv_b", self.conv_b[:], d["mb_conv_b"]),
                      ("mb_skip", self.skip[:], d["mb_skip"]), ("mb_norm_w", self.norm_w[:], d["mb_norm_w"]), ("mb_wo", self.wo[:], d["mb_wo"]),
                      ("mb_dt_bias", self.dt_bias[:], d["mb_dt_bias"].to_broadcast([P, 2 * NH])),
                      ("mb_a_log", self.a_log[:], d["mb_a_log"].to_broadcast([P, 2 * NH]))]
        core.await_together("mamba", self.loads)

    def open(self, ctx, name, xT, side, main):
        core = self.core
        self.xT, self.side = xT, side
        sb = lambda n, shape, dt=F32: core.sb(f"{name}_{n}", shape, dt, ctx)
        sem = lambda n: core.sem(f"{name}_{n}", ctx)
        XP = T + 2 * (TAPS - 1)
        self.padded = sb("padded", [P, 2, XP])
        self.act_t = sb("act", [P, 2, 4, T])
        self.z = sb("z", [P, 2, 2, T])
        self.strict, self.incl, self.ones = sb("strict", [P, 2, P]), sb("incl", [P, 2, P]), sb("ones", [P, P])
        small = lambda n: sb(n, [P, TILES, 2 * NH])
        self.dt, self.a, self.whole = small("dt"), small("a"), small("whole")
        self.v, self.ab, self.ex, self.sq, self.poly = (sb(n, [P, TPB, 2 * NH]) for n in ("v", "ab", "ex", "sq", "poly"))
        self.a_exp, self.to_end = sb("a_exp", [P, 2 * NH]), sb("to_end", [P, 2, TILES, NH])
        self.cut, self.e_seg, self.mt = (sb(n, [P, 2, NH, P]) for n in ("cut", "e_seg", "mt"))
        self.e_cum, self.gm, self.bs = sb("e_cum", [P, 2, 2, P]), sb("gm", [P, 2, P]), sb("bs", [P, 2, 2 * P])
        self.xdt, self.xw, self.h, self.h_dec = sb("xdt", [P, 2, DIN]), sb("xw", [P, 2, DIN]), sb("h", [P, 2, DIN]), sb("h_dec", [P, DIN])
        self.y_in, self.y_old, self.y2 = sb("y_in", [P, 2, 2, P]), sb("y_old", [P, 2, 2, P]), sb("y2", [P, 2, 2, P])
        self.var, self.std, self.rstd = (sb(n, [P, self.NC]) for n in ("var", "std", "rstd"))
        self.ps_seg, self.ps_cb, self.ps_x, self.ps_y, self.ps_st, self.ps_o = (main[:, i, :] for i in range(6))
        (self.masks, self.pads, self.dt_done, self.dt_in, self.dt_exp, self.a_exped, self.a_done, self.sums_done, self.decays, self.norm_done) = (
            sem(n) for n in ("masks", "pads", "dt_done", "dt_in", "dt_exp", "a_exped", "a_done", "sums_done", "decays", "norm_done"))
        self.proj_done, self.proj_read, self.tapped, self.conv_done, self.act_ready = (
            sem(n) for n in ("proj_done", "proj_read", "tapped", "conv_done", "act_ready"))
        (self.cut_done, self.seg_done, self.cb_done, self.x_done, self.y_done, self.st_done, self.seg_exp, self.cb_read, self.x_read) = (
            sem(n) for n in ("cut_done", "seg_done", "cb_done", "x_done", "y_done", "st_done", "seg_exp", "cb_read", "x_read"))
        (self.gm_done, self.mt_done, self.xw_done, self.h_decayed, self.h_ready, self.y_read, self.y_sum, self.gate_done) = (
            sem(n) for n in ("gm_done", "mt_done", "xw_done", "h_decayed", "h_ready", "y_read", "y_sum", "gate_done"))
        (self.squared, self.ss_done, self.ss_read, self.std_done, self.rms_done, self.out_done, self.out_read) = (
            sem(n) for n in ("squared", "ss_done", "ss_read", "std_done", "rms_done", "out_done", "out_read"))

    def at(self, g):
        u, i = g // self.NC, g % self.NC
        di, b = self.UNITS[u]
        j = i if di == 0 else self.NC - 1 - i
        return u, di, b, i, b * TPB + j, slice(j * P, (j + 1) * P)

    def carried(self, g):
        return (g // self.NC) * (self.NC - 1) + g % self.NC

    def passed(self, g):
        return (g // self.NC) * (self.NC - 1) + min(g % self.NC + 1, self.NC - 1)

    def passes_on(self, g):
        return g % self.NC < self.NC - 1


    def make_masks(self, pool):
        nc = self.core.nc
        for m in (self.ones, self.strict, self.incl):
            nc.gpsimd.memset(m[:], 1.0).then_inc(self.masks, 1)
        nc.gpsimd.memset(self.padded[:], 0.0).then_inc(self.pads, 1)
        pool.wait_ge(self.masks, 3)
        for m, di, op, sign in ((self.strict, 0, ALU.is_gt, 1), (self.strict, 1, ALU.is_gt, -1), (self.incl, 0, ALU.is_ge, -1), (self.incl, 1, ALU.is_ge, 1)):
            nc.gpsimd.affine_select(out=m[:, di, :], in_=m[:, di, :], compare_op=op, fill=0.0, base=0,
                                    pattern=[[-sign, P]], channel_multiplier=sign).then_inc(self.masks, 1)
        pool.wait_ge(self.masks, 7)

    def steps(self, pe, b):
        bank = self.side.take(pe, ("dt", b), self.dt_in, b + 1)
        for j in range(TPB):
            n = b * TPB + j
            ins = self.core.nc.tensor.matmul(bank[:, j * 2 * NH:(j + 1) * 2 * NH], self.xT[:, n * P:(n + 1) * P], self.w_dt[:], start=True, stop=True)
        ins.then_inc(self.dt_done, 1)

    def sums(self, pe, b):
        nc, tiles = self.core.nc, slice(b * TPB, (b + 1) * TPB)
        pe.wait_ge(self.a_done, b + 1)
        pe.wait_ge(self.masks, 7)
        bank = self.side.take(pe, ("sums", b), self.decays, 3 * (b + 1))
        n = TPB * NH
        for di in range(2):
            nc.tensor.matmul(bank[:, di * n:(di + 1) * n], self.strict[:, di, :], self.a[:, tiles, di * NH:(di + 1) * NH], start=True, stop=True)
        nc.tensor.matmul(bank[:, 2 * n:4 * n], self.ones[:], self.a[:, tiles, :], start=True, stop=True).then_inc(self.sums_done, 1)

    def exp_a(self, act):
        self.core.landed(act, "mb_a_log", "mb_conv_b")
        self.core.nc.scalar.activation(self.a_exp[:], self.a_log[:], ACT.Exp).then_inc(self.a_exped, 1)

    def exp_dt(self, act, b):
        act.wait_ge(self.dt_in, b + 1)
        self.core.nc.scalar.activation(self.ex[:], self.ab[:], ACT.Exp, scale=-1.0).then_inc(self.dt_exp, 1)

    def exp_sums(self, act, b):
        nc, tiles, n = self.core.nc, slice(b * TPB, (b + 1) * TPB), TPB * NH
        act.wait_ge(self.sums_done, b + 1)
        bank = self.side.of(("sums", b))
        for di in range(2):
            nc.scalar.activation(self.to_end[:, di, tiles, :], bank[:, di * n:(di + 1) * n].rearrange("p (j h) -> p j h", h=NH), ACT.Exp)\
              .then_inc(self.decays, 1)
        nc.scalar.activation(self.whole[:, tiles, :], bank[:, 2 * n:4 * n].rearrange("p (j h) -> p j h", h=2 * NH), ACT.Exp).then_inc(self.decays, 1)

    def weigh_out(self, dve):
        self.core.landed(dve, "mb_norm_w", "mb_wo", "mb_dt_bias", "mb_taps", "mb_skip")
        for di in range(2):
            for c in range(2):
                ins = self.core.nc.vector.tensor_scalar(self.wo[:, di, c, :], self.wo[:, di, c, :], self.norm_w[:, di, c:c + 1], None, ALU.mult)
        ins.then_inc(self.norm_done, 1)

    STEP_PARTS = 4

    def step_sizes(self, dve, ch, b, part):
        nc, tiles, every = self.core.nc, slice(b * TPB, (b + 1) * TPB), [P, TPB, 2 * NH]
        v, ab, ex, sq, poly = self.v, self.ab, self.ex, self.sq, self.poly
        middle = self.LOG_TERMS // 2

        def then(ins):
            ch.step(ins)
            ch.wait()

        def series(terms):
            for k in terms:
                then(nc.vector.scalar_tensor_tensor(poly[:], poly[:], 1.0 / (2 * k + 1), sq[:], ALU.add, ALU.mult))

        if part == 0:
            dve.wait_ge(self.dt_done, b + 1)
            then(nc.vector.tensor_tensor(v[:], self.side.of(("dt", b))[:, 0:TPB * 2 * NH].rearrange("p (j h) -> p j h", h=2 * NH),
                                         self.dt_bias[:].unsqueeze(1).to_broadcast(every), ALU.add))
            nc.vector.scalar_tensor_tensor(ab[:], v[:], -1.0, v[:], ALU.mult, ALU.max).then_inc(self.dt_in, 1)
        if part == 1:
            dve.wait_ge(self.dt_exp, b + 1)
            then(nc.vector.tensor_scalar(poly[:], ex[:], 2.0, None, ALU.add))
            then(nc.vector.reciprocal(poly[:], poly[:]))
            then(nc.vector.tensor_tensor(ex[:], ex[:], poly[:], ALU.mult))
            then(nc.vector.tensor_tensor(sq[:], ex[:], ex[:], ALU.mult))
            then(nc.vector.tensor_scalar(poly[:], sq[:], 1.0 / (2 * self.LOG_TERMS + 1), None, ALU.mult))
        if part == 2:
            series(range(self.LOG_TERMS - 1, middle - 1, -1))
        if part == 3:
            series(range(middle - 1, 0, -1))
            then(nc.vector.scalar_tensor_tensor(poly[:], poly[:], 1.0, ex[:], ALU.add, ALU.mult))
            then(nc.vector.tensor_scalar(v[:], v[:], 0.0, None, ALU.max))
            then(nc.vector.scalar_tensor_tensor(self.dt[:, tiles, :], poly[:], 2.0, v[:], ALU.mult, ALU.add))
            dve.wait_ge(self.a_exped, 1)
            nc.vector.scalar_tensor_tensor(self.a[:, tiles, :], self.dt[:, tiles, :], -1.0, self.a_exp[:].unsqueeze(1).to_broadcast(every), ALU.mult, ALU.mult)\
              .then_inc(self.a_done, 1)


    def project(self, pe, u, c):
        di, b = self.UNITS[u]
        weight = self.w_xbc[:, di, c, :] if c < 4 else self.w_z[:, di, c - 4, :]
        for half in range(2):
            w = (u * self.PIECES + c) * 2 + half
            bank = self.side.take(pe, ("proj", w), self.proj_read, w + 1)
            t0 = b * T + half * BANK
            self.core.nc.tensor.matmul(bank[:], weight, self.xT[:, t0:t0 + BANK], start=True, stop=True).then_inc(self.proj_done, 1)

    def take(self, act, u, c):
        if c < 4:
            if u >= 1 or c >= 2:
                act.wait_ge(self.conv_done, 4 * u + c - 1)
        elif u >= 2:
            act.wait_ge(self.out_done, len(self.PARTS_OUT) * (u - 1))
        for half in range(2):
            w = (u * self.PIECES + c) * 2 + half
            act.wait_ge(self.proj_done, w + 1)
            t0 = half * BANK
            dst = self.padded[:, c % 2, TAPS - 1 + t0:TAPS - 1 + t0 + BANK] if c < 4 else self.z[:, u % 2, c - 4, t0:t0 + BANK]
            self.core.nc.scalar.activation(dst, self.side.of(("proj", w)), ACT.Copy if c < 4 else ACT.Silu).then_inc(self.proj_read, 1)

    def window(self, u, c, k):
        di, b = self.UNITS[u]
        t0 = k if di == 0 else 2 * (TAPS - 1) - k
        return self.padded[:, c % 2, t0:t0 + T], self.taps[:, di, c, k:k + 1]

    def first_tap(self, act, u, c):
        src, tap = self.window(u, c, 0)
        act.wait_ge(self.proj_read, (u * self.PIECES + c) * 2 + 2)
        if u >= 2:
            act.wait_ge(self.y_read, self.NC * (u - 1))
        self.core.nc.scalar.activation(self.act_t[:, u % 2, c, :], src, ACT.Copy, scale=tap).then_inc(self.tapped, 1)

    def convolve(self, dve, ch, u, c, k):
        (src, tap), out = self.window(u, c, k), self.act_t[:, u % 2, c, :]
        if k == 1:
            dve.wait_ge(self.tapped, 4 * u + c + 1)
        else:
            ch.wait()
        ins = self.core.nc.vector.scalar_tensor_tensor(out, src, tap, out, ALU.mult, ALU.add)
        ch.step(ins) if k < TAPS - 1 else ins.then_inc(self.conv_done, 1)

    def silu_rows(self, act, u, tiles=range(4)):
        di, b = self.UNITS[u]
        for c in tiles:
            act.wait_ge(self.conv_done, 4 * u + c + 1)
            self.core.nc.scalar.activation(self.act_t[:, u % 2, c, :], self.act_t[:, u % 2, c, :], ACT.Silu, bias=self.conv_b[:, di, c:c + 1])\
                .then_inc(self.act_ready, 1)


    def cut_a(self, pool, g):
        u, di, b, i, n, cols = self.at(g)
        pool.wait_ge(self.a_done, b + 1)
        if g >= 2:
            pool.wait_ge(self.seg_done, g - 1)
        self.core.nc.gpsimd.tensor_tensor(self.cut[:, g % 2, :, :], self.strict[:, di, :].unsqueeze(1).to_broadcast([P, NH, P]),
                                          self.a[:, n, di * NH:(di + 1) * NH].unsqueeze(2).to_broadcast([P, NH, P]), ALU.mult)\
            .then_inc(self.cut_done, 1)

    def before(self, pe, g):
        nc = self.core.nc
        u, di, b, i, n, cols = self.at(g)
        act = self.act_t[:, u % 2, :, :]
        pe.wait_ge(self.cut_done, g + 1)
        if g >= 1:
            pe.wait_ge(self.seg_exp, g)
        for hh in range(NH):
            ins = nc.tensor.matmul(self.ps_seg[:, hh * P:(hh + 1) * P], self.cut[:, g % 2, hh, :], self.incl[:, di, :], start=True, stop=True)
        ins.then_inc(self.seg_done, 1)
        pe.wait_ge(self.act_ready, 4 * (u + 1))
        if g >= 1:
            pe.wait_ge(self.x_read, g)
        for c in range(2):
            ins = nc.tensor.transpose(self.ps_x[:, c * P:(c + 1) * P], act[:, c, cols], self.core.ident[:])
        ins.then_inc(self.x_done, 1)
        if g >= 1:
            pe.wait_ge(self.cb_read, g)
        if i:
            for hh in range(NH):
                nc.tensor.matmul(self.ps_cb[HP * (hh % 2):HP * (hh % 2) + HP, hh // 2 * P:hh // 2 * P + P],
                                 self.a[:, n, di * NH + hh:di * NH + hh + 1].to_broadcast([P, HP]), self.incl[:, di, :], start=True, stop=True)
        nc.tensor.transpose(self.ps_cb[:, 2 * P:3 * P], act[:, 2, cols], self.core.ident[:])
        nc.tensor.matmul(self.ps_cb[:, 3 * P:4 * P], act[:, 2, cols], act[:, 3, cols], start=True, stop=True).then_inc(self.cb_done, 1)

    def exps(self, act, g):
        nc = self.core.nc
        u, di, b, i, n, cols = self.at(g)
        act.wait_ge(self.seg_done, g + 1)
        if g >= 2:
            act.wait_ge(self.mt_done, g - 1)
        nc.scalar.activation(self.e_seg[:, g % 2, :, :], self.ps_seg.rearrange("p (h t) -> p h t", h=NH), ACT.Exp).then_inc(self.seg_exp, 1)
        act.wait_ge(self.cb_done, g + 1)
        if g >= 2:
            act.wait_ge(self.y_read, g - 1)
            act.wait_ge(self.st_done, self.passed(g - 2))
            act.wait_ge(self.gm_done, g - 1)
        if i:
            nc.scalar.activation(self.e_cum[:, g % 2, :, :], self.ps_cb[:, 0:2 * P].rearrange("p (c t) -> p c t", c=2), ACT.Exp)
        nc.scalar.copy(self.bs[:, g % 2, :], self.ps_cb[:, 2 * P:4 * P]).then_inc(self.cb_read, 1)

    def by_head(self, ap):
        return ap.rearrange("p (h c) -> p h c", h=NH)

    def heads(self, ap):
        return ap.unsqueeze(2).to_broadcast([P, NH, HP])

    def front(self, dve, g):
        nc = self.core.nc
        u, di, b, i, n, cols = self.at(g)
        dve.wait_ge(self.x_done, g + 1)
        if g >= 2:
            dve.wait_ge(self.y_done, g - 1)
            if self.passes_on(g - 2):
                dve.wait_ge(self.xw_done, self.passed(g - 2))
        nc.vector.tensor_tensor(self.by_head(self.xdt[:, g % 2, :]), self.by_head(self.ps_x[:, 0:DIN]), self.heads(self.dt[:, n, di * NH:(di + 1) * NH]), ALU.mult)\
          .then_inc(self.x_read, 1)
        dve.wait_ge(self.cb_read, g + 1)
        if g >= 2:
            dve.wait_ge(self.mt_done, g - 1)
        nc.vector.tensor_tensor(self.gm[:, g % 2, :], self.bs[:, g % 2, P:2 * P], self.incl[:, di, :], ALU.mult).then_inc(self.gm_done, 1)
        dve.wait_ge(self.seg_exp, g + 1)
        dve.wait_ge(self.gm_done, g + 1)
        nc.vector.tensor_tensor(self.mt[:, g % 2, :, :], self.e_seg[:, g % 2, :, :], self.gm[:, g % 2, :].unsqueeze(1).to_broadcast([P, NH, P]),
                                ALU.mult).then_inc(self.mt_done, 1)

    def to_state(self, pool, g):
        u, di, b, i, n, cols = self.at(g)
        if not self.passes_on(g):
            return
        pool.wait_ge(self.x_read, g + 1)
        pool.wait_ge(self.decays, 3 * (b + 1))
        if self.carried(g) >= 2:
            pool.wait_ge(self.st_done, self.carried(g) - 1)
        self.core.nc.gpsimd.tensor_tensor(self.by_head(self.xw[:, g % 2, :]), self.by_head(self.xdt[:, g % 2, :]), self.heads(self.to_end[:, di, n, :]), ALU.mult)\
            .then_inc(self.xw_done, 1)

    def state(self, pe, g):
        if not self.passes_on(g):
            return
        n = self.carried(g)
        pe.wait_ge(self.cb_read, g + 1)
        pe.wait_ge(self.xw_done, n + 1)
        if n >= 1:
            pe.wait_ge(self.h_ready, n)
        self.core.nc.tensor.matmul(self.ps_st[:, 0:DIN], self.bs[:, g % 2, 0:P], self.xw[:, g % 2, :], start=True, stop=True).then_inc(self.st_done, 1)

    def decay(self, pool, g):
        u, di, b, i, n, cols = self.at(g)
        if i == 0 or not self.passes_on(g):
            return
        pool.wait_ge(self.h_ready, self.carried(g))
        self.core.nc.gpsimd.tensor_tensor(self.by_head(self.h_dec[:]), self.by_head(self.h[:, (g - 1) % 2, :]),
                                          self.heads(self.whole[:, n, di * NH:(di + 1) * NH]), ALU.mult).then_inc(self.h_decayed, 1)

    def pass_state(self, dve, g):
        u, di, b, i, n, cols = self.at(g)
        if not self.passes_on(g):
            return
        if g >= 1:
            dve.wait_ge(self.y_done, g)
        dve.wait_ge(self.st_done, self.carried(g) + 1)
        if i == 0:
            self.core.nc.vector.tensor_copy(self.h[:, g % 2, :], self.ps_st[:, 0:DIN]).then_inc(self.h_ready, 1)
            return
        dve.wait_ge(self.h_decayed, u * (self.NC - 2) + i)
        self.core.nc.vector.tensor_tensor(self.h[:, g % 2, :], self.h_dec[:], self.ps_st[:, 0:DIN], ALU.add).then_inc(self.h_ready, 1)

    def outputs(self, pe, g):
        nc = self.core.nc
        u, di, b, i, n, cols = self.at(g)
        if g >= 1:
            pe.wait_ge(self.y_read, g)
        if i:
            pe.wait_ge(self.h_ready, self.carried(g))
            for c in range(2):
                nc.tensor.matmul(self.ps_y[:, (2 + c) * P:(3 + c) * P], self.h[:, (g - 1) % 2, c * P:(c + 1) * P], self.act_t[:, u % 2, 3, cols],
                                 start=True, stop=True)
        pe.wait_ge(self.mt_done, g + 1)
        pe.wait_ge(self.x_read, g + 1)
        for hh in range(NH):
            out = self.ps_y[HP * (hh % 2):HP * (hh % 2) + HP, hh // 2 * P:hh // 2 * P + P]
            ins = nc.tensor.matmul(out, self.xdt[:, g % 2, hh * HP:(hh + 1) * HP], self.mt[:, g % 2, hh, :], start=True, stop=True)
        ins.then_inc(self.y_done, 1)

    def back(self, dve, g):
        nc = self.core.nc
        u, di, b, i, n, cols = self.at(g)
        dve.wait_ge(self.y_done, g + 1)
        if g >= 2:
            dve.wait_ge(self.gate_done, g - 1)
        if i:
            dve.wait_ge(self.cb_read, g + 1)
            nc.vector.tensor_tensor(self.y_old[:, g % 2, :, :], self.e_cum[:, g % 2, :, :], self.ps_y[:, 2 * P:4 * P].rearrange("p (c t) -> p c t", c=2), ALU.mult)
        for c in range(2):
            ins = nc.vector.scalar_tensor_tensor(self.y_in[:, g % 2, c, :], self.act_t[:, u % 2, c, cols], self.skip[:, di, c:c + 1], self.ps_y[:, c * P:(c + 1) * P],
                                                 ALU.mult, ALU.add)
        ins.then_inc(self.y_read, 1)

    def gate(self, eng, ops, g):
        u, di, b, i, n, cols = self.at(g)
        eng.wait_ge(self.y_read, g + 1)
        eng.wait_ge(self.proj_read, (u + 1) * self.PIECES * 2)
        if i:
            ops.tensor_tensor(self.y_in[:, g % 2, :, :], self.y_in[:, g % 2, :, :], self.y_old[:, g % 2, :, :], ALU.add).then_inc(self.y_sum, 1)
            eng.wait_ge(self.y_sum, self.carried(g))
        ops.tensor_tensor(self.z[:, u % 2, :, cols], self.y_in[:, g % 2, :, :], self.z[:, u % 2, :, cols], ALU.mult).then_inc(self.gate_done, 1)


    def square(self, act, g):
        u, di, b, i, n, cols = self.at(g)
        act.wait_ge(self.gate_done, g + 1)
        if g >= 2:
            act.wait_ge(self.ss_done, g - 1)
        self.core.nc.scalar.activation(self.y2[:, g % 2, :, :], self.z[:, u % 2, :, cols], ACT.Square).then_inc(self.squared, 1)

    def squares(self, pe, g, parts):
        u, di, b, i, n, cols = self.at(g)
        pe.wait_ge(self.squared, g + 1)
        if parts:
            pe.wait_ge(self.out_read, parts)
        if i == 0 and u >= 1:
            pe.wait_ge(self.ss_read, u)
        col = 3 * D + n % TPB
        for c in range(2):
            ins = self.core.nc.tensor.matmul(self.ps_o[:, col:col + 1], self.y2[:, g % 2, c, :], self.ones[:, 0:1], start=(c == 0), stop=(c == 1))
        ins.then_inc(self.ss_done, 1)

    def variance(self, dve, u):
        dve.wait_ge(self.ss_done, self.NC * (u + 1))
        if u >= 1:
            dve.wait_ge(self.std_done, u)
        self.core.nc.vector.tensor_scalar(self.var[:], self.ps_o[:, 3 * D:3 * D + self.NC], 1.0 / DIN, None, ALU.mult).then_inc(self.ss_read, 1)

    def deviation(self, act, u):
        act.wait_ge(self.ss_read, u + 1)
        if u >= 1:
            act.wait_ge(self.rms_done, u)
        self.core.nc.scalar.activation(self.std[:], self.var[:], ACT.Sqrt, bias=self.core.eps[:]).then_inc(self.std_done, 1)

    def output(self, pe, u, part):
        parts = len(self.PARTS_OUT)
        pe.wait_ge(self.gate_done, self.NC * (u + 1))
        pe.wait_ge(self.ss_read, u + 1)
        if u or part:
            pe.wait_ge(self.out_read, parts * u + part)
        for q, j in enumerate(self.PARTS_OUT[part]):
            for c in range(2):
                ins = self.core.nc.tensor.matmul(self.ps_o[:, q * D:(q + 1) * D], self.z[:, u % 2, c, j * P:(j + 1) * P],
                                                 self.wo[:, self.UNITS[u][0], c, :], start=(c == 0), stop=(c == 1))
        ins.then_inc(self.out_done, 1)

    def add(self, dve, ch, u, part):
        nc, core, (di, b) = self.core.nc, self.core, self.UNITS[u]
        if part == 0:
            dve.wait_ge(self.std_done, u + 1)
            nc.vector.reciprocal(self.rstd[:], self.std[:]).then_inc(self.rms_done, 1)
            dve.wait_ge(self.rms_done, u + 1)
            ch.step(nc.vector.tensor_scalar(self.rstd[:], self.rstd[:], 0.5, None, ALU.mult))
            ch.wait()
        dve.wait_ge(self.out_done, len(self.PARTS_OUT) * u + part + 1)
        for q, j in enumerate(self.PARTS_OUT[part]):
            n = b * TPB + j
            ins = nc.vector.scalar_tensor_tensor(core.x[:, n, :], self.ps_o[:, q * D:(q + 1) * D], self.rstd[:, j:j + 1], core.x[:, n, :], ALU.mult, ALU.add)
        ins.then_inc(self.out_read, 1)
        if part == len(self.PARTS_OUT) - 1:
            dve.wait_ge(self.out_read, len(self.PARTS_OUT) * (u + 1))


def moe_mamba_moe(core):
    nc, moe, mamba = core.nc, core.moe, core.mamba
    NC, N, UNITS = mamba.NC, mamba.N, len(mamba.UNITS)
    HALF = B * E_
    with ExitStack() as ctx:
        norm = core.norm
        norm.side = SideBanks(ctx.enter_context(nc.psum_tensor("ps_side", [P, 2, BANK], F32)), 2)
        main = ctx.enter_context(nc.psum_tensor("ps_main", [P, 6, BANK], F32))
        moe.open(ctx, "moe", main)
        mamba.open(ctx, "mb", norm.xT, norm.side, main)
        moe.y += [lent.rearrange("p a c t -> p (a c t)")[:, 0:3 * D].rearrange("p (s d) -> p s d", s=3) for lent in (mamba.y2[:], mamba.y_old[:])]
        ffn = FfnOfBatch(core, B + 1, 12, mamba.act_t[:, 1, :, :].rearrange("p c (h t) -> p (c h) t", h=2)[:, 0:6, :])
        chain = core.sem("dve_chain", ctx)
        PARTS_OUT = len(mamba.PARTS_OUT)
        share = lambda units, c: units[len(units) * c // FCH:len(units) * (c + 1) // FCH]
        UNITS_AT = [range(0, 4), range(4, 10), range(10, INNER)]

        with nc.Block() as block:
            @block.tensor
            def _(pe):
                core.landed(pe, "moe_gate", "ident", "moe_w1", "moe_w3", "moe_w2", "mb_w_dt", "mb_w_xbc", "mb_w_z")
                moe.turn(pe, 0)
                for i in (12, 13):
                    norm.turn(pe, i)
                moe.hidden(pe, 0, [0])
                ffn.project(pe)
                for u in range(HALF):
                    if u == E_:
                        moe.results(pe, u - 1)
                        moe.turn(pe, u)
                    if u + 1 < HALF and u + 1 != E_:
                        moe.turn(pe, u + 1)
                    for c in range(FCH):
                        if u or c:
                            moe.hidden(pe, u, [c])
                        if u == 3 and c < 2:
                            ffn.output(pe, c)
                        if u == 4 and c == 1:
                            for i in (14, 15):
                                norm.turn(pe, i)
                        if u == 5 and c == 0:
                            moe.counts(pe, 1)
                        if u == 11 and c == 1:
                            norm.turn(pe, 16)
                            norm.turn(pe, 17)
                        if u == 13 and c == 0:
                            mamba.sums(pe, 0)
                        if u == 15 and c == 1:
                            mamba.project(pe, 0, 4)
                    if u == 4:
                        pe.wait_ge(norm.ready, 16)
                        moe.logits(pe, 1)
                    if u and u != E_:
                        moe.results(pe, u - 1)
                    if u == 11:
                        pe.wait_ge(norm.ready, 18)
                        mamba.steps(pe, 0)
                    if 11 <= u < 15:
                        mamba.project(pe, 0, u - 11)
                moe.results(pe, HALF - 1)
                mamba.project(pe, 0, 5)
                pe.wait_ge(moe.y_read, 3 * HALF)
                pe.wait_ge(mamba.norm_done, 1)
                mamba.before(pe, 0)
                for g in range(N):
                    u, i = g // NC, g % NC
                    if g + 1 < N:
                        mamba.before(pe, g + 1)
                    mamba.state(pe, g)
                    if u == 1 and i == 0:
                        pe.wait_ge(norm.ready, 20)
                    if u + 1 < UNITS:
                        for c in mamba.PIECES_AT[i]:
                            mamba.project(pe, u + 1, c)
                    mamba.outputs(pe, g)
                    if g >= 2:
                        mamba.squares(pe, g - 2, 0 if u == 0 else PARTS_OUT * (u - 1) + min(max(i - 3, 0), PARTS_OUT))
                    if u >= 1 and i in (3, 4, 5):
                        mamba.output(pe, u - 1, i - 3)
                    if u == 0 and i == 7:
                        norm.turn(pe, 18)
                        norm.turn(pe, 19)
                    if u == 1 and i == 1:
                        mamba.steps(pe, 1)
                    if u == 1 and i == 4:
                        mamba.sums(pe, 1)
                    if u == 2 and i == 7:
                        norm.turn(pe, 20)
                        norm.turn(pe, 21)
                    if u == 3 and i == 0:
                        pe.wait_ge(norm.ready, 22)
                        moe.logits(pe, 2)
                    if u == 3 and i == 1:
                        moe.counts(pe, 2)
                pe.wait_ge(mamba.seg_exp, N)
                pe.wait_ge(mamba.cb_read, N)
                pe.wait_ge(mamba.x_read, N)
                pe.wait_ge(mamba.y_read, N)
                pe.wait_ge(mamba.h_ready, UNITS * (NC - 1))
                for g in (N - 2, N - 1):
                    mamba.squares(pe, g, PARTS_OUT * (UNITS - 1))
                mamba.output(pe, UNITS - 1, 0)
                moe.turn(pe, HALF)
                for u in range(HALF, 2 * HALF):
                    if u + 1 < 2 * HALF:
                        moe.turn(pe, u + 1)
                    for c in range(FCH):
                        moe.hidden(pe, u, [c])
                        if u == HALF and c in (1, 3):
                            mamba.output(pe, UNITS - 1, (c + 1) // 2)
                        if u == HALF + 1 and c == 3:
                            norm.turn(pe, 22)
                            norm.turn(pe, 23)
                        if u == HALF + 2 and c == 1:
                            pe.wait_ge(norm.ready, 24)
                            moe.logits(pe, 3)
                        if u == HALF + 3 and c == 0:
                            moe.counts(pe, 3)
                    if u == HALF + 1:
                        pe.wait_ge(mamba.out_read, PARTS_OUT * UNITS)
                    if u > HALF:
                        moe.results(pe, u - 1)
                moe.results(pe, 2 * HALF - 1)

            @block.sync
            def _(sp):
                for u in range(2 * HALF):
                    moe.load(sp, u)
                    if u in (E_ + 3, HALF + E_ + 4):
                        moe.fetch(sp, u // E_ - 1)
                    if u == HALF - 1:
                        moe.fetch(sp, 1)
                for half in range(2):
                    sp.wait_ge(moe.combined, 2 * 2 + half + 1)
                    sp.dma_start(core.stored_rows(0, half), core.x[:, half * GROUP:(half + 1) * GROUP, :]).then_inc(core.stored, 16)
                moe.fetch(sp, 3)
                for half in range(2):
                    sp.wait_ge(moe.combined, 2 * 3 + half + 1)
                    sp.dma_start(core.stored_rows(1, half), core.x[:, TPB + half * GROUP:TPB + (half + 1) * GROUP, :]).then_inc(core.stored, 16)
                sp.wait_ge(core.stored, 16 * 2 * B)

            @block.gpsimd
            def _(pool):
                ffn.base(pool)
                mamba.make_masks(pool)
                for u in range(HALF):
                    if u == 4:
                        moe.scatter(pool, 1)
                    if u == HALF - 1:
                        for g in range(2):
                            mamba.cut_a(pool, g)
                    moe.send(pool, u)
                mamba.to_state(pool, 0)
                for g in range(N):
                    u, i = g // NC, g % NC
                    if g + 2 < N:
                        mamba.cut_a(pool, g + 2)
                    if g + 1 < N:
                        mamba.to_state(pool, g + 1)
                    if u < 3:
                        mamba.gate(pool, nc.gpsimd, g)
                    if i < NC - 1:
                        mamba.decay(pool, g + 1)
                    if u == 3 and i >= 2:
                        moe.scatter(pool, 2, 3 * (i - 2), min(3 * (i - 1), TOPK * TPB))
                for u in range(HALF, 2 * HALF):
                    if u == HALF + 2:
                        moe.scatter(pool, 3)
                    moe.send(pool, u)

            @block.vector
            def _(dve):
                ch = Chain(dve, chain)

                nc.vector.memset(moe.xs[64:P, :, moe.FULL, :], 0.0).then_inc(moe.tail_clear, 1)
                for i in (12, 13):
                    norm.stats_of(dve, ch, i)
                norm.normalise(dve, ch, 12)
                moe.take(dve, 0)
                norm.normalise(dve, ch, 13)
                for u in range(HALF):
                    if u == 0:
                        ffn.take(dve)
                    if u == E_:
                        moe.take(dve, u)
                    if u + 1 < HALF and u + 1 != E_:
                        moe.take(dve, u + 1)
                    for c in range(FCH):
                        moe.gating(dve, u, [c])
                        if u < 3:
                            for h in share(UNITS_AT[u], c):
                                ffn.add(dve, h)
                        if u == 3 and c in (1, 2):
                            ffn.finish(dve, c - 1)
                            norm.stats_of(dve, ch, c + 13)
                        if u == 3 and c == 3:
                            for i in (14, 15):
                                norm.normalise(dve, ch, i)
                        if u == 4 and c == 3:
                            moe.shift(dve, ch, 1)
                            moe.pick(dve, ch, 1)
                        if u == 5 and c == 0:
                            moe.put(dve, ch, 1)
                        if u == 10 and c in (1, 2):
                            moe.combine(dve, ch, 0, c - 1)
                            norm.stats_of(dve, ch, c + 15)
                        if u == 10 and c == 3:
                            for i in (16, 17):
                                norm.normalise(dve, ch, i)
                        if u == 11 and c == 3:
                            mamba.step_sizes(dve, ch, 0, 0)
                        if u == 12 and c < 3:
                            mamba.step_sizes(dve, ch, 0, c + 1)
                        n = (u - 12) * FCH + c - 3
                        if 0 <= n < 4 * (TAPS - 1):
                            mamba.convolve(dve, ch, 0, n // (TAPS - 1), n % (TAPS - 1) + 1)
                    moe.address(dve, u)
                    if u == 8:
                        mamba.weigh_out(dve)
                dve.wait_ge(mamba.decays, 3)
                mamba.front(dve, 0)
                for g in range(N):
                    u, i = g // NC, g % NC
                    if u >= 1 and i == 2:
                        mamba.variance(dve, u - 1)
                    if g + 1 < N:
                        mamba.front(dve, g + 1)
                    mamba.pass_state(dve, g)
                    if g == 1:
                        dve.wait_ge(moe.y_out[3], 48 * HALF // moe.OUT)
                    mamba.back(dve, g)
                    if u == 3:
                        if i == 0:
                            dve.wait_ge(mamba.squared, g)
                        mamba.gate(dve, nc.vector, g)
                    if u >= 1 and i in (3, 4, 5):
                        mamba.add(dve, ch, u - 1, i - 3)
                    if u + 1 < UNITS:
                        for c, k in mamba.TAPS_AT[i]:
                            mamba.convolve(dve, ch, u + 1, c, k)
                    if u == 0 and i in (3, 4):
                        moe.combine(dve, ch, 1, i - 3)
                        norm.stats_of(dve, ch, i + 15)
                    if u == 0 and i in (5, 6):
                        norm.normalise(dve, ch, i + 13)
                    if u == 1 and i == 2:
                        for part in range(mamba.STEP_PARTS):
                            mamba.step_sizes(dve, ch, 1, part)
                    if u == 2 and i == 5:
                        norm.stats_of(dve, ch, 20)
                        norm.stats_of(dve, ch, 21)
                    if u == 2 and i == 6:
                        norm.normalise(dve, ch, 20)
                        norm.normalise(dve, ch, 21)
                    if u == 3 and i == 0:
                        moe.shift(dve, ch, 2)
                        moe.pick(dve, ch, 2)
                    if u == 3 and i == 1:
                        moe.put(dve, ch, 2)
                mamba.variance(dve, UNITS - 1)
                moe.take(dve, HALF)
                for u in range(HALF, 2 * HALF):
                    if u + 1 < 2 * HALF:
                        moe.take(dve, u + 1)
                    for c in range(FCH):
                        moe.gating(dve, u, [c])
                        if u == HALF and c in (0, 2):
                            mamba.add(dve, ch, UNITS - 1, c // 2)
                        if u == HALF + 1 and c == 0:
                            mamba.add(dve, ch, UNITS - 1, 2)
                            for i in (22, 23):
                                norm.stats_of(dve, ch, i)
                        if u == HALF + 1 and c == 2:
                            for i in (22, 23):
                                norm.normalise(dve, ch, i)
                        if u == HALF + 2 and c == 2:
                            moe.shift(dve, ch, 3)
                            moe.pick(dve, ch, 3)
                        if u == HALF + 3 and c == 0:
                            moe.put(dve, ch, 3)
                    moe.address(dve, u)
                    if u == HALF + 13:
                        for half in range(2):
                            moe.combine(dve, ch, 2, half)
                for half in range(2):
                    moe.combine(dve, ch, 3, half)

            @block.scalar
            def _(act):
                for i in (12, 13):
                    norm.root(act, i)
                for i in (12, 13):
                    norm.copy(act, nc.scalar.copy, i)
                for u in range(HALF):
                    for c in range(FCH):
                        moe.silu(act, u, [c])
                        if u < 3:
                            for h in share(UNITS_AT[u], c):
                                ffn.relu(act, h)
                        if u == 3 and c == 3:
                            for i in (14, 15):
                                norm.root(act, i)
                        if u == 4 and c == 1:
                            for i in (14, 15):
                                norm.copy(act, nc.scalar.copy, i)
                        if u == 4 and c == 3:
                            moe.exp(act, 1)
                            mamba.exp_a(act)
                        if u == E_ and c == 0:
                            act.wait_ge(mamba.pads, 1)
                        if u == 10 and c == 3:
                            norm.root(act, 16)
                            norm.root(act, 17)
                        if u == 11 and c == 1:
                            norm.copy(act, nc.scalar.copy, 16)
                            norm.copy(act, nc.scalar.copy, 17)
                        if u == 11 and c == 3:
                            mamba.exp_dt(act, 0)
                        if u == 13 and c == 0:
                            mamba.exp_sums(act, 0)
                        if u == 15 and c == 1:
                            mamba.silu_rows(act, 0, range(2))
                        if u == 15 and c == 3:
                            mamba.take(act, 0, 4)
                    if u:
                        moe.weigh(act, u - 1)
                    if 11 <= u < 15:
                        mamba.take(act, 0, u - 11)
                        mamba.first_tap(act, 0, u - 11)
                moe.weigh(act, HALF - 1)
                mamba.silu_rows(act, 0, range(2, 4))
                mamba.take(act, 0, 5)
                mamba.exps(act, 0)
                for g in range(N):
                    u, i = g // NC, g % NC
                    if g + 1 < N:
                        mamba.exps(act, g + 1)
                    if u >= 1 and i == 2:
                        mamba.deviation(act, u - 1)
                    if u + 1 < UNITS:
                        for c in mamba.PIECES_AT[i]:
                            if c >= 4:
                                mamba.silu_rows(act, u + 1, range(2 * (c - 4), 2 * (c - 3)))
                            mamba.take(act, u + 1, c)
                            if c < 4:
                                mamba.first_tap(act, u + 1, c)
                    if g == 1:
                        act.wait_ge(moe.y_out[2], 48 * HALF // moe.OUT)
                    if g >= 1:
                        mamba.square(act, g - 1)
                    if u == 0 and i == 5:
                        norm.root(act, 18)
                        norm.root(act, 19)
                    if u == 0 and i == 7:
                        norm.copy(act, nc.scalar.copy, 18)
                        norm.copy(act, nc.scalar.copy, 19)
                    if u == 1 and i == 2:
                        mamba.exp_dt(act, 1)
                    if u == 1 and i == 4:
                        mamba.exp_sums(act, 1)
                    if u == 2 and i == 6:
                        norm.root(act, 20)
                        norm.root(act, 21)
                    if u == 2 and i == 7:
                        norm.copy(act, nc.scalar.copy, 20)
                        norm.copy(act, nc.scalar.copy, 21)
                    if u == 3 and i == 0:
                        moe.exp(act, 2)
                mamba.square(act, N - 1)
                mamba.deviation(act, UNITS - 1)
                for u in range(HALF, 2 * HALF):
                    for c in range(FCH):
                        moe.silu(act, u, [c])
                        if u == HALF + 1 and c == 1:
                            norm.root(act, 22)
                            norm.root(act, 23)
                        if u == HALF + 1 and c == 3:
                            norm.copy(act, nc.scalar.copy, 22)
                            norm.copy(act, nc.scalar.copy, 23)
                        if u == HALF + 2 and c == 2:
                            moe.exp(act, 3)
                    if u > HALF:
                        moe.weigh(act, u - 1)
                moe.weigh(act, 2 * HALF - 1)




def macaron(nc, dram, out, stages=99):
    with ExitStack() as ctx:
        core = Core(nc, dram, ctx)
        core.stored = core.sem("stored")
        core.stored_rows = lambda b, half: out[b].rearrange("(g j p) d -> p g j d", g=2, p=P)[:, half, :, :]
        load_constants(core, ctx)
        core.moe = Moe(core)
        core.mamba = Mamba(core)
        load_ffn(core, ctx)
        core.rows = core.sb("rows", [P, TILES, core.moe.ROW])
        core.norm = Norm(core, "norm", ctx, lambda n: core.rows[:, n, 0:D], core.sb("norm_xT", [D, B * T]), None,
                         ([0, 1] * 2 + [2, 3] * 2) * 2 + [0, 1, 2, 3] * 2)
        core.moe.open_routing(ctx, "moe", core.rows, core.norm.xT, core.norm)
        core.early = ExitStack()
        core.attention = Attention(core, "attn")
        setup = Setup(core)
        todo = [lambda: ffn_and_attention(core, setup), lambda: moe_mamba_moe(core)]
        for n, stage in enumerate(todo[:stages]):
            stage()
            core.end_stage()
            if n == 0:
                core.early.close()
        core.early.close()
        if stages < 2:
            with nc.Block() as block:
                @block.sync
                def _(sp):
                    for g in range(GROUPS):
                        sp.dma_start(core.stored_rows(g // 2, g % 2), core.x[:, g * GROUP:(g + 1) * GROUP, :]).then_inc(core.stored, 16)
                    sp.wait_ge(core.stored, 64)


def kernel(**inputs):
    import concourse.bacc as bacc
    from concourse.bass_utils import run_bass_kernel_spmd as run

    nc = bacc.Bacc("TRN2", target_bir_lowering=False, num_devices=1)
    arrays = layout(inputs)
    dram = {k: nc.dram_tensor(f"in_{k}", v.shape, mybir.dt.from_np(v.dtype), kind="ExternalInput").ap() for k, v in arrays.items()}
    out = nc.dram_tensor("out", (B, T, D), F32, kind="ExternalOutput").ap()
    macaron(nc, dram, out)
    r = run(nc, [{f"in_{k}": v for k, v in arrays.items()}], core_ids=[0])
    return r.results[0]["out"]
```
